# Optimizing a Trainium2 kernel written in Bass

```python
import numpy as np
import jax
import jax.numpy as jnp

def _softmax(x, axis=-1):
    return jax.nn.softmax(x, axis=axis)

def _gelu(x):
    return jax.nn.gelu(x, approximate=True)

def _silu(x):
    return jax.nn.silu(x)

def _sigmoid(x):
    return jax.nn.sigmoid(x)

def _layernorm(x, axis=-1, eps=1e-05):
    m = jnp.mean(x, axis=axis, keepdims=True)
    v = jnp.var(x, axis=axis, keepdims=True)
    return (x - m) / jnp.sqrt(v + eps)

def _scatter_add(tgt, idx, src, axis=0):
    return tgt.at[idx].add(src)

def _segment_sum(src, seg, n):
    return jax.ops.segment_sum(src, seg, n)
kernel_name = 'mk_adaln_d2_jaxref_r8_fccb05'

def setup_inputs(seed: int=0):
    np.random.seed(seed)
    _w = jnp.asarray

    def _L0_attn_setup():
        import jax, jax.numpy as jnp
        import numpy as np
        B, T, C = (8, 256, 128)
        HS = 64
        H = C // HS
        LORA_R = 32
        TD_R = 64

        def _wkv6(r, k, v, w, u):
            n = r.shape[-1]
            decay = jnp.exp(-jnp.exp(w))

            def per_head(rt, kt, vt, dt, uh):

                def step(S, inp):
                    ri, ki, vi, di = inp
                    kv = ki[:, None] * vi[None, :]
                    y = ri @ (S + uh[:, None] * kv)
                    S = di[:, None] * S + kv
                    return (S, y)
                S0 = jnp.zeros((n, n), rt.dtype)
                _, ys = jax.lax.scan(step, S0, (rt, kt, vt, dt))
                return ys
            f = jax.vmap(per_head, in_axes=(0, 0, 0, 0, 0))
            f = jax.vmap(f, in_axes=(0, 0, 0, 0, None))
            return f(r, k, v, decay, u)
        key = jax.random.key(seed)
        ks = jax.random.split(key, 20)
        inp = {'x': jax.random.normal(ks[0], (B, T, C), jnp.float32), 'miu_x': jax.random.uniform(ks[1], (1, 1, C), jnp.float32), 'lambda_': jax.random.uniform(ks[2], (5, 1, 1, C), jnp.float32), 'A_lora': jax.random.normal(ks[3], (C, LORA_R * 5), jnp.float32) * 0.01, 'B_lora': jax.random.normal(ks[4], (5, LORA_R, C), jnp.float32) * 0.01, 'td_miu': -6.0 + 5.0 * jax.random.uniform(ks[5], (1, 1, C), jnp.float32), 'td_A': jax.random.normal(ks[6], (C, TD_R), jnp.float32) * 0.01, 'td_B': jax.random.normal(ks[7], (TD_R, C), jnp.float32) * 0.01, 'u': jax.random.normal(ks[8], (H, HS), jnp.float32) * 0.1, 'Wr': jax.random.normal(ks[9], (C, C), jnp.float32) * 0.02, 'Wk': jax.random.normal(ks[10], (C, C), jnp.float32) * 0.02, 'Wv': jax.random.normal(ks[11], (C, C), jnp.float32) * 0.02, 'Wg': jax.random.normal(ks[12], (C, C), jnp.float32) * 0.02, 'Wo': jax.random.normal(ks[13], (C, C), jnp.float32) * 0.02, 'gn_gamma': jnp.ones((C,), jnp.float32), 'gn_beta': jnp.zeros((C,), jnp.float32)}
        return inp
    _L0_attn_in = _L0_attn_setup()

    def _L0_ffn_setup():
        import jax, jax.numpy as jnp
        import numpy as np
        B, S, D, F, E = (2, 256, 128, 256, 16)
        key = jax.random.key(seed)
        k = jax.random.split(key, 4)
        scale1 = float(np.sqrt(2.0 / D))
        scale2 = float(np.sqrt(2.0 / F))
        return {'h': jax.random.normal(k[0], (B, S, D), dtype=jnp.float32), 'router_w': jax.random.normal(k[1], (D, E), dtype=jnp.float32) * (1.0 / np.sqrt(D)), 'w1': jax.random.normal(k[2], (E, D, F), dtype=jnp.float32) * scale1, 'b1': jnp.zeros((E, F), dtype=jnp.float32), 'w2': jax.random.normal(k[3], (E, F, D), dtype=jnp.float32) * scale2, 'b2': jnp.zeros((E, D), dtype=jnp.float32)}
    _L0_ffn_in = _L0_ffn_setup()
    _L0_c = _w((lambda *s: np.random.randn(*s).astype(np.float32) * 0.05)(2, 128))
    _L0_wmod = _w((lambda *s: np.random.randn(*s).astype(np.float32) * 0.05)(128, 6 * 128) * 128 ** (-0.5))

    def _L1_attn_setup():
        import jax, jax.numpy as jnp
        import numpy as np
        B, T, D = (4, 128, 128)
        H, DK, DV = (16, 32, 32)
        GAMMA = 0.99

        def _xavier(key, shape, gain=0.1):
            fan_in, fan_out = shape
            lim = gain * jnp.sqrt(6.0 / (fan_in + fan_out))
            return jax.random.uniform(key, shape, jnp.float32, -lim, lim)

        def _hla_forward(x, Wq, Wk, Wv, Wo):
            Bs, Ts, _ = x.shape
            q = (x @ Wq).reshape(Bs, Ts, H, DK).transpose(1, 0, 2, 3)
            k = (x @ Wk).reshape(Bs, Ts, H, DK).transpose(1, 0, 2, 3)
            v = (x @ Wv).reshape(Bs, Ts, H, DV).transpose(1, 0, 2, 3)
            S_K0 = jnp.zeros((Bs, H, DK, DK), x.dtype)
            C_QV0 = jnp.zeros((Bs, H, DK, DV), x.dtype)
            G0 = jnp.zeros((Bs, H, DK, DV), x.dtype)

            def step(carry, qkv):
                S_K, C_QV, G = carry
                q_t, k_t, v_t = qkv
                C_prev = GAMMA * C_QV
                k_C = jnp.einsum('bhk,bhkv->bhv', k_t, C_prev)
                G = GAMMA * G + k_t[..., :, None] * k_C[..., None, :]
                S_K = GAMMA * S_K + k_t[..., :, None] * k_t[..., None, :]
                C_QV = C_prev + q_t[..., :, None] * v_t[..., None, :]
                S_C = jnp.einsum('bhij,bhjv->bhiv', S_K, C_QV)
                o_t = jnp.einsum('bhk,bhkv->bhv', q_t, S_C - G)
                return ((S_K, C_QV, G), o_t)
            _, outs = jax.lax.scan(step, (S_K0, C_QV0, G0), (q, k, v))
            out = outs.transpose(1, 0, 2, 3).reshape(Bs, Ts, H * DV)
            return out @ Wo
        key = jax.random.key(seed)
        kx, kq, kk, kv, ko = jax.random.split(key, 5)
        return {'x': jax.random.normal(kx, (B, T, D), jnp.float32), 'Wq': _xavier(kq, (D, H * DK)), 'Wk': _xavier(kk, (D, H * DK)), 'Wv': _xavier(kv, (D, H * DV)), 'Wo': _xavier(ko, (H * DV, D))}
    _L1_attn_in = _L1_attn_setup()

    def _L1_ffn_setup():
        import jax, jax.numpy as jnp
        import numpy as np
        B, S, D = (2, 256, 128)
        E, H, K = (8, 704, 2)
        N_RESERVED = 4
        key = jax.random.key(seed)
        ks = jax.random.split(key, 5)
        scale = 0.02
        x = jax.random.normal(ks[0], (B, S, D), dtype=jnp.float32)
        gate_w = jax.random.normal(ks[1], (E, D), dtype=jnp.float32) * scale
        w1 = jax.random.normal(ks[2], (E, D, H), dtype=jnp.float32) * scale
        w3 = jax.random.normal(ks[3], (E, D, H), dtype=jnp.float32) * scale
        w2 = jax.random.normal(ks[4], (E, H, D), dtype=jnp.float32) * scale
        return {'x': x, 'gate_w': gate_w, 'w1': w1, 'w2': w2, 'w3': w3}
    _L1_ffn_in = _L1_ffn_setup()
    _L1_c = _w((lambda *s: np.random.randn(*s).astype(np.float32) * 0.05)(2, 128))
    _L1_wmod = _w((lambda *s: np.random.randn(*s).astype(np.float32) * 0.05)(128, 6 * 128) * 128 ** (-0.5))
    _d = {'L0_attn_x': _L0_attn_in['x'], 'L0_attn_miu_x': _L0_attn_in['miu_x'], 'L0_attn_lambda_': _L0_attn_in['lambda_'], 'L0_attn_A_lora': _L0_attn_in['A_lora'], 'L0_attn_B_lora': _L0_attn_in['B_lora'], 'L0_attn_td_miu': _L0_attn_in['td_miu'], 'L0_attn_td_A': _L0_attn_in['td_A'], 'L0_attn_td_B': _L0_attn_in['td_B'], 'L0_attn_u': _L0_attn_in['u'], 'L0_attn_Wr': _L0_attn_in['Wr'], 'L0_attn_Wk': _L0_attn_in['Wk'], 'L0_attn_Wv': _L0_attn_in['Wv'], 'L0_attn_Wg': _L0_attn_in['Wg'], 'L0_attn_Wo': _L0_attn_in['Wo'], 'L0_attn_gn_gamma': _L0_attn_in['gn_gamma'], 'L0_attn_gn_beta': _L0_attn_in['gn_beta'], 'L0_ffn_router_w': _L0_ffn_in['router_w'], 'L0_ffn_w1': _L0_ffn_in['w1'], 'L0_ffn_b1': _L0_ffn_in['b1'], 'L0_ffn_w2': _L0_ffn_in['w2'], 'L0_ffn_b2': _L0_ffn_in['b2'], 'L0_c': _L0_c, 'L0_wmod': _L0_wmod, 'L1_attn_Wq': _L1_attn_in['Wq'], 'L1_attn_Wk': _L1_attn_in['Wk'], 'L1_attn_Wv': _L1_attn_in['Wv'], 'L1_attn_Wo': _L1_attn_in['Wo'], 'L1_ffn_gate_w': _L1_ffn_in['gate_w'], 'L1_ffn_w1': _L1_ffn_in['w1'], 'L1_ffn_w2': _L1_ffn_in['w2'], 'L1_ffn_w3': _L1_ffn_in['w3'], 'L1_c': _L1_c, 'L1_wmod': _L1_wmod}
    _x0 = _d['L0_attn_x']
    _d['L0_attn_x'] = jax.random.normal(jax.random.fold_in(jax.random.key(seed), 1), (2, 1024, 128), dtype=_x0.dtype)
    del _x0
    return _d

def reference(L0_attn_x, L0_attn_miu_x, L0_attn_lambda_, L0_attn_A_lora, L0_attn_B_lora, L0_attn_td_miu, L0_attn_td_A, L0_attn_td_B, L0_attn_u, L0_attn_Wr, L0_attn_Wk, L0_attn_Wv, L0_attn_Wg, L0_attn_Wo, L0_attn_gn_gamma, L0_attn_gn_beta, L0_ffn_router_w, L0_ffn_w1, L0_ffn_b1, L0_ffn_w2, L0_ffn_b2, L0_c, L0_wmod, L1_attn_Wq, L1_attn_Wk, L1_attn_Wv, L1_attn_Wo, L1_ffn_gate_w, L1_ffn_w1, L1_ffn_w2, L1_ffn_w3, L1_c, L1_wmod):

    def _L0_attn_ref(x, miu_x, lambda_, A_lora, B_lora, td_miu, td_A, td_B, u, Wr, Wk, Wv, Wg, Wo, gn_gamma, gn_beta):
        import jax, jax.numpy as jnp
        import numpy as np
        B, T, C = (8, 256, 128)
        HS = 64
        H = C // HS
        LORA_R = 32
        TD_R = 64

        def _wkv6(r, k, v, w, u):
            n = r.shape[-1]
            decay = jnp.exp(-jnp.exp(w))

            def per_head(rt, kt, vt, dt, uh):

                def step(S, inp):
                    ri, ki, vi, di = inp
                    kv = ki[:, None] * vi[None, :]
                    y = ri @ (S + uh[:, None] * kv)
                    S = di[:, None] * S + kv
                    return (S, y)
                S0 = jnp.zeros((n, n), rt.dtype)
                _, ys = jax.lax.scan(step, S0, (rt, kt, vt, dt))
                return ys
            f = jax.vmap(per_head, in_axes=(0, 0, 0, 0, 0))
            f = jax.vmap(f, in_axes=(0, 0, 0, 0, None))
            return f(r, k, v, decay, u)
        b, t, c = x.shape
        h, n = u.shape
        x_last = jnp.pad(x, ((0, 0), (1, 0), (0, 0)))[:, :t]
        dxa = x_last - x
        xm = x + dxa * miu_x
        lora_h = jnp.tanh(xm @ A_lora).reshape(b, t, 5, -1)
        miu = lambda_ + jnp.einsum('btfi,fic->fbtc', lora_h, B_lora)
        xx = x[None] + dxa[None] * miu
        w_in, k_in, v_in, r_in, g_in = xx
        k = k_in @ Wk.T
        v = v_in @ Wv.T
        r = r_in @ Wr.T
        g = jax.nn.silu(g_in @ Wg.T)
        w = td_miu + jnp.tanh(w_in @ td_A) @ td_B

        def to_heads(z):
            return z.reshape(b, t, h, n).transpose(0, 2, 1, 3)
        y = _wkv6(to_heads(r), to_heads(k), to_heads(v), to_heads(w), u)
        y = y.transpose(0, 2, 1, 3)
        eps = 1e-05 * h
        mean = y.mean(-1, keepdims=True)
        var = y.var(-1, keepdims=True)
        yn = (y - mean) * jax.lax.rsqrt(var + eps)
        yn = yn * gn_gamma.reshape(h, n) + gn_beta.reshape(h, n)
        yn = yn.reshape(b, t, c)
        return yn * g @ Wo.T

    def _L0_ffn_ref(h, router_w, w1, b1, w2, b2):
        import jax, jax.numpy as jnp
        import numpy as np
        B, S, D, F, E = (2, 256, 128, 256, 16)
        b, s, d = h.shape
        x = h.reshape(-1, d)
        logits = x @ router_w
        assign = jnp.argmax(logits, axis=-1)
        w = jax.nn.sigmoid(jnp.take_along_axis(logits, assign[:, None], axis=1)[:, 0])
        hh = jnp.einsum('nd,edf->nef', x, w1) + b1
        hh = jax.nn.gelu(hh, approximate=False)
        all_out = jnp.einsum('nef,efd->ned', hh, w2) + b2
        out = jnp.take_along_axis(all_out, assign[:, None, None], axis=1)[:, 0, :]
        out = out * w[:, None]
        return out.reshape(b, s, d)

    def _L1_attn_ref(x, Wq, Wk, Wv, Wo):
        import jax, jax.numpy as jnp
        import numpy as np
        B, T, D = (4, 128, 128)
        H, DK, DV = (16, 32, 32)
        GAMMA = 0.99

        def _xavier(key, shape, gain=0.1):
            fan_in, fan_out = shape
            lim = gain * jnp.sqrt(6.0 / (fan_in + fan_out))
            return jax.random.uniform(key, shape, jnp.float32, -lim, lim)

        def _hla_forward(x, Wq, Wk, Wv, Wo):
            Bs, Ts, _ = x.shape
            q = (x @ Wq).reshape(Bs, Ts, H, DK).transpose(1, 0, 2, 3)
            k = (x @ Wk).reshape(Bs, Ts, H, DK).transpose(1, 0, 2, 3)
            v = (x @ Wv).reshape(Bs, Ts, H, DV).transpose(1, 0, 2, 3)
            S_K0 = jnp.zeros((Bs, H, DK, DK), x.dtype)
            C_QV0 = jnp.zeros((Bs, H, DK, DV), x.dtype)
            G0 = jnp.zeros((Bs, H, DK, DV), x.dtype)

            def step(carry, qkv):
                S_K, C_QV, G = carry
                q_t, k_t, v_t = qkv
                C_prev = GAMMA * C_QV
                k_C = jnp.einsum('bhk,bhkv->bhv', k_t, C_prev)
                G = GAMMA * G + k_t[..., :, None] * k_C[..., None, :]
                S_K = GAMMA * S_K + k_t[..., :, None] * k_t[..., None, :]
                C_QV = C_prev + q_t[..., :, None] * v_t[..., None, :]
                S_C = jnp.einsum('bhij,bhjv->bhiv', S_K, C_QV)
                o_t = jnp.einsum('bhk,bhkv->bhv', q_t, S_C - G)
                return ((S_K, C_QV, G), o_t)
            _, outs = jax.lax.scan(step, (S_K0, C_QV0, G0), (q, k, v))
            out = outs.transpose(1, 0, 2, 3).reshape(Bs, Ts, H * DV)
            return out @ Wo
        return _hla_forward(x, Wq, Wk, Wv, Wo)

    def _L1_ffn_ref(x, gate_w, w1, w2, w3):
        import jax, jax.numpy as jnp
        import numpy as np
        B, S, D = (2, 256, 128)
        E, H, K = (8, 704, 2)
        N_RESERVED = 4
        b, s, d = x.shape
        T = b * s
        xf = x.reshape(T, d)
        logits = xf @ gate_w.T
        expert_ids = jnp.arange(E)
        logits = jnp.where(expert_ids[None, :] >= E - N_RESERVED, -jnp.inf, logits)
        weights = jax.nn.softmax(logits, axis=-1)
        top_w, top_idx = jax.lax.top_k(weights, K)
        top_w = top_w / jnp.sum(top_w, axis=-1, keepdims=True)
        cw = jnp.zeros((T, E), dtype=x.dtype).at[jnp.arange(T)[:, None], top_idx].add(top_w)
        h = jax.nn.silu(jnp.einsum('td,edh->teh', xf, w1)) * jnp.einsum('td,edh->teh', xf, w3)
        y = jnp.einsum('teh,ehd->ted', h, w2)
        out = jnp.einsum('te,ted->td', cw, y)
        return out.reshape(b, s, d)
    x = L0_attn_x
    mod = (_silu(L0_c) @ L0_wmod).reshape(L0_c.shape[0], 6, 1, -1)
    sa, ca, ga, sb, cb, gb = (mod[:, 0], mod[:, 1], mod[:, 2], mod[:, 3], mod[:, 4], mod[:, 5])
    ga = (2 * (ga >= 0) - 1) * jnp.maximum(jnp.abs(ga), 0.25)
    gb = (2 * (gb >= 0) - 1) * jnp.maximum(jnp.abs(gb), 0.25)
    h = _layernorm(x, axis=-1) * (1 + ca) + sa
    x = x + ga * _L0_attn_ref(h, L0_attn_miu_x, L0_attn_lambda_, L0_attn_A_lora, L0_attn_B_lora, L0_attn_td_miu, L0_attn_td_A, L0_attn_td_B, L0_attn_u, L0_attn_Wr, L0_attn_Wk, L0_attn_Wv, L0_attn_Wg, L0_attn_Wo, L0_attn_gn_gamma, L0_attn_gn_beta)
    h = _layernorm(x, axis=-1) * (1 + cb) + sb
    x = x + gb * _L0_ffn_ref(h, L0_ffn_router_w, L0_ffn_w1, L0_ffn_b1, L0_ffn_w2, L0_ffn_b2)
    mod = (_silu(L1_c) @ L1_wmod).reshape(L1_c.shape[0], 6, 1, -1)
    sa, ca, ga, sb, cb, gb = (mod[:, 0], mod[:, 1], mod[:, 2], mod[:, 3], mod[:, 4], mod[:, 5])
    ga = (2 * (ga >= 0) - 1) * jnp.maximum(jnp.abs(ga), 0.25)
    gb = (2 * (gb >= 0) - 1) * jnp.maximum(jnp.abs(gb), 0.25)
    h = _layernorm(x, axis=-1) * (1 + ca) + sa
    x = x + ga * _L1_attn_ref(h, L1_attn_Wq, L1_attn_Wk, L1_attn_Wv, L1_attn_Wo)
    h = _layernorm(x, axis=-1) * (1 + cb) + sb
    x = x + gb * _L1_ffn_ref(h, L1_ffn_gate_w, L1_ffn_w1, L1_ffn_w2, L1_ffn_w3)
    return x

_drawn_inputs = setup_inputs


def setup_inputs(seed=0):
    import zlib

    import numpy as np

    out = dict(_drawn_inputs(seed))
    spreads = {'L0_attn_gn_gamma': (1.0, 0.6),
     'L0_attn_gn_beta': (0.0, 0.8),
     'L0_ffn_b1': (0.0, 0.396),
     'L0_ffn_b2': (0.0, 0.389)}
    factors = {'L0_attn_miu_x': 8.0,
     'L0_attn_lambda_': 3.533,
     'L0_attn_A_lora': 8.0,
     'L0_attn_B_lora': 8.0,
     'L0_attn_td_miu': 3.73,
     'L0_attn_td_A': 8.0,
     'L0_attn_td_B': 25.456,
     'L0_attn_u': 8.0,
     'L0_attn_Wr': 2.751,
     'L0_attn_Wk': 2.781,
     'L0_attn_Wv': 2.891,
     'L0_attn_Wg': 3.017,
     'L0_attn_Wo': 2.92,
     'L1_attn_Wq': 8.0,
     'L1_attn_Wk': 8.0,
     'L1_attn_Wv': 8.0,
     'L1_attn_Wo': 8.0,
     'L1_ffn_gate_w': 8.0,
     'L1_ffn_w1': 8.0,
     'L1_ffn_w2': 8.0,
     'L1_ffn_w3': 8.0,
     'L1_c': 8.0,
     'L1_wmod': 8.0}
    for name, (base, spread) in spreads.items():
        noise = np.random.default_rng([zlib.crc32(name.encode()), seed]).standard_normal(out[name].shape)
        drawn = base * np.exp(spread * noise) if base else spread * noise
        out[name] = jnp.asarray(drawn.astype(out[name].dtype))
    for name, factor in factors.items():
        out[name] = (out[name] * factor).astype(out[name].dtype)
    return out
```

```python
from contextlib import ExitStack

import numpy as np

import concourse.bass as bass
from concourse import mybir

F32 = mybir.dt.float32
I32 = mybir.dt.int32
U32 = mybir.dt.uint32
ALU = mybir.AluOpType
ACT = mybir.ActivationFunctionType
AX = mybir.AxisListType

P = 128
BATCH, SEQ, C = 2, 1024, 128
CHUNKS = SEQ // P
TILES = BATCH * CHUNKS
LN_EPS = 1e-5

RW_HEADS, RW_DIM = 2, 64
LORA = 32
MIXES = 5
TD_RANK = 64
LEAF = 32
GN_EPS = 1e-5 * RW_HEADS
LEVELS = 7

E0, F0 = 16, 256
SLOT_TILES = 32
SLOTS = SLOT_TILES * P

HL_HEADS, HL_DIM = 16, 32
GROUPS = HL_HEADS * HL_DIM // P
HPG = P // HL_DIM
GAMMA = 0.99

E1, E1_LIVE, F1 = 8, 4, 704
FULL1 = F1 // P
TAIL1 = F1 - FULL1 * P


def shape_constants():
    i = np.arange(P)
    row, col = i[:, None], i[None, :]
    parts = {}
    parts["ident"] = (row == col)
    parts["before"] = (row < col)
    parts["ones"] = np.ones((P, P))
    parts["head2"] = (row // RW_DIM == col // RW_DIM)
    parts["head4"] = (row // HL_DIM == col // HL_DIM)
    lag = (col - row).astype(np.float64)
    parts["decay_incl"] = np.where(lag >= 0, GAMMA ** np.maximum(lag, 0), 0)
    parts["decay_excl"] = np.where(lag > 0, GAMMA ** np.maximum(lag, 0), 0)
    parts["decay_row"] = np.broadcast_to(GAMMA ** (col + 1.0), (P, P))
    parts["decay_col"] = GAMMA ** (P - 1.0 - row)
    s, t = row % LEAF, np.arange(LEAF)[None, :]
    leaf = [(s // 2 == t // 2) & (s <= t)]
    for m in (2, 4, 8, 16):
        leaf.append((s // (2 * m) == t // (2 * m)) & (s % (2 * m) < m) & (t % (2 * m) >= m))
    parts["leaf"] = np.concatenate(leaf, axis=1)
    parts["iota16"] = np.broadcast_to(np.arange(E0), (P, E0))
    parts["iota32"] = np.broadcast_to(np.arange(SLOT_TILES), (P, SLOT_TILES))
    at, cols = {}, 0
    for name, a in parts.items():
        at[name] = (cols, cols + a.shape[1])
        cols += a.shape[1]
    return at, np.concatenate([np.asarray(a, np.float32) for a in parts.values()], axis=1)


CONST_AT, _ = shape_constants()
CONST_COLS = max(b for _, b in CONST_AT.values())


def bass_adaln_stack(nc, t, out):
    ctx = ExitStack()
    with ctx:
        def sb(name, shape, dt=F32):
            return ctx.enter_context(nc.sbuf_tensor(name, shape, dt))

        def sem(name):
            return ctx.enter_context(nc.semaphore(name))

        const = sb("const", [P, CONST_COLS])

        def cst(name):
            a, b = CONST_AT[name]
            return const[:, a:b]

        x_sb = sb("x_sb", [P, TILES, C])
        x_bc = x_sb[:, :, :].rearrange("p (b c) n -> p b c n", b=BATCH)
        eps_pow = sb("eps_pow", [P, 16])
        mod_col = sb("mod_col", [P, 2, 4, BATCH])
        mod_row = sb("mod_row", [P, 2, 2, BATCH, C])
        sbw = sb("sbw", [P, 2, 2, BATCH, C])

        bank = [ctx.enter_context(nc.psum_tensor(f"bank{i}", [P, 512], F32)) for i in range(4)]
        bank.append(None)
        pair = ctx.enter_context(nc.psum_tensor("pair", [P, 1024], F32))
        bank[4] = ctx.enter_context(nc.psum_tensor("bank6", [P, 512], F32))
        bank.append(ctx.enter_context(nc.psum_tensor("bank7", [P, 512], F32)))

        W1 = {n: sb(f"hla_w{n}", [P, HL_HEADS * HL_DIM]) for n in "qkv"}
        W1["o"] = sb("hla_wo", [P, GROUPS, C])
        s_w1 = sem("s_w1")
        W2 = {"w1": sb("moe_w1", [P, E1_LIVE, F1]), "w3": sb("moe_w3", [P, E1_LIVE, F1]),
              "w2": sb("moe_w2", [P, E1_LIVE, FULL1, C]), "w2_tail": sb("moe_w2_tail", [P, E1_LIVE // 2, C])}
        s_w2 = sem("s_w2")
        with nc.cleanup_on_exit():
            setup_phase(nc, t, const, x_sb, eps_pow, mod_col, mod_row, sbw, bank, cst, W1, s_w1, W2, s_w2)
        with nc.cleanup_on_exit():
            rwkv_phase(nc, t, x_bc, eps_pow, mod_col, mod_row, bank, pair, cst)
        keep = {"slot": sb("slot_of_token", [P, TILES], U32), "weight": sb("router_weight", [P, TILES]),
                "expert": sb("expert_of_tile", [1, SLOT_TILES], I32)}
        with nc.cleanup_on_exit():
            expert_route_phase(nc, t, x_bc, eps_pow, sbw[:, 0], bank, cst, keep)
        with nc.cleanup_on_exit():
            expert_phase(nc, t, x_sb, mod_row, bank, cst, keep)
        with nc.sbuf_tensor("hT_all", [P, TILES, P], F32) as hT_all:
            with nc.cleanup_on_exit():
                norm_transpose_phase(nc, x_bc, eps_pow, mod_col, bank, cst, hT_all)
            with nc.cleanup_on_exit():
                hla_phase(nc, x_bc, mod_row, bank, pair, cst, hT_all, W1, s_w1)
        with nc.sbuf_tensor("xT_all", [P, TILES, P], F32) as xT_all, \
                nc.sbuf_tensor("xsT_all", [P, E1_LIVE, TILES, P], F32) as xsT_all:
            with nc.cleanup_on_exit():
                swiglu_route_phase(nc, t, x_bc, eps_pow, sbw[:, 1], bank, cst, xT_all, xsT_all)
            with nc.cleanup_on_exit():
                swiglu_phase(nc, x_sb, mod_row, bank, pair, cst, xT_all, xsT_all, W2, s_w2, out)


def setup_phase(nc, t, const, x_sb, eps_pow, mod_col, mod_row, sbw, bank, cst, W1, s_w1, W2, s_w2):
    with ExitStack() as ctx:
        def sb(name, shape, dt=F32):
            return ctx.enter_context(nc.sbuf_tensor(name, shape, dt))

        def sem(name):
            return nc.alloc_semaphore(name)

        cT = sb("cT", [P, 2, BATCH])
        eT = sb("eT", [P, 2, BATCH])
        silu_c = sb("silu_c", [P, 2, BATCH])
        wmod = sb("wmod", [P, 2, 6 * C])
        absr = sb("absr", [P, 2, 2, BATCH, C])
        sgn = sb("sgn", [P, 2, 2, BATCH, C])
        s_const = sem("s_const")
        s_x = sem("s_x")
        s_c = sem("s_c")
        s_wmod = sem("s_wmod")
        s_exp = sem("s_exp")
        s_silu = sem("s_silu")
        s_cols = sem("s_cols")
        s_rows = sem("s_rows")
        s_colv = sem("s_colv")
        s_clamp = sem("s_clamp")
        s_set = sem("s_set")
        block = ctx.enter_context(nc.Block())

        @block.sync
        def _(sp):
            sp.dma_start(cT[:, :, :], t["c_cols"]).then_inc(s_c, 16)
            sp.dma_start(wmod[:, :, :], t["wmod"].rearrange("l k n -> k l n")).then_inc(s_wmod, 16)
            sp.dma_start(const[:, :], t["const"]).then_inc(s_const, 16)
            for b in range(BATCH):
                sp.dma_start(x_sb[:, b * CHUNKS:(b + 1) * CHUNKS, :],
                             t["L0_attn_x"][b].rearrange("(c p) n -> p c n", p=P)).then_inc(s_x, 16)
            for n in "qkv":
                sp.dma_start(W1[n][:, :], t["L1_attn_W" + n]).then_inc(s_w1, 16)
            sp.dma_start(W1["o"][:, :, :], t["L1_attn_Wo"].rearrange("(j p) n -> p j n", p=P)).then_inc(s_w1, 16)
            for n in ("w1", "w3"):
                sp.dma_start(W2[n][:, :, :], t["moe_" + n].rearrange("e k n -> k e n")).then_inc(s_w2, 16)
            for e in range(E1_LIVE):
                sp.dma_start(W2["w2"][:, e, :, :], t["moe_w2"][e, 0:FULL1 * P, :].rearrange("(f p) n -> p f n", p=P))\
                    .then_inc(s_w2, 16)
                rows = slice((e % 2) * TAIL1, (e % 2 + 1) * TAIL1)
                sp.dma_start(W2["w2_tail"][rows, e // 2, :], t["moe_w2"][e, FULL1 * P:F1, :]).then_inc(s_w2, 16)
            sp.wait_ge(s_const, 16)
            sp.wait_ge(s_x, 32)

        @block.gpsimd
        def _(pool):
            pool.memset(eps_pow[:, :], -0.5).then_inc(s_set, 1)
            pool.wait_ge(s_set, 1)

        @block.scalar
        def _(act):
            act.wait_ge(s_c, 16)
            act.activation(eT[:, :, :], cT[:, :, :], ACT.Exp, scale=-1.0).then_inc(s_exp, 1)

        @block.vector
        def _(dve):
            dve.wait_ge(s_exp, 1)
            dve.tensor_scalar(eT[:, :, :], eT[:, :, :], 1.0, None, ALU.add).then_inc(s_silu, 1)
            dve.wait_ge(s_silu, 1)
            dve.reciprocal(eT[:, :, :], eT[:, :, :]).then_inc(s_silu, 1)
            dve.wait_ge(s_silu, 2)
            dve.tensor_tensor(silu_c[:, :, :], eT[:, :, :], cT[:, :, :], ALU.mult).then_inc(s_silu, 1)
            dve.wait_ge(s_cols, 1)
            for n, plus in enumerate((0.0, 1.0, 0.0, 1.0)):
                dve.tensor_scalar(mod_col[:, :, n, :],
                                  bank[0][:, 0:16].rearrange("p (l n b) -> p l n b", l=2, n=4)[:, :, n, :],
                                  plus, None, ALU.add).then_inc(s_colv, 1)
            dve.wait_ge(s_rows, 1)
            for layer in range(2):
                rows = bank[1 + layer][:, :].rearrange("p (g b n) -> p g b n", g=2, b=BATCH)
                flat_rows = bank[1 + layer][:, :]
                neg = absr[:, layer].rearrange("p g b n -> p (g b n)")
                dve.tensor_scalar(neg, flat_rows, -1.0, None, ALU.mult).then_inc(s_clamp, 1)
                dve.tensor_scalar(sgn[:, layer], rows, 0.0, 2.0, ALU.is_ge, ALU.mult).then_inc(s_clamp, 1)
                dve.wait_ge(s_clamp, 3 * layer + 1)
                dve.scalar_tensor_tensor(out=neg, in0=neg, scalar=0.25, in1=flat_rows, op0=ALU.max,
                                         op1=ALU.max).then_inc(s_clamp, 1)
            dve.wait_ge(s_clamp, 6)
            dve.scalar_tensor_tensor(out=mod_row[:, :, :, :, :].rearrange("p l g b n -> p (l g b n)"),
                                     in0=sgn[:, :, :, :, :].rearrange("p l g b n -> p (l g b n)"), scalar=-1.0,
                                     in1=absr[:, :, :, :, :].rearrange("p l g b n -> p (l g b n)"),
                                     op0=ALU.add, op1=ALU.mult).then_inc(s_clamp, 1)
            for layer in range(2):
                srows = bank[3 + layer][:, :].rearrange("p (k b n) -> p k b n", k=2, b=BATCH)
                dve.tensor_scalar(sbw[:, layer, 0], srows[:, 0], 0.0, None, ALU.add).then_inc(s_clamp, 1)
                dve.tensor_scalar(sbw[:, layer, 1], srows[:, 1], 1.0, None, ALU.add).then_inc(s_clamp, 1)
            dve.wait_ge(s_clamp, 11)
            dve.wait_ge(s_colv, 4)

        @block.tensor
        def _(pe):
            pe.wait_ge(s_silu, 3)
            pe.wait_ge(s_wmod, 16)
            for layer in range(2):
                for n, part in enumerate((0, 1, 3, 4)):
                    at = (layer * 4 + n) * 2
                    last = pe.matmul(bank[0][:, at:at + 2], wmod[:, layer, part * C:(part + 1) * C],
                                     silu_c[:, layer, :], start=True, stop=True)
            last.then_inc(s_cols, 1)
            for layer in range(2):
                for g, part in enumerate((2, 5)):
                    for b in range(BATCH):
                        at = (g * 2 + b) * C
                        pe.matmul(bank[1 + layer][:, at:at + C], silu_c[:, layer, b:b + 1].to_broadcast([P, P]),
                                  wmod[:, layer, part * C:(part + 1) * C], start=True, stop=True)
                for k, part in enumerate((3, 4)):
                    for b in range(BATCH):
                        at = (k * 2 + b) * C
                        last = pe.matmul(bank[3 + layer][:, at:at + C], silu_c[:, layer, b:b + 1].to_broadcast([P, P]),
                                         wmod[:, layer, part * C:(part + 1) * C], start=True, stop=True)
            last.then_inc(s_rows, 1)


def rwkv_phase(nc, t, x_bc, eps_pow, mod_col, mod_row, bank, pair, cst):
    with ExitStack() as ctx:
        def sb(name, shape, dt=F32):
            return ctx.enter_context(nc.sbuf_tensor(name, shape, dt))

        def sem(name):
            return nc.alloc_semaphore(name)

        N = BATCH * P
        lamb = sb("lamb", [P, MIXES])
        miu = sb("miu", [P, 1])
        td_miu = sb("td_miu", [P, 1])
        bonus = sb("bonus", [P, 1])
        gamma = sb("gamma", [P, 1])
        beta = sb("beta", [P, 1])
        a_lora = sb("a_lora", [P, MIXES * LORA])
        b_pad = sb("b_pad", [P, MIXES, C])
        td_a = sb("td_a", [P, TD_RANK])
        td_b = sb("td_b", [TD_RANK, C])
        wT = sb("wT", [P, 5, C])
        stats = sb("stats", [P, TILES, 6])
        mv = sb("mv", [P, TILES, 2])
        rstd = sb("rstd", [P, TILES])
        xn = sb("xn", [P, BATCH, C])
        hT = sb("hT", [P, BATCH, P + 1])
        dxa = sb("dxa", [P, BATCH, P])
        xm = sb("xm", [P, BATCH, P])
        lh = sb("lh", [P, N])
        lh4 = sb("lh4", [LORA, N])
        xx = sb("xx", [P, MIXES, BATCH, P])
        tw = sb("tw", [TD_RANK, N])
        ew = sb("ew", [P, N])
        rl = [sb(f"rl{m}", [P, N]) for m in range(LEVELS + 1)]
        kl = [sb(f"kl{m}", [P, N]) for m in range(LEVELS + 1)]
        tot = [sb(f"tot{m}", [P, N >> m]) for m in range(LEVELS + 1)]
        rd = sb("rd", [P, N])
        kd = sb("kd", [P, N])
        v_sb = sb("v_sb", [P, BATCH, C])
        eg = sb("eg", [P, N])
        gT = sb("gT", [P, N])
        prod = sb("prod", [P, 4, 160])
        leafs = sb("leafs", [P, 4, LEAF])
        att = sb("att", [P, 4, P])
        ktm = sb("ktm", [P, BATCH, P])
        state = sb("state", [P, BATCH, P])
        kv = sb("kv", [P, BATCH, P])
        gst = sb("gst", [P, 4, 6])
        gmv = sb("gmv", [P, 4, 2])
        grs = sb("grs", [P, 4])
        yn = sb("yn", [P, BATCH, C])
        zT = sb("zT", [P, BATCH, P])
        gated = sb("gated", [P, BATCH, C])

        s_w = sem("s_w")
        s_zero = sem("s_zero")
        s_stat = sem("s_stat")
        s_var = sem("s_var")
        s_rstd = sem("s_rstd")
        s_xn = sem("s_xn")
        s_xt = sem("s_xt")
        s_ht = sem("s_ht")
        s_dxa = sem("s_dxa")
        s_xm = sem("s_xm")
        s_lora = sem("s_lora")
        s_lh = sem("s_lh")
        s_mix = sem("s_mix")
        s_scaled = sem("s_scaled")
        s_xx = sem("s_xx")
        s_proj = sem("s_proj")
        s_td = sem("s_td")
        s_tw = sem("s_tw")
        s_ew = sem("s_ew")
        s_evac = sem("s_evac")
        s_diag = sem("s_diag")
        s_r = sem("s_r")
        s_k = sem("s_k")
        s_tot = sem("s_tot")
        s_rc = sem("s_rc")
        s_leafmm = sem("s_leafmm")
        s_prod = sem("s_prod")
        s_leaf = sem("s_leaf")
        s_att = sem("s_att")
        s_off = sem("s_off")
        s_ktT = sem("s_ktT")
        s_ktm = sem("s_ktm")
        s_y = sem("s_y")
        s_kv = sem("s_kv")
        s_state = sem("s_state")
        s_gn = sem("s_gn")
        s_grs = sem("s_grs")
        s_yn = sem("s_yn")
        s_zt = sem("s_zt")
        s_z = sem("s_z")
        s_zg = sem("s_zg")
        s_o = sem("s_o")
        s_gate = sem("s_gate")
        s_gated = sem("s_gated")
        s_gT = sem("s_gT")
        s_iter = sem("s_iter")
        block = ctx.enter_context(nc.Block())
        flat = "p b n -> p (b n)"
        lv = [mm for mm in range(LEVELS)]

        def halves(a, m):
            return a[:, :].rearrange("p (k h e) -> p k h e", h=2, e=1 << m)

        def per(a, m):
            return a[:, :].rearrange("p (k h) -> p k h", h=2)

        @block.sync
        def _(sp):
            sp.dma_start(lamb[:, :], t["lambda_cols"]).then_inc(s_w, 16)
            sp.dma_start(miu[:, :], t["miu_col"]).then_inc(s_w, 16)
            sp.dma_start(td_miu[:, :], t["td_miu_col"]).then_inc(s_w, 16)
            sp.dma_start(bonus[:, :], t["u_col"]).then_inc(s_w, 16)
            sp.dma_start(gamma[:, :], t["gn_gamma_col"]).then_inc(s_w, 16)
            sp.dma_start(beta[:, :], t["gn_beta_col"]).then_inc(s_w, 16)
            sp.dma_start(a_lora[:, :], t["L0_attn_A_lora"]).then_inc(s_w, 16)
            sp.dma_start(b_pad[:, :, :], t["b_lora_rows"].rearrange("f k n -> k f n")).then_inc(s_w, 16)
            sp.dma_start(td_a[:, :], t["L0_attn_td_A"]).then_inc(s_w, 16)
            sp.dma_start(td_b[:, :], t["L0_attn_td_B"]).then_inc(s_w, 16)
            sp.dma_start(wT[:, :, :], t["rwkv_wT"].rearrange("w k n -> k w n")).then_inc(s_w, 16)
        LOADS = 16 * 11

        def iteration_free(eng, i):
            eng.wait_ge(s_iter, i * 2 + 2)

        @block.vector
        def _(dve):
            dve.wait_ge(s_w, LOADS)
            dve.memset(state[:, :, :], 0.0).then_inc(s_zero, 1)
            dve.memset(att[:, :, :], 0.0).then_inc(s_zero, 1)
            dve.memset(hT[:, :, P:P + 1], 0.0).then_inc(s_zero, 1)
            for c in range(TILES):
                dve.bn_stats(stats[:, c, :], x_bc[:, c // CHUNKS, c % CHUNKS, :]).then_inc(s_stat, 1)
            dve.wait_ge(s_stat, TILES)
            for c in range(TILES):
                dve.bn_aggr(mv[:, c, :], stats[:, c, :]).then_inc(s_var, 1)
            dve.wait_ge(s_rstd, 2)
            dve.wait_ge(s_zero, 3)
            with dve.Fori(0, CHUNKS) as i:
                iteration_free(dve, i)
                dve.tensor_copy(hT[:, :, 0:1], hT[:, :, P:P + 1]).then_inc(s_xn, 1)
                for b in range(BATCH):
                    dve.tensor_scalar(xn[:, b, :], x_bc[:, b, bass.ds(i, 1), :],
                                      mv[:, bass.ds(i + b * CHUNKS, 1), 0:1], rstd[:, bass.ds(i + b * CHUNKS, 1)],
                                      ALU.subtract, ALU.mult).then_inc(s_xn, 1)
                dve.wait_ge(s_dxa, i + 1)
                dve.scalar_tensor_tensor(out=xm[:, :, :], in0=dxa[:, :, :], scalar=miu[:, 0:1], in1=hT[:, :, 1:],
                                         op0=ALU.mult, op1=ALU.add).then_inc(s_xm, 1)
                for f in range(MIXES):
                    if f % 2 == 0:
                        dve.wait_ge(s_mix, i * 3 + (f // 2 + 1))
                    src = bank[(2, 3, 4)[f // 2]][:, f % 2 * N:(f % 2 + 1) * N].rearrange("p (b n) -> p b n", b=BATCH)
                    dve.scalar_tensor_tensor(out=xx[:, f], in0=src, scalar=lamb[:, f:f + 1], in1=dxa[:, :, :],
                                             op0=ALU.add, op1=ALU.mult).then_inc(s_scaled, 1)
                dve.wait_ge(s_evac, i * 3 + 3)
                rh, kh = halves(rl[0], 0), halves(kl[0], 0)
                dve.tensor_scalar(halves(rd, 0)[:, :, 0], rh[:, :, 0], bonus[:, 0:1], None, ALU.mult).then_inc(s_diag, 1)
                dve.tensor_copy(halves(rd, 0)[:, :, 1], rh[:, :, 1]).then_inc(s_diag, 1)
                dve.tensor_copy(halves(kd, 0)[:, :, 0], kh[:, :, 0]).then_inc(s_diag, 1)
                dve.tensor_scalar(halves(kd, 0)[:, :, 1], kh[:, :, 1], bonus[:, 0:1], None, ALU.mult).then_inc(s_diag, 1)
                dve.wait_ge(s_ew, i * 2 + 2)
                for m in lv:
                    if m:
                        dve.wait_ge(s_tot, i * LEVELS + m)
                        dve.wait_ge(s_r, i * LEVELS + m)
                        dve.wait_ge(s_rc, i * 2 * LEVELS + 2 * m)
                    tp = per(tot[m], m)
                    dve.tensor_tensor(tot[m + 1][:, :], tp[:, :, 0], tp[:, :, 1], ALU.mult).then_inc(s_tot, 1)
                    dve.tensor_tensor(halves(rl[m + 1], m)[:, :, 1], halves(rl[m], m)[:, :, 1],
                                      tp[:, :, 0:1].to_broadcast([P, N >> (m + 1), 1 << m]), ALU.mult).then_inc(s_r, 1)
                dve.wait_ge(s_gT, i + 1)
                dve.tensor_scalar(eg[:, :], eg[:, :], 1.0, None, ALU.add).then_inc(s_gate, 1)
                dve.wait_ge(s_gate, i * 3 + 1)
                dve.reciprocal(eg[:, :], eg[:, :]).then_inc(s_gate, 1)
                dve.wait_ge(s_gate, i * 3 + 2)
                dve.tensor_tensor(gT[:, :], eg[:, :], bank[4][:, 0:N], ALU.mult).then_inc(s_gate, 1)
                scores = pair[:, :].rearrange("p (u n) -> p u n", u=4)
                dve.wait_ge(s_leafmm, i + 1)
                dve.tensor_tensor(prod[:, :, :], scores[:, :, 0:160],
                                  cst("leaf")[:, None, :].to_broadcast([P, 4, 160]), ALU.mult).then_inc(s_prod, 1)
                dve.wait_ge(s_prod, i + 1)
                dve.tensor_reduce(leafs[:, :, :], prod[:, :, :].rearrange("p u (l n) -> p u n l", n=LEAF), AX.X,
                                  ALU.add).then_inc(s_leaf, 1)
                dve.wait_ge(s_leaf, i + 1)
                for q in range(4):
                    rows = slice(q * LEAF, (q + 1) * LEAF)
                    dve.tensor_copy(att[rows, :, rows], leafs[rows, :, :]).then_inc(s_att, 1)
                dve.wait_ge(s_kv, i + 1)
                dve.tensor_tensor(kv[:, :, :], bank[5][:, N:2 * N].rearrange("p (b n) -> p b n", b=BATCH),
                                  cst("head2")[:, None, :].to_broadcast([P, BATCH, P]), ALU.mult).then_inc(s_state, 1)
                dve.wait_ge(s_state, i * 3 + 1)
                for b in range(BATCH):
                    dve.scalar_tensor_tensor(out=state[:, b, :], in0=state[:, b, :], scalar=tot[LEVELS][:, b:b + 1],
                                             in1=kv[:, b, :], op0=ALU.mult, op1=ALU.add).then_inc(s_state, 1)
                y = bank[5][:, 0:N].rearrange("p (u n) -> p u n", u=4)
                for u in range(4):
                    dve.bn_stats(gst[:, u, :], y[:, u, :]).then_inc(s_gn, 1)
                dve.wait_ge(s_gn, i * 8 + 4)
                dve.nop(nofuse=True)
                for u in range(4):
                    dve.bn_aggr(gmv[:, u, :], gst[:, u, :]).then_inc(s_gn, 1)
                dve.wait_ge(s_grs, i * 2 + 2)
                for u in range(4):
                    dve.tensor_scalar(yn[:, u // 2, (u % 2) * RW_DIM:(u % 2 + 1) * RW_DIM], y[:, u, :], gmv[:, u, 0:1],
                                      grs[:, u:u + 1], ALU.subtract, ALU.mult).then_inc(s_yn, 1)
                dve.wait_ge(s_state, i * 3 + 3)
                dve.sem_inc(s_iter, 1)
                dve.wait_ge(s_o, i + 1)
                dve.tensor_tensor(gated[:, :, :], bank[2][:, 0:N].rearrange("p (b n) -> p b n", b=BATCH),
                                  mod_row[:, 0, 0], ALU.mult).then_inc(s_gated, 1)

        @block.gpsimd
        def _(pool):
            pool.sem_inc(s_iter, 2)
            pool.wait_ge(s_var, TILES)
            pool.tensor_scalar(rstd[:, :], mv[:, :, 1], LN_EPS, None, ALU.add).then_inc(s_rstd, 1)
            pool.wait_ge(s_rstd, 1)
            pool.tensor_tensor(rstd[:, :], rstd[:, :], eps_pow[:, 0:TILES], ALU.pow).then_inc(s_rstd, 1)
            with pool.Fori(0, CHUNKS) as i:
                iteration_free(pool, i)
                pool.wait_ge(s_ht, i * 2 + 2)
                pool.wait_ge(s_xn, i * 3 + 1)
                pool.tensor_tensor(dxa[:, :, :], hT[:, :, 0:P], hT[:, :, 1:], ALU.subtract).then_inc(s_dxa, 1)
                for f in range(MIXES):
                    pool.wait_ge(s_scaled, i * MIXES + (f + 1))
                    pool.tensor_tensor(xx[:, f], xx[:, f], hT[:, :, 1:], ALU.add).then_inc(s_xx, 1)
                pool.wait_ge(s_evac, i * 3 + 3)
                pool.wait_ge(s_ew, i * 2 + 2)
                for m in lv:
                    if m:
                        pool.wait_ge(s_tot, i * LEVELS + m)
                        pool.wait_ge(s_k, i * LEVELS + m)
                        pool.wait_ge(s_rc, i * 2 * LEVELS + 2 * m)
                    pool.tensor_tensor(halves(kl[m + 1], m)[:, :, 0], halves(kl[m], m)[:, :, 0],
                                       per(tot[m], m)[:, :, 1:2].to_broadcast([P, N >> (m + 1), 1 << m]),
                                       ALU.mult).then_inc(s_k, 1)
                pool.wait_ge(s_gn, i * 8 + 8)
                pool.nop(nofuse=True)
                pool.tensor_scalar(grs[:, :], gmv[:, :, 1], GN_EPS, None, ALU.add).then_inc(s_grs, 1)
                pool.wait_ge(s_grs, i * 2 + 1)
                pool.tensor_tensor(grs[:, :], grs[:, :], eps_pow[:, 0:4], ALU.pow).then_inc(s_grs, 1)
                pool.wait_ge(s_z, i + 1)
                pool.wait_ge(s_gate, i * 3 + 3)
                pool.tensor_tensor(zT[:, :, :], zT[:, :, :], gT[:, :].rearrange("p (b n) -> p b n", b=BATCH),
                                   ALU.mult).then_inc(s_zg, 1)
                pool.wait_ge(s_gated, i + 1)
                pool.tensor_tensor(x_bc[:, :, bass.ds(i, 1), :], x_bc[:, :, bass.ds(i, 1), :],
                                   gated[:, :, None, :], ALU.add).then_inc(s_iter, 1)
            pool.wait_ge(s_iter, 2 * CHUNKS + 2)

        @block.scalar
        def _(act):
            act.wait_ge(s_w, LOADS)
            with act.Fori(0, CHUNKS) as i:
                iteration_free(act, i)
                act.wait_ge(s_xt, i + 1)
                act.wait_ge(s_xn, i * 3 + 1)
                for b in range(BATCH):
                    act.activation(hT[:, b, 1:], bank[0][:, b * P:(b + 1) * P], ACT.Identity,
                                   bias=mod_col[:, 0, 0, b:b + 1], scale=mod_col[:, 0, 1, b:b + 1]).then_inc(s_ht, 1)
                act.wait_ge(s_lora, i + 1)
                act.activation(lh[:, :], bank[1][:, 0:N], ACT.Tanh).then_inc(s_lh, 1)
                act.activation(lh4[:, :], bank[1][0:LORA, N:2 * N], ACT.Tanh).then_inc(s_lh, 1)
                act.wait_ge(s_td, i * 2 + 1)
                act.activation(tw[:, :], bank[1][0:TD_RANK, 0:N], ACT.Tanh).then_inc(s_tw, 1)
                act.wait_ge(s_proj, i * 4 + 1)
                act.activation(kl[0][:, :], bank[2][:, 0:N], ACT.Copy).then_inc(s_evac, 1)
                act.wait_ge(s_td, i * 2 + 2)
                act.activation(ew[:, :], bank[1][:, N:2 * N], ACT.Exp, bias=td_miu[:, 0:1]).then_inc(s_ew, 1)
                act.wait_ge(s_ew, i * 2 + 1)
                act.activation(tot[0][:, :], ew[:, :], ACT.Exp, scale=-1.0).then_inc(s_ew, 1)
                act.wait_ge(s_proj, i * 4 + 2)
                act.activation(v_sb[:, :, :], bank[0][:, 0:N].rearrange("p (b n) -> p b n", b=BATCH),
                               ACT.Copy).then_inc(s_evac, 1)
                act.wait_ge(s_proj, i * 4 + 3)
                act.activation(rl[0][:, :], bank[3][:, 0:N], ACT.Copy).then_inc(s_evac, 1)
                act.wait_ge(s_proj, i * 4 + 4)
                act.activation(eg[:, :], bank[4][:, 0:N], ACT.Exp, scale=-1.0).then_inc(s_gT, 1)
                act.wait_ge(s_evac, i * 3 + 3)
                for m in lv:
                    if m:
                        act.wait_ge(s_r, i * LEVELS + m)
                        act.wait_ge(s_k, i * LEVELS + m)
                        act.wait_ge(s_rc, i * 2 * LEVELS + 2 * m)
                    act.activation(halves(rl[m + 1], m)[:, :, 0], halves(rl[m], m)[:, :, 0],
                                   ACT.Copy).then_inc(s_rc, 1)
                    act.activation(halves(kl[m + 1], m)[:, :, 1], halves(kl[m], m)[:, :, 1],
                                   ACT.Copy).then_inc(s_rc, 1)
                scores = pair[:, :].rearrange("p (u n) -> p u n", u=4)
                act.wait_ge(s_leaf, i + 1)
                act.activation(att[0:64, :, 64:128], scores[0:64, :, 160:224], ACT.Copy).then_inc(s_off, 1)
                act.activation(att[0:32, :, 32:64], scores[0:32, :, 224:256], ACT.Copy).then_inc(s_off, 1)
                act.activation(att[64:96, :, 96:128], scores[64:96, :, 224:256], ACT.Copy).then_inc(s_off, 1)
                act.wait_ge(s_ktT, i + 1)
                act.activation(ktm[:, :, :], bank[1][:, 0:N].rearrange("p (b n) -> p b n", b=BATCH),
                               ACT.Copy).then_inc(s_ktm, 1)
                act.wait_ge(s_zt, i + 1)
                act.activation(zT[:, :, :], bank[0][:, 0:N].rearrange("p (b n) -> p b n", b=BATCH), ACT.Identity,
                               bias=beta[:, 0:1], scale=gamma[:, 0:1]).then_inc(s_z, 1)

        @block.tensor
        def _(pe):
            pe.wait_ge(s_w, LOADS)
            with pe.Fori(0, CHUNKS) as i:
                iteration_free(pe, i)
                pe.wait_ge(s_xn, i * 3 + 3)
                for b in range(BATCH):
                    last = pe.transpose(bank[0][:, b * P:(b + 1) * P], xn[:, b, :], cst("ident"))
                last.then_inc(s_xt, 1)
                pe.wait_ge(s_xm, i + 1)
                pe.matmul(bank[1][:, 0:N], a_lora[:, 0:P], xm[:, :, :].rearrange(flat), start=True, stop=True)
                pe.matmul(bank[1][0:LORA, N:2 * N], a_lora[:, P:P + LORA], xm[:, :, :].rearrange(flat),
                          start=True, stop=True).then_inc(s_lora, 1)
                pe.wait_ge(s_lh, i * 2 + 2)
                for f in range(4):
                    mm = pe.matmul(bank[2 + f // 2][:, f % 2 * N:(f % 2 + 1) * N], b_pad[:, f, :], lh[:, :],
                                   start=True, stop=True)
                    if f % 2:
                        mm.then_inc(s_mix, 1)
                pe.matmul(bank[4][:, 0:N], b_pad[0:LORA, 4, :], lh4[:, :], start=True, stop=True).then_inc(s_mix, 1)
                pe.wait_ge(s_xx, i * MIXES + 1)
                pe.matmul(bank[1][0:TD_RANK, 0:N], td_a[:, :], xx[:, 0].rearrange(flat), start=True,
                          stop=True).then_inc(s_td, 1)
                pe.wait_ge(s_xx, i * MIXES + 2)
                pe.matmul(bank[2][:, 0:N], wT[:, 0, :], xx[:, 1].rearrange(flat), start=True,
                          stop=True).then_inc(s_proj, 1)
                pe.wait_ge(s_tw, i + 1)
                pe.matmul(bank[1][:, N:2 * N], td_b[:, :], tw[:, :], start=True, stop=True).then_inc(s_td, 1)
                pe.wait_ge(s_xx, i * MIXES + 3)
                for b in range(BATCH):
                    last = pe.matmul(bank[0][:, b * P:(b + 1) * P], xx[:, 2, b, :], wT[:, 1, :], start=True, stop=True)
                last.then_inc(s_proj, 1)
                pe.wait_ge(s_xx, i * MIXES + 4)
                pe.matmul(bank[3][:, 0:N], wT[:, 2, :], xx[:, 3].rearrange(flat), start=True,
                          stop=True).then_inc(s_proj, 1)
                pe.wait_ge(s_xx, i * MIXES + 5)
                pe.matmul(bank[4][:, 0:N], wT[:, 3, :], xx[:, 4].rearrange(flat), start=True,
                          stop=True).then_inc(s_proj, 1)

                def leaf_scores(slot, k_op, r_op):
                    for u in range(4):
                        h, b = u // 2, u % 2
                        rows = slice(h * RW_DIM, (h + 1) * RW_DIM)
                        for q in range(4):
                            cols = slice(b * P + q * LEAF, b * P + (q + 1) * LEAF)
                            pe.matmul(pair[q * LEAF:(q + 1) * LEAF, u * 256 + slot * LEAF:u * 256 + (slot + 1) * LEAF],
                                      k_op[rows, cols], r_op[rows, cols], start=True, stop=True,
                                      tile_position=(h * RW_DIM, q * LEAF))

                pe.wait_ge(s_diag, i * 4 + 4)
                pe.nop(nofuse=True)
                leaf_scores(0, kd, rd)
                for m in (1, 2, 3, 4):
                    pe.wait_ge(s_r, i * LEVELS + m)
                    pe.wait_ge(s_k, i * LEVELS + m)
                    pe.wait_ge(s_rc, i * 2 * LEVELS + 2 * m)
                    pe.nop(nofuse=True)
                    leaf_scores(m, kl[m], rl[m])
                pe.wait_ge(s_r, i * LEVELS + 6)
                pe.wait_ge(s_k, i * LEVELS + 6)
                pe.wait_ge(s_rc, i * 2 * LEVELS + 12)
                pe.nop(nofuse=True)
                for u in range(4):
                    h, b = u // 2, u % 2
                    rows = slice(h * RW_DIM, (h + 1) * RW_DIM)
                    for q in (0, 2):
                        s0 = b * P + q * LEAF
                        pe.matmul(pair[q * LEAF:(q + 1) * LEAF, u * 256 + 224:u * 256 + 256],
                                  kl[5][rows, s0:s0 + LEAF], rl[5][rows, s0 + LEAF:s0 + 2 * LEAF], start=True,
                                  stop=True, tile_position=(h * RW_DIM, q * LEAF))
                    last = pe.matmul(pair[0:64, u * 256 + 160:u * 256 + 224], kl[6][rows, b * P:b * P + 64],
                                     rl[6][rows, b * P + 64:b * P + 128], start=True, stop=True,
                                     tile_position=(h * RW_DIM, 0))
                last.then_inc(s_leafmm, 1)
                pe.wait_ge(s_k, i * LEVELS + 7)
                pe.wait_ge(s_r, i * LEVELS + 7)
                pe.wait_ge(s_rc, i * 2 * LEVELS + 14)
                for b in range(BATCH):
                    last = pe.transpose(bank[1][:, b * P:(b + 1) * P], kl[7][:, b * P:(b + 1) * P], cst("ident"))
                last.then_inc(s_ktT, 1)
                pe.wait_ge(s_att, i * 4 + 4)
                pe.wait_ge(s_off, i * 3 + 3)
                pe.wait_ge(s_evac, i * 3 + 3)
                for b in range(BATCH):
                    pe.matmul(bank[5][:, b * P:(b + 1) * P], rl[7][:, b * P:(b + 1) * P], state[:, b, :],
                              start=True, stop=False, skip_group_check=True)
                    for h in range(RW_HEADS):
                        pe.matmul(bank[5][:, b * P + h * RW_DIM:b * P + (h + 1) * RW_DIM], att[:, h * BATCH + b, :],
                                  v_sb[:, b, h * RW_DIM:(h + 1) * RW_DIM], start=False, stop=True,
                                  skip_group_check=True)
                pe.wait_ge(s_ktm, i + 1)
                for b in range(BATCH):
                    last = pe.matmul(bank[5][:, N + b * P:N + (b + 1) * P], ktm[:, b, :], v_sb[:, b, :], start=True,
                                     stop=True, skip_group_check=True)
                last.then_inc(s_kv, 1)
                pe.wait_ge(s_yn, i * 4 + 4)
                for b in range(BATCH):
                    last = pe.transpose(bank[0][:, b * P:(b + 1) * P], yn[:, b, :], cst("ident"))
                last.then_inc(s_zt, 1)
                pe.wait_ge(s_zg, i + 1)
                for b in range(BATCH):
                    last = pe.matmul(bank[2][:, b * P:(b + 1) * P], zT[:, b, :], wT[:, 4, :], start=True, stop=True)
                last.then_inc(s_o, 1)


def expert_route_phase(nc, t, x_bc, eps_pow, sbw, bank, cst, keep):
    with ExitStack() as ctx:
        def sb(name, shape, dt=F32):
            return ctx.enter_context(nc.sbuf_tensor(name, shape, dt))

        def sem(name):
            return nc.alloc_semaphore(name)

        router = sb("router", [P, E0])
        zero = sb("zero", [P, 1024])
        st = sb("r_st", [P, BATCH, 6])
        mv = sb("r_mv", [P, BATCH, 2])
        rstd = sb("r_rstd", [P, BATCH])
        xn = sb("r_xn", [P, BATCH, C])
        h = sb("r_h", [P, BATCH, C])
        h_all = sb("r_h_all", [P, TILES, C])
        h_bc = h_all[:, :, :].rearrange("p (b c) n -> p b c n", b=BATCH)
        hT = sb("r_hT", [P, BATCH, P])
        lg = sb("r_lg", [P, BATCH, E0])
        mx = sb("r_mx", [P, BATCH, 8])
        idx = sb("r_idx", [P, BATCH, 8], U32)
        idf = sb("r_idf", [P, BATCH])
        oh = sb("r_oh", [P, BATCH, E0])
        oh_all = sb("r_oh_all", [P, TILES, E0])
        oh_bc = oh_all[:, :, :].rearrange("p (b c) n -> p b c n", b=BATCH)
        seen = sb("r_seen", [P, E0])
        pick = sb("r_pick", [P, BATCH, E0])
        rank = sb("r_rank", [P, TILES])
        rank_bc = rank[:, :].rearrange("p (b c) -> p b c", b=BATCH)
        top = sb("r_top", [P, TILES])
        top_bc = top[:, :].rearrange("p (b c) -> p b c", b=BATCH)
        cnt_i = sb("r_cnt_i", [P, E0], I32)
        ntile = sb("r_ntile", [P, E0])
        ends = sb("r_ends", [P, E0])
        base = sb("r_base", [P, E0])
        pick_all = sb("r_pick_all", [P, TILES, E0])
        le = sb("r_le", [1, SLOT_TILES, E0])
        te = sb("r_te", [1, SLOT_TILES])

        s_in, s_zero, s_fill = sem("r_in"), sem("r_zero"), sem("r_fill")
        s_st, s_mv, s_rstd, s_xn = sem("r_s_st"), sem("r_s_mv"), sem("r_s_rstd"), sem("r_s_xn")
        s_h, s_xt, s_ht, s_hall = sem("r_s_h"), sem("r_s_xt"), sem("r_s_ht"), sem("r_s_hall")
        s_logit, s_lg, s_mx, s_idx = sem("r_s_logit"), sem("r_s_lg"), sem("r_s_mx"), sem("r_s_idx")
        s_idf, s_oh, s_rank, s_pick = sem("r_s_idf"), sem("r_s_oh"), sem("r_s_rank"), sem("r_s_pick")
        s_tile, s_seen, s_cnt, s_step, s_exp = (sem("r_s_tile"), sem("r_s_seen"), sem("r_s_cnt"), sem("r_s_step"),
                                               sem("r_s_exp"))
        s_sent = sem("r_s_sent")
        block = ctx.enter_context(nc.Block())

        @block.sync
        def _(sp):
            sp.dma_start(router[:, :], t["L0_ffn_router_w"]).then_inc(s_in, 16)
            sp.wait_ge(s_zero, 1)
            slots = t["slots_in"].rearrange("(q p a) n -> q p (a n)", p=P, a=8)
            for q in range(SLOTS * C // (P * 1024)):
                sp.dma_start(slots[q], zero[:, :]).then_inc(s_fill, 16)
            sp.wait_ge(s_fill, 16 * (SLOTS * C // (P * 1024)))

        @block.gpsimd
        def _(pool):
            pool.memset(zero[:, :], 0.0).then_inc(s_zero, 1)
            pool.sem_inc(s_tile, 1)
            with pool.Fori(0, CHUNKS) as i:
                pool.wait_ge(s_mv, i * 2 + 2)
                pool.nop(nofuse=True)
                pool.tensor_scalar(rstd[:, :], mv[:, :, 1], LN_EPS, None, ALU.add).then_inc(s_rstd, 1)
                pool.wait_ge(s_rstd, i * 2 + 1)
                pool.tensor_tensor(rstd[:, :], rstd[:, :], eps_pow[:, 0:BATCH], ALU.pow).then_inc(s_rstd, 1)
                pool.wait_ge(s_xn, i * 2 + 2)
                pool.wait_ge(s_hall, i + 1)
                pool.tensor_tensor(h[:, :, :], xn[:, :, :], sbw[:, 1], ALU.mult).then_inc(s_h, 1)
                pool.wait_ge(s_h, i * 2 + 1)
                pool.tensor_tensor(h[:, :, :], h[:, :, :], sbw[:, 0], ALU.add).then_inc(s_h, 1)
            pool.wait_ge(s_fill, 16 * (SLOTS * C // (P * 1024)))
            pool.wait_ge(s_step, 10)
            pool.wait_ge(s_hall, CHUNKS + 1)
            for c in range(TILES):
                pool.indirect_dma_start(out=t["slots_in"], out_offset=bass.IndirectOffsetOnAxis(
                    ap=keep["slot"][:, c:c + 1], axis=0), in_=h_all[:, c, :], in_offset=None).then_inc(s_sent, 16)
            pool.wait_ge(s_sent, 16 * TILES)

        @block.scalar
        def _(act):
            act.sem_inc(s_hall, 1)
            with act.Fori(0, CHUNKS) as i:
                act.wait_ge(s_xt, i + 1)
                act.activation(hT[:, :, :], bank[0][:, 0:BATCH * P].rearrange("p (b n) -> p b n", b=BATCH),
                               ACT.Copy).then_inc(s_ht, 1)
                act.activation(h_bc[:, :, bass.ds(i, 1), :], h[:, :, None, :], ACT.Copy).then_inc(s_hall, 1)
            act.wait_ge(s_tile, CHUNKS + 1)
            act.activation(keep["weight"][:, :], top[:, :], ACT.Exp, scale=-1.0).then_inc(s_exp, 1)

        @block.vector
        def _(dve):
            dve.memset(seen[:, :], 0.0).then_inc(s_seen, 1)
            with dve.Fori(0, CHUNKS) as i:
                for b in range(BATCH):
                    dve.bn_stats(st[:, b, :], x_bc[:, b, bass.ds(i, 1), :]).then_inc(s_st, 1)
                dve.wait_ge(s_st, i * 2 + 2)
                dve.nop(nofuse=True)
                for b in range(BATCH):
                    dve.bn_aggr(mv[:, b, :], st[:, b, :]).then_inc(s_mv, 1)
                dve.wait_ge(s_rstd, i * 2 + 2)
                for b in range(BATCH):
                    dve.tensor_scalar(xn[:, b, :], x_bc[:, b, bass.ds(i, 1), :], mv[:, b, 0:1], rstd[:, b:b + 1],
                                      ALU.subtract, ALU.mult).then_inc(s_xn, 1)
                dve.wait_ge(s_logit, i + 1)
                dve.tensor_copy(lg[:, :, :], bank[1][:, 0:BATCH * E0].rearrange("p (b n) -> p b n",
                                                                                b=BATCH)).then_inc(s_lg, 1)
                dve.wait_ge(s_lg, i + 1)
                dve.nop(nofuse=True)
                for b in range(BATCH):
                    dve.max(mx[:, b, :], lg[:, b, :]).then_inc(s_mx, 1)
                dve.wait_ge(s_mx, i * 2 + 2)
                dve.nop(nofuse=True)
                for b in range(BATCH):
                    dve.max_index(idx[:, b, :], mx[:, b, :], lg[:, b, :]).then_inc(s_idx, 1)
                dve.wait_ge(s_idx, i * 2 + 2)
                dve.tensor_copy(idf[:, :], idx[:, :, 0]).then_inc(s_idf, 1)
                dve.tensor_copy(top_bc[:, :, bass.ds(i, 1)], mx[:, :, 0:1]).then_inc(s_tile, 1)
                dve.wait_ge(s_idf, i + 1)
                for b in range(BATCH):
                    dve.tensor_scalar(oh[:, b, :], cst("iota16"), idf[:, b:b + 1], None, ALU.is_equal).then_inc(s_oh, 1)
                dve.wait_ge(s_oh, i * 2 + 2)
                dve.tensor_copy(oh_bc[:, :, bass.ds(i, 1), :], oh[:, :, None, :]).then_inc(s_pick, 1)
                dve.wait_ge(s_rank, i + 1)
                dve.tensor_tensor(pick[:, :, :], bank[2][:, 0:BATCH * E0].rearrange("p (b n) -> p b n", b=BATCH),
                                  oh[:, :, :], ALU.mult).then_inc(s_pick, 1)
                dve.tensor_tensor(seen[:, :], seen[:, :], oh[:, 0, :], ALU.add).then_inc(s_seen, 1)
                dve.wait_ge(s_pick, i * 3 + 2)
                dve.tensor_reduce(rank_bc[:, :, bass.ds(i, 1)], pick[:, :, None, :], AX.X, ALU.add).then_inc(s_pick, 1)
                dve.wait_ge(s_seen, i * 2 + 2)
                dve.tensor_tensor(seen[:, :], seen[:, :], oh[:, 1, :], ALU.add).then_inc(s_seen, 1)
                dve.wait_ge(s_seen, i * 2 + 3)
            dve.wait_ge(s_exp, 1)
            dve.tensor_scalar(keep["weight"][:, :], keep["weight"][:, :], 1.0, None, ALU.add).then_inc(s_exp, 1)
            dve.wait_ge(s_exp, 2)
            dve.reciprocal(keep["weight"][:, :], keep["weight"][:, :]).then_inc(s_exp, 1)
            dve.wait_ge(s_cnt, 1)
            dve.tensor_scalar(cnt_i[:, :], bank[3][:, 0:E0], float(P - 1), None, ALU.add).then_inc(s_step, 1)
            dve.wait_ge(s_step, 1)
            dve.tensor_scalar(cnt_i[:, :], cnt_i[:, :], 7, None, ALU.logical_shift_right).then_inc(s_step, 1)
            dve.wait_ge(s_step, 2)
            dve.tensor_copy(ntile[:, :], cnt_i[:, :]).then_inc(s_step, 1)
            dve.wait_ge(s_step, 3)
            dve.tensor_tensor_scan(ends[:, :], cst("ones")[:, 0:E0], ntile[:, :], 0.0, ALU.mult,
                                   ALU.add).then_inc(s_step, 1)
            dve.wait_ge(s_step, 4)
            dve.tensor_tensor(base[:, :], ends[:, :], ntile[:, :], ALU.subtract).then_inc(s_step, 1)
            dve.wait_ge(s_step, 5)
            dve.tensor_tensor(pick_all[:, :, :], oh_all[:, :, :], base[:, None, :].to_broadcast([P, TILES, E0]),
                              ALU.mult).then_inc(s_step, 1)
            dve.wait_ge(s_step, 6)
            dve.tensor_reduce(top[:, :], pick_all[:, :, :], AX.X, ALU.add).then_inc(s_step, 1)
            dve.tensor_tensor(le[:, :, :], ends[0:1, None, :].to_broadcast([1, SLOT_TILES, E0]),
                              cst("iota32")[0:1, :, None].to_broadcast([1, SLOT_TILES, E0]),
                              ALU.is_le).then_inc(s_step, 1)
            dve.wait_ge(s_step, 8)
            dve.scalar_tensor_tensor(out=keep["slot"][:, :], in0=top[:, :], scalar=float(P), in1=rank[:, :],
                                     op0=ALU.mult, op1=ALU.add).then_inc(s_step, 1)
            dve.tensor_reduce(te[:, :], le[:, :, :], AX.X, ALU.add).then_inc(s_step, 1)
            dve.wait_ge(s_step, 10)
            dve.tensor_scalar(keep["expert"][:, :], te[:, :], float(E0 - 1), None, ALU.min).then_inc(s_step, 1)

        @block.tensor
        def _(pe):
            pe.wait_ge(s_in, 16)
            with pe.Fori(0, CHUNKS) as i:
                pe.wait_ge(s_h, i * 2 + 2)
                for b in range(BATCH):
                    last = pe.transpose(bank[0][:, b * P:(b + 1) * P], h[:, b, :], cst("ident"))
                last.then_inc(s_xt, 1)
                pe.wait_ge(s_ht, i + 1)
                for b in range(BATCH):
                    last = pe.matmul(bank[1][:, b * E0:(b + 1) * E0], hT[:, b, :], router[:, :], start=True, stop=True)
                last.then_inc(s_logit, 1)
                pe.wait_ge(s_oh, i * 2 + 2)
                pe.wait_ge(s_seen, i * 2 + 1)
                pe.matmul(bank[2][:, 0:E0], cst("before"), oh[:, 0, :], start=True, stop=False)
                pe.matmul(bank[2][:, 0:E0], cst("ones"), seen[:, :], start=False, stop=True)
                pe.matmul(bank[2][:, E0:2 * E0], cst("before"), oh[:, 1, :], start=True, stop=False)
                pe.matmul(bank[2][:, E0:2 * E0], cst("ones"), oh[:, 0, :], start=False, stop=False)
                pe.matmul(bank[2][:, E0:2 * E0], cst("ones"), seen[:, :], start=False, stop=True).then_inc(s_rank, 1)
            pe.wait_ge(s_seen, 2 * CHUNKS + 1)
            pe.matmul(bank[3][:, 0:E0], cst("ones"), seen[:, :], start=True, stop=True).then_inc(s_cnt, 1)


def expert_phase(nc, t, x_sb, mod_row, bank, cst, keep):
    with ExitStack() as ctx:
        def sb(name, shape, dt=F32):
            return ctx.enter_context(nc.sbuf_tensor(name, shape, dt))

        def sem(name):
            return nc.alloc_semaphore(name)

        DEPTH = 4
        W = 2 * F0 + 2
        weights = [sb(f"e_w{p}", [P, W]) for p in range(DEPTH)]
        b2 = [sb(f"e_b2{p}", [1, C]) for p in range(DEPTH)]
        xg = [sb(f"e_xg{p}", [P, C]) for p in range(DEPTH)]
        xgT = [sb(f"e_xgT{p}", [P, P]) for p in range(DEPTH)]
        hT = [sb(f"e_hT{p}", [P, 2, P]) for p in range(DEPTH)]
        yg = [sb(f"e_yg{p}", [P, C]) for p in range(DEPTH)]
        yt = sb("e_yt", [P, TILES, C])
        s_x = [sem(f"e_s_x{p}") for p in range(DEPTH)]
        s_wt = [sem(f"e_s_wt{p}") for p in range(DEPTH)]
        s_xt, s_xc, s_up, s_gelu = sem("e_s_xt"), sem("e_s_xc"), sem("e_s_up"), sem("e_s_gelu")
        s_down, s_y, s_st = sem("e_s_down"), sem("e_s_y"), [sem(f"e_s_st{p}") for p in range(DEPTH)]
        s_back, s_add = sem("e_s_back"), sem("e_s_add")
        block = ctx.enter_context(nc.Block())
        ROUNDS = SLOT_TILES // DEPTH

        def tr(p):
            return bank[p][:, 2 * P:3 * P]

        def down(p):
            return bank[p][:, 3 * P:4 * P]

        @block.sync
        def _(sp):
            sp.sem_inc(s_down, DEPTH)
            with sp.Fori(0, ROUNDS) as i:
                for p in range(DEPTH):
                    sp.wait_ge(s_down, i * DEPTH + p + 1)
                    j = i * DEPTH + p
                    e = sp.value_load(keep["expert"][0:1, bass.ds(j, 1)], min_val=0, max_val=E0 - 1)
                    sp.dma_start(weights[p][:, :], t["experts0"][bass.ds(e, 1), :, :].rearrange("e p n -> p (e n)"))\
                        .then_inc(s_wt[p], 16)
                    sp.dma_start(xg[p][:, :], t["slots_in"][bass.ds(j * P, P), :]).then_inc(s_x[p], 16)
                    sp.dma_start(b2[p][:, :], t["L0_ffn_b2"][bass.ds(e, 1), :]).then_inc(s_wt[p], 16)

        @block.scalar
        def _(act):
            for p in range(DEPTH):
                act.sem_inc(s_st[p], 16)
            with act.Fori(0, ROUNDS) as i:
                for p in range(DEPTH):
                    act.wait_ge(s_xt, i * DEPTH + p + 1)
                    act.activation(xgT[p][:, :], tr(p), ACT.Copy).then_inc(s_xc, 1)
                for p in range(DEPTH):
                    act.wait_ge(s_up, i * DEPTH + p + 1)
                    for k in range(2):
                        act.activation(hT[p][:, k, :], bank[p][:, k * P:(k + 1) * P], ACT.Gelu,
                                       bias=weights[p][:, 2 * F0 + k:2 * F0 + k + 1]).then_inc(s_gelu, 1)
                for p in range(DEPTH):
                    act.wait_ge(s_y, i * DEPTH + (p + 1 + DEPTH))
                    act.dma_start(t["slots_out"][bass.ds((i * DEPTH + p) * P, P), :], yg[p][:, :])\
                        .then_inc(s_st[p], 16)

        @block.vector
        def _(dve):
            with dve.Fori(0, ROUNDS) as i:
                for p in range(DEPTH):
                    dve.wait_ge(s_down, i * DEPTH + (p + 1 + DEPTH))
                    dve.wait_ge(s_st[p], i * 16 + 16)
                    dve.tensor_copy(yg[p][:, :], down(p)).then_inc(s_y, 1)
            gb = mod_row[:, 0, 1]
            for b in range(BATCH):
                dve.wait_ge(s_back, 16 * TILES)
                part = yt[:, b * CHUNKS:(b + 1) * CHUNKS, :]
                dve.tensor_tensor(part, part, gb[:, b, None, :].to_broadcast([P, CHUNKS, C]), ALU.mult)\
                    .then_inc(s_add, 1)
            dve.wait_ge(s_add, BATCH)
            for c in range(TILES):
                dve.scalar_tensor_tensor(out=x_sb[:, c, :], in0=yt[:, c, :], scalar=keep["weight"][:, c:c + 1],
                                         in1=x_sb[:, c, :], op0=ALU.mult, op1=ALU.add).then_inc(s_add, 1)
            dve.wait_ge(s_add, BATCH + TILES)

        @block.gpsimd
        def _(pool):
            pool.sem_inc(s_y, DEPTH)
            for p in range(DEPTH):
                pool.wait_ge(s_st[p], 16 * (ROUNDS + 1))
            for c in range(TILES):
                pool.indirect_dma_start(out=yt[:, c, :], out_offset=None, in_=t["slots_out"],
                                        in_offset=bass.IndirectOffsetOnAxis(ap=keep["slot"][:, c:c + 1], axis=0))\
                    .then_inc(s_back, 16)

        @block.tensor
        def _(pe):
            with pe.Fori(0, ROUNDS) as i:
                for p in range(DEPTH):
                    pe.wait_ge(s_x[p], i * 16 + 16)
                    pe.wait_ge(s_y, i * DEPTH + p + 1)
                    pe.transpose(tr(p), xg[p][:, :], cst("ident")).then_inc(s_xt, 1)
                for p in range(DEPTH):
                    pe.wait_ge(s_xc, i * DEPTH + p + 1)
                    pe.wait_ge(s_wt[p], i * 32 + 32)
                    for k in range(2):
                        last = pe.matmul(bank[p][:, k * P:(k + 1) * P], weights[p][:, k * P:(k + 1) * P], xgT[p][:, :],
                                         start=True, stop=True)
                    last.then_inc(s_up, 1)
                for p in range(DEPTH):
                    pe.wait_ge(s_gelu, i * 2 * DEPTH + (2 * p + 2))
                    for k in range(2):
                        pe.matmul(down(p), hT[p][:, k, :], weights[p][:, F0 + k * P:F0 + (k + 1) * P],
                                  start=(k == 0), stop=False)
                    pe.matmul(down(p), cst("ones")[0:1, :], b2[p][:, :], start=False, stop=True).then_inc(s_down, 1)


def norm_transpose_phase(nc, x_bc, eps_pow, mod_col, bank, cst, hT_all):
    with ExitStack() as ctx:
        def sb(name, shape, dt=F32):
            return ctx.enter_context(nc.sbuf_tensor(name, shape, dt))

        def sem(name):
            return nc.alloc_semaphore(name)

        st = sb("n_st", [P, TILES, 6])
        mv = sb("n_mv", [P, TILES, 2])
        rstd = sb("n_rstd", [P, TILES])
        xn = sb("n_xn", [P, BATCH, 2, C])
        hT_bc = hT_all[:, :, :].rearrange("p (b c) n -> p b c n", b=BATCH)
        s_st, s_mv, s_rstd = sem("n_s_st"), sem("n_s_mv"), sem("n_s_rstd")
        s_xn, s_xt, s_ht = sem("n_s_xn"), sem("n_s_xt"), sem("n_s_ht")
        block = ctx.enter_context(nc.Block())
        PAIRS = CHUNKS // 2

        @block.vector
        def _(dve):
            for c in range(TILES):
                dve.bn_stats(st[:, c, :], x_bc[:, c // CHUNKS, c % CHUNKS, :]).then_inc(s_st, 1)
            dve.wait_ge(s_st, TILES)
            for c in range(TILES):
                dve.bn_aggr(mv[:, c, :], st[:, c, :]).then_inc(s_mv, 1)
            dve.wait_ge(s_rstd, 2)
            dve.sem_inc(s_xt, 2)
            with dve.Fori(0, PAIRS) as i:
                for b in range(BATCH):
                    dve.wait_ge(s_xt, i * 2 + (b + 1))
                    for k in range(2):
                        at = i * 2 + (b * CHUNKS + k)
                        dve.tensor_scalar(xn[:, b, k, :], x_bc[:, b, bass.ds(i * 2 + k, 1), :],
                                          mv[:, bass.ds(at, 1), 0:1], rstd[:, bass.ds(at, 1)], ALU.subtract,
                                          ALU.mult).then_inc(s_xn, 1)

        @block.gpsimd
        def _(pool):
            pool.wait_ge(s_mv, TILES)
            pool.tensor_scalar(rstd[:, :], mv[:, :, 1], LN_EPS, None, ALU.add).then_inc(s_rstd, 1)
            pool.wait_ge(s_rstd, 1)
            pool.tensor_tensor(rstd[:, :], rstd[:, :], eps_pow[:, 0:TILES], ALU.pow).then_inc(s_rstd, 1)

        @block.tensor
        def _(pe):
            pe.sem_inc(s_ht, 2)
            with pe.Fori(0, PAIRS) as i:
                for b in range(BATCH):
                    pe.wait_ge(s_xn, i * 4 + (2 * b + 2))
                    pe.wait_ge(s_ht, i * 2 + (b + 1))
                    for k in range(2):
                        last = pe.transpose(bank[b][:, k * P:(k + 1) * P], xn[:, b, k, :], cst("ident"))
                    last.then_inc(s_xt, 1)

        @block.scalar
        def _(act):
            with act.Fori(0, PAIRS) as i:
                for b in range(BATCH):
                    act.wait_ge(s_xt, i * 2 + (b + 3))
                    act.activation(hT_bc[:, b, bass.ds(i * 2, 2), :],
                                   bank[b][:, 0:2 * P].rearrange("p (k n) -> p k n", k=2), ACT.Identity,
                                   bias=mod_col[:, 1, 0, b:b + 1], scale=mod_col[:, 1, 1, b:b + 1]).then_inc(s_ht, 1)


def hla_phase(nc, x_bc, mod_row, bank, pair, cst, hT_all, W, s_weights):
    with ExitStack() as ctx:
        def sb(name, shape, dt=F32):
            return ctx.enter_context(nc.sbuf_tensor(name, shape, dt))

        def sem(name):
            return nc.alloc_semaphore(name)

        J = range(GROUPS)
        hT = [sb(f"h_hT{b}", [P, P]) for b in range(BATCH)]
        v_sb = [sb(f"h_v{b}", [P, HL_HEADS * HL_DIM]) for b in range(BATCH)]
        qk = [sb(f"h_qk{j}", [P, 2, P]) for j in J]
        qkd = [sb(f"h_qkd{j}", [P, 2, P]) for j in J]
        qB = [sb(f"h_qB{j}", [P, HPG, P]) for j in J]
        kB = [sb(f"h_kB{j}", [P, HPG, P]) for j in J]
        kg = [sb(f"h_kg{j}", [P, 2, P]) for j in J]
        kqd = [sb(f"h_kqd{j}", [P, 2, P]) for j in J]
        m1 = [sb(f"h_m1{j}", [P, HPG, P]) for j in J]
        m2 = [sb(f"h_m2{j}", [P, HPG, P]) for j in J]
        m3 = [sb(f"h_m3{j}", [P, HPG, P]) for j in J]
        aT = [sb(f"h_aT{j}", [P, P]) for j in J]
        aTd = [sb(f"h_aTd{j}", [P, P]) for j in J]
        oT = [sb(f"h_oT{j}", [P, P]) for j in J]
        states = [[sb(f"h_state{b}{j}", [P, 3, P]) for j in J] for b in range(BATCH)]
        fresh = [sb(f"h_fresh{k}", [P, 3, P]) for k in range(2)]
        gated = sb("h_gated", [P, C])

        X = [k[:, :] for k in bank[0:4]]
        ring = [pair[:, 0:512], pair[:, 512:1024], bank[4][:, :]]
        upd = bank[5]
        s_zero, s_hT, s_v, s_vc = sem("h_s_zero"), sem("h_s_hT"), sem("h_s_v"), sem("h_s_vc")
        s_qk, s_qkc, s_qkd, s_bd = sem("h_s_qk"), sem("h_s_qkc"), sem("h_s_qkd"), sem("h_s_bd")
        s_tm, s_tmc, s_sc, s_mask = sem("h_s_tm"), sem("h_s_tmc"), sem("h_s_sc"), sem("h_s_mask")
        s_ga, s_gac, s_aTd, s_o, s_oc = sem("h_s_ga"), sem("h_s_gac"), sem("h_s_aTd"), sem("h_s_o"), sem("h_s_oc")
        s_upd, s_new, s_st, s_out = sem("h_s_upd"), sem("h_s_new"), sem("h_s_st"), sem("h_s_out")
        s_gated, s_x = sem("h_s_gated"), sem("h_s_x")
        block = ctx.enter_context(nc.Block())

        def nth(i, b, per_tile, k):
            return i * (BATCH * per_tile) + (b * per_tile + k + 1)

        hT_bc = hT_all[:, :, :].rearrange("p (b c) n -> p b c n", b=BATCH)
        heads = cst("head4")

        @block.gpsimd
        def _(pool):
            pool.sem_inc(s_v, 2)
            with pool.Fori(0, CHUNKS) as i:
                for b in range(BATCH):
                    pool.wait_ge(s_v, nth(i, b, 1, 1))
                    pool.nop(nofuse=True)
                    pool.tensor_tensor(hT[b][:, None, :], hT_bc[:, b, bass.ds(i, 1), :],
                                       cst("ones")[:, None, :], ALU.mult).then_inc(s_hT, 1)
                    for j in J:
                        pool.wait_ge(s_qkc, nth(i, b, GROUPS, j))
                        pool.wait_ge(s_o, nth(i, b, GROUPS, j))
                        for k, full in ((1, kB), (0, qB)):
                            pool.tensor_tensor(full[j][:, :, :], qk[j][:, k, None, :].to_broadcast([P, HPG, P]),
                                               heads[:, 0::HL_DIM, None].to_broadcast([P, HPG, P]),
                                               ALU.mult).then_inc(s_bd, 1)
                        pool.tensor_tensor(qkd[j][:, :, :], qk[j][:, :, :],
                                           cst("decay_row")[:, None, :].to_broadcast([P, 2, P]),
                                           ALU.mult).then_inc(s_qkd, 1)
                    pool.wait_ge(s_gated, nth(i, b, 1, 1))
                    pool.tensor_tensor(x_bc[:, b, bass.ds(i, 1), :], x_bc[:, b, bass.ds(i, 1), :],
                                       gated[:, None, :], ALU.add).then_inc(s_x, 1)
            pool.wait_ge(s_x, TILES + 1)

        @block.scalar
        def _(act):
            with act.Fori(0, CHUNKS) as i:
                for b in range(BATCH):
                    act.wait_ge(s_v, nth(i, b, 1, 2))
                    act.wait_ge(s_upd, nth(i, b, GROUPS, GROUPS - 1))
                    act.activation(v_sb[b][:, :], X[3], ACT.Copy).then_inc(s_vc, 1)
                    for j in J:
                        act.wait_ge(s_qk, nth(i, b, GROUPS, j))
                        act.activation(qk[j][:, :, :], X[j][:, 0:2 * P].rearrange("p (k n) -> p k n", k=2),
                                       ACT.Copy).then_inc(s_qkc, 1)
                    for j in J:
                        act.wait_ge(s_tm, nth(i, b, GROUPS, j))
                        act.activation(kg[j][:, 0, :], X[j][:, 2 * P:3 * P], ACT.Copy).then_inc(s_tmc, 1)
                        act.activation(kqd[j][:, :, :], X[j][:, 2 * P:4 * P].rearrange("p (k n) -> p k n", k=2),
                                       ACT.Copy, scale=cst("decay_col")[:, 0:1]).then_inc(s_tmc, 1)
                    for j in J:
                        act.wait_ge(s_ga, nth(i, b, GROUPS, j))
                        act.activation(aT[j][:, :], X[j][:, P:2 * P], ACT.Copy).then_inc(s_gac, 1)
                        act.activation(kg[j][:, 1, :], X[j][:, 0:P], ACT.Copy, scale=-1.0).then_inc(s_gac, 1)
                    for j in J:
                        act.wait_ge(s_o, nth(i, b, GROUPS, j + GROUPS))
                        act.activation(oT[j][:, :], X[j][:, 2 * P:3 * P], ACT.Copy).then_inc(s_oc, 1)

        @block.vector
        def _(dve):
            for b in range(BATCH):
                for j in J:
                    dve.memset(states[b][j][:, :, :], 0.0).then_inc(s_zero, 1)
            dve.wait_ge(s_zero, BATCH * GROUPS)
            dve.sem_inc(s_x, 1)
            dve.sem_inc(s_st, 2 * GROUPS)
            incl = cst("decay_incl")[:, None, :].to_broadcast([P, HPG, P])
            excl = cst("decay_excl")[:, None, :].to_broadcast([P, HPG, P])
            with dve.Fori(0, CHUNKS) as i:
                for b in range(BATCH):
                    n = 0
                    for kind, dsts, mask in ((0, (m1, m2), (incl, excl)), (1, (m3,), (incl,))):
                        for j in J:
                            for dst, msk in zip(dsts, mask):
                                dve.wait_ge(s_sc, nth(i, b, 12, n))
                                dve.tensor_tensor(dst[j][:, :, :], ring[n % 3].rearrange("p (h n) -> p h n", h=HPG),
                                                  msk, ALU.mult).then_inc(s_mask, 1)
                                n += 1
                        if kind == 0:
                            for j in J:
                                dve.wait_ge(s_gac, nth(i, b, 2 * GROUPS, 2 * j + 1))
                                dve.tensor_tensor(aTd[j][:, :], X[j][:, P:2 * P], cst("decay_row"),
                                                  ALU.mult).then_inc(s_aTd, 1)
                    for j in J:
                        dve.wait_ge(s_upd, nth(i, b, GROUPS, j + 2 * GROUPS))
                        dve.wait_ge(s_st, nth(i, b, GROUPS, j + 2 * GROUPS - 2))
                        dve.tensor_tensor(fresh[j % 2][:, :, :], upd[:, 0:3 * P].rearrange("p (k n) -> p k n", k=3),
                                          heads[:, None, :].to_broadcast([P, 3, P]), ALU.mult).then_inc(s_new, 1)
                        dve.wait_ge(s_new, nth(i, b, GROUPS, j + 1))
                        flat = "p k n -> p (k n)"
                        dve.scalar_tensor_tensor(out=states[b][j][:, :, :].rearrange(flat),
                                                 in0=states[b][j][:, :, :].rearrange(flat), scalar=GAMMA ** P,
                                                 in1=fresh[j % 2][:, :, :].rearrange(flat), op0=ALU.mult,
                                                 op1=ALU.add).then_inc(s_st, 1)
                    dve.wait_ge(s_out, nth(i, b, 1, 0))
                    dve.wait_ge(s_x, nth(i, b, 1, 0))
                    dve.tensor_tensor(gated[:, :], X[0][:, 3 * P:4 * P], mod_row[:, 1, 0, b, :],
                                      ALU.mult).then_inc(s_gated, 1)

        @block.tensor
        def _(pe):
            pe.wait_ge(s_weights, 16 * 4)
            pe.sem_inc(s_oc, GROUPS)
            pe.sem_inc(s_gated, 1)
            pe.sem_inc(s_o, GROUPS)
            pe.sem_inc(s_mask, 3)
            pe.sem_inc(s_new, 1)
            pe.sem_inc(s_upd, 2 * GROUPS)
            with pe.Fori(0, CHUNKS) as i:
                for b in range(BATCH):
                    pe.wait_ge(s_hT, nth(i, b, 1, 0))
                    pe.wait_ge(s_oc, nth(i, b, GROUPS, GROUPS - 1))
                    pe.matmul(X[3], hT[b][:, :], W["v"][:, :], start=True, stop=True).then_inc(s_v, 1)
                    for j in J:
                        if j == 0:
                            pe.wait_ge(s_gated, nth(i, b, 1, 0))
                        if j == 3:
                            pe.wait_ge(s_vc, nth(i, b, 1, 0))
                        cols = slice(j * P, (j + 1) * P)
                        pe.matmul(X[j][:, 0:P], W["q"][:, cols], hT[b][:, :], start=True, stop=True)
                        pe.matmul(X[j][:, P:2 * P], W["k"][:, cols], hT[b][:, :], start=True,
                                  stop=True).then_inc(s_qk, 1)
                    n = 0

                    def scores(j, lhs, rhs, n):
                        pe.wait_ge(s_mask, nth(i, b, 12, n))
                        for h in range(HPG):
                            last = pe.matmul(ring[n % 3][:, h * P:(h + 1) * P], lhs[:, h, :], rhs, start=True,
                                             stop=True)
                        last.then_inc(s_sc, 1)

                    for j in J:
                        pe.wait_ge(s_qkc, nth(i, b, GROUPS, j))
                        pe.transpose(X[j][:, 2 * P:3 * P], qk[j][:, 1, :], cst("ident"))
                        pe.transpose(X[j][:, 3 * P:4 * P], qk[j][:, 0, :], cst("ident")).then_inc(s_tm, 1)
                    for j in J:
                        pe.wait_ge(s_bd, nth(i, b, 2 * GROUPS, 2 * j))
                        scores(j, kB[j], qk[j][:, 0, :], 2 * j)
                        pe.wait_ge(s_bd, nth(i, b, 2 * GROUPS, 2 * j + 1))
                        scores(j, qB[j], qk[j][:, 1, :], 2 * j + 1)
                    for j in J:
                        pe.wait_ge(s_tmc, nth(i, b, 2 * GROUPS, 2 * j + 1))
                        pe.wait_ge(s_qkd, nth(i, b, GROUPS, j))
                        pe.wait_ge(s_st, nth(i, b, GROUPS, j))
                        pe.wait_ge(s_mask, nth(i, b, 12, 2 * j + 3 + 1))
                        if j == 0:
                            pe.wait_ge(s_vc, nth(i, b, 1, 0))
                        g, a = X[j][:, 0:P], X[j][:, P:2 * P]
                        pe.matmul(g, qkd[j][:, 1, :], states[b][j][:, 2, :], start=True, stop=False,
                                  skip_group_check=True)
                        for h in range(HPG):
                            rows = slice(h * HL_DIM, (h + 1) * HL_DIM)
                            pe.matmul(g[:, rows], m2[j][:, h, :],
                                      v_sb[b][:, j * P + h * HL_DIM:j * P + (h + 1) * HL_DIM], start=False,
                                      stop=True, skip_group_check=True)
                        pe.matmul(a, states[b][j][:, 0, :], qkd[j][:, 0, :], start=True, stop=False,
                                  skip_group_check=True)
                        for h in range(HPG):
                            rows = slice(h * HL_DIM, (h + 1) * HL_DIM)
                            last = pe.matmul(a[rows, :], kg[j][:, 0, rows], m1[j][:, h, :], start=False, stop=True,
                                             skip_group_check=True, tile_position=(0, h * HL_DIM))
                        last.then_inc(s_ga, 1)
                    for j in J:
                        pe.wait_ge(s_gac, nth(i, b, 2 * GROUPS, 2 * j))
                        scores(j, qB[j], aT[j][:, :], 8 + j)
                    for j in J:
                        pe.wait_ge(s_gac, nth(i, b, 2 * GROUPS, 2 * j + 1))
                        pe.wait_ge(s_aTd, nth(i, b, GROUPS, j))
                        pe.wait_ge(s_mask, nth(i, b, 12, 8 + j + 3))
                        o = X[j][:, 2 * P:3 * P]
                        pe.matmul(o, states[b][j][:, 2, :], aTd[j][:, :], start=True, stop=False,
                                  skip_group_check=True)
                        pe.matmul(o, states[b][j][:, 1, :], qkd[j][:, 0, :], start=False, stop=False,
                                  skip_group_check=True)
                        for h in range(HPG):
                            rows = slice(h * HL_DIM, (h + 1) * HL_DIM)
                            pe.matmul(o[rows, :], v_sb[b][:, j * P + h * HL_DIM:j * P + (h + 1) * HL_DIM],
                                      m3[j][:, h, :], start=False, stop=False, skip_group_check=True,
                                      tile_position=(0, h * HL_DIM))
                        for h in range(HPG):
                            rows = slice(h * HL_DIM, (h + 1) * HL_DIM)
                            last = pe.matmul(o[rows, :], kg[j][:, 1, rows], m1[j][:, h, :], start=False, stop=True,
                                             skip_group_check=True, tile_position=(0, h * HL_DIM))
                        last.then_inc(s_o, 1)
                        pe.wait_ge(s_new, nth(i, b, GROUPS, j))
                        pe.matmul(upd[:, 0:2 * P], kqd[j][:, 0, :], kg[j][:, :, :].rearrange("p k n -> p (k n)"),
                                  start=True, stop=True)
                        pe.matmul(upd[:, 2 * P:3 * P], kqd[j][:, 1, :], v_sb[b][:, j * P:(j + 1) * P], start=True,
                                  stop=True).then_inc(s_upd, 1)
                    for j in J:
                        pe.wait_ge(s_oc, nth(i, b, GROUPS, j + GROUPS))
                        last = pe.matmul(X[0][:, 3 * P:4 * P], oT[j][:, :], W["o"][:, j, :], start=(j == 0),
                                         stop=(j == GROUPS - 1))
                    last.then_inc(s_out, 1)


def swiglu_route_phase(nc, t, x_bc, eps_pow, sbw, bank, cst, xT_all, xsT_all):
    with ExitStack() as ctx:
        def sb(name, shape, dt=F32):
            return ctx.enter_context(nc.sbuf_tensor(name, shape, dt))

        def sem(name):
            return nc.alloc_semaphore(name)

        gate = sb("g_gate", [P, E1_LIVE])
        st = sb("g_st", [P, BATCH, 6])
        mv = sb("g_mv", [P, BATCH, 2])
        rstd = sb("g_rstd", [P, BATCH])
        xn = sb("g_xn", [P, BATCH, C])
        h = sb("g_h", [P, BATCH, C])
        hT = sb("g_hT", [P, BATCH, P])
        neg = sb("g_neg", [P, BATCH])
        prob = sb("g_prob", [P, BATCH, 8])
        mx = sb("g_mx", [P, BATCH, 8])
        idx = sb("g_idx", [P, BATCH, 8], U32)
        idf = sb("g_idf", [P, BATCH, 2])
        den = sb("g_den", [P, BATCH])
        cw = sb("g_cw", [P, 2, BATCH, E1_LIVE])
        hs = sb("g_hs", [P, BATCH, E1_LIVE, C])
        xT_bc = xT_all[:, :, :].rearrange("p (b c) n -> p b c n", b=BATCH)
        xsT_bc = xsT_all[:, :, :, :].rearrange("p e (b c) n -> p e b c n", b=BATCH)
        s_gate, s_pad, s_st, s_mv, s_rstd = sem("g_s_gate"), sem("g_s_pad"), sem("g_s_st"), sem("g_s_mv"), sem("g_s_rstd")
        s_xn, s_h, s_xt, s_ht, s_keep = sem("g_s_xn"), sem("g_s_h"), sem("g_s_xt"), sem("g_s_ht"), sem("g_s_keep")
        s_logit, s_neg, s_prob, s_mx, s_idx = (sem("g_s_logit"), sem("g_s_neg"), sem("g_s_prob"), sem("g_s_mx"),
                                              sem("g_s_idx"))
        s_cw, s_hs, s_hst, s_hsc = sem("g_s_cw"), sem("g_s_hs"), sem("g_s_hst"), sem("g_s_hsc")
        block = ctx.enter_context(nc.Block())

        @block.sync
        def _(sp):
            sp.dma_start(gate[:, :], t["gate_cols"]).then_inc(s_gate, 16)

        @block.gpsimd
        def _(pool):
            with pool.Fori(0, CHUNKS) as i:
                pool.wait_ge(s_mv, i * 2 + 2)
                pool.nop(nofuse=True)
                pool.tensor_scalar(rstd[:, :], mv[:, :, 1], LN_EPS, None, ALU.add).then_inc(s_rstd, 1)
                pool.wait_ge(s_rstd, i * 2 + 1)
                pool.tensor_tensor(rstd[:, :], rstd[:, :], eps_pow[:, 0:BATCH], ALU.pow).then_inc(s_rstd, 1)
                pool.wait_ge(s_xn, i * 2 + 2)
                pool.wait_ge(s_hs, i * (2 * E1_LIVE) + 2 * E1_LIVE)
                pool.tensor_tensor(h[:, :, :], xn[:, :, :], sbw[:, 1], ALU.mult).then_inc(s_h, 1)
                pool.wait_ge(s_h, i * 2 + 1)
                pool.tensor_tensor(h[:, :, :], h[:, :, :], sbw[:, 0], ALU.add).then_inc(s_h, 1)

        @block.scalar
        def _(act):
            with act.Fori(0, CHUNKS) as i:
                act.wait_ge(s_xt, i + 1)
                src = bank[0][:, 0:BATCH * P].rearrange("p (b n) -> p b n", b=BATCH)
                act.activation(hT[:, :, :], src, ACT.Copy).then_inc(s_ht, 1)
                act.activation(xT_bc[:, :, bass.ds(i, 1), :], src[:, :, None, :], ACT.Copy).then_inc(s_keep, 1)
                act.wait_ge(s_neg, i * 2 + 2)
                for b in range(BATCH):
                    act.activation(prob[:, b, 0:E1_LIVE], bank[1][:, b * E1_LIVE:(b + 1) * E1_LIVE], ACT.Exp,
                                   bias=neg[:, b:b + 1]).then_inc(s_prob, 1)
                for b in range(BATCH):
                    act.wait_ge(s_hst, i * 2 + (b + 1))
                    act.activation(xsT_bc[:, :, b, bass.ds(i, 1), :],
                                   bank[2 + b][:, :].rearrange("p (e n) -> p e n", e=E1_LIVE)[:, :, None, :],
                                   ACT.Copy).then_inc(s_hsc, 1)

        @block.vector
        def _(dve):
            dve.memset(prob[:, :, :], -1.0).then_inc(s_pad, 1)
            dve.wait_ge(s_pad, 1)
            dve.sem_inc(s_hs, 2 * E1_LIVE)
            with dve.Fori(0, CHUNKS) as i:
                for b in range(BATCH):
                    dve.bn_stats(st[:, b, :], x_bc[:, b, bass.ds(i, 1), :]).then_inc(s_st, 1)
                dve.wait_ge(s_st, i * 2 + 2)
                dve.nop(nofuse=True)
                for b in range(BATCH):
                    dve.bn_aggr(mv[:, b, :], st[:, b, :]).then_inc(s_mv, 1)
                dve.wait_ge(s_rstd, i * 2 + 2)
                for b in range(BATCH):
                    dve.tensor_scalar(xn[:, b, :], x_bc[:, b, bass.ds(i, 1), :], mv[:, b, 0:1], rstd[:, b:b + 1],
                                      ALU.subtract, ALU.mult).then_inc(s_xn, 1)
                dve.wait_ge(s_logit, i + 1)
                dve.tensor_reduce(den[:, :], bank[1][:, 0:BATCH * E1_LIVE].rearrange("p (b n) -> p b n", b=BATCH),
                                  AX.X, ALU.max).then_inc(s_neg, 1)
                dve.wait_ge(s_neg, i * 2 + 1)
                dve.tensor_scalar(neg[:, :], den[:, :], -1.0, None, ALU.mult).then_inc(s_neg, 1)
                dve.wait_ge(s_prob, i * 2 + 2)
                dve.nop(nofuse=True)
                for b in range(BATCH):
                    dve.max(mx[:, b, :], prob[:, b, :]).then_inc(s_mx, 1)
                dve.wait_ge(s_mx, i * 2 + 2)
                dve.nop(nofuse=True)
                for b in range(BATCH):
                    dve.max_index(idx[:, b, :], mx[:, b, :], prob[:, b, :]).then_inc(s_idx, 1)
                dve.wait_ge(s_idx, i * 2 + 2)
                dve.tensor_copy(idf[:, :, :], idx[:, :, 0:2]).then_inc(s_cw, 1)
                dve.tensor_tensor(den[:, :], mx[:, :, 0], mx[:, :, 1], ALU.add).then_inc(s_cw, 1)
                dve.wait_ge(s_cw, i * 9 + 2)
                dve.reciprocal(den[:, :], den[:, :]).then_inc(s_cw, 1)
                for b in range(BATCH):
                    for k in range(2):
                        dve.tensor_scalar(cw[:, k, b, :], cst("iota16")[:, 0:E1_LIVE], idf[:, b, k:k + 1],
                                          mx[:, b, k:k + 1], ALU.is_equal, ALU.mult).then_inc(s_cw, 1)
                dve.wait_ge(s_cw, i * 9 + 7)
                dve.tensor_tensor(cw[:, 0], cw[:, 0], cw[:, 1], ALU.add).then_inc(s_cw, 1)
                dve.wait_ge(s_cw, i * 9 + 8)
                dve.tensor_tensor(cw[:, 0], cw[:, 0], den[:, :, None].to_broadcast([P, BATCH, E1_LIVE]),
                                  ALU.mult).then_inc(s_cw, 1)
                dve.wait_ge(s_cw, i * 9 + 9)
                for b in range(BATCH):
                    for e in range(E1_LIVE):
                        dve.tensor_scalar(hs[:, b, e, :], h[:, b, :], cw[:, 0, b, e:e + 1], None,
                                          ALU.mult).then_inc(s_hs, 1)

        @block.tensor
        def _(pe):
            pe.wait_ge(s_gate, 16)
            pe.sem_inc(s_keep, 1)
            pe.sem_inc(s_hsc, 2)
            with pe.Fori(0, CHUNKS) as i:
                pe.wait_ge(s_h, i * 2 + 2)
                pe.wait_ge(s_keep, i + 1)
                for b in range(BATCH):
                    last = pe.transpose(bank[0][:, b * P:(b + 1) * P], h[:, b, :], cst("ident"))
                last.then_inc(s_xt, 1)
                pe.wait_ge(s_ht, i + 1)
                for b in range(BATCH):
                    last = pe.matmul(bank[1][:, b * E1_LIVE:(b + 1) * E1_LIVE], hT[:, b, :], gate[:, :], start=True,
                                     stop=True)
                last.then_inc(s_logit, 1)
                for b in range(BATCH):
                    pe.wait_ge(s_hs, i * (2 * E1_LIVE) + (b + 3) * E1_LIVE)
                    pe.wait_ge(s_hsc, i * 2 + (b + 1))
                    for e in range(E1_LIVE):
                        last = pe.transpose(bank[2 + b][:, e * P:(e + 1) * P], hs[:, b, e, :], cst("ident"))
                    last.then_inc(s_hst, 1)


def swiglu_phase(nc, x_sb, mod_row, bank, pair, cst, xT_all, xsT_all, W, s_weights, out):
    with ExitStack() as ctx:
        def sb(name, shape, dt=F32):
            return ctx.enter_context(nc.sbuf_tensor(name, shape, dt))

        def sem(name):
            return nc.alloc_semaphore(name)

        N = 512
        TPG = N // P
        sa = [sb(f"f_sa{k}", [P, N]) for k in range(2)]
        hh = [sb(f"f_h{k}", [P, N]) for k in range(2)]
        oT = [sb(f"f_oT{b}", [P, N]) for b in range(BATCH)]
        gated = [sb(f"f_gated{b}", [P, TPG, C]) for b in range(BATCH)]
        xg = [sb(f"f_xg{b}", [P, 1 + E1_LIVE, N]) for b in range(BATCH)]
        up_a = [bank[0], bank[1]]
        up_b = [bank[2], bank[3]]
        acc = [bank[4], bank[5]]
        back = [pair[:, 0:512], pair[:, 512:1024]]
        units = []
        for e in range(0, E1_LIVE, 2):
            units += [(e, f) for f in range(FULL1)] + [(e + 1, f) for f in range(FULL1)] + [(e, None)]
        U = len(units)
        assert U % 2 == 0
        s_a, s_b, s_sa, s_hh = sem("f_s_a"), sem("f_s_b"), sem("f_s_sa"), sem("f_s_hh")
        s_down, s_acc, s_accc, s_back = sem("f_s_down"), sem("f_s_acc"), sem("f_s_accc"), sem("f_s_back")
        s_gated, s_x, s_out = sem("f_s_gated"), sem("f_s_x"), sem("f_s_out")
        s_xg = sem("f_s_xg")
        block = ctx.enter_context(nc.Block())

        def unit(i, b, n):
            return i * (BATCH * U) + (b * U + n)

        @block.tensor
        def _(pe):
            pe.wait_ge(s_weights, 16 * (2 + 2 * E1_LIVE))
            pe.sem_inc(s_sa, 2)
            pe.sem_inc(s_hh, 2)
            pe.sem_inc(s_accc, 2)
            pe.sem_inc(s_gated, 2)
            with pe.Fori(0, TILES // TPG // BATCH) as i:
                for b in range(BATCH):
                    pe.wait_ge(s_xg, i * (2 * BATCH) + 2 * (b + 1))

                    def up(dst, w, src, e, f):
                        if f is not None:
                            return pe.matmul(dst[:, :], w[:, e, f * P:(f + 1) * P], src(e), start=True, stop=True)
                        for k in range(2):
                            last = pe.matmul(dst[k * TAIL1:(k + 1) * TAIL1, :], w[:, e + k, FULL1 * P:F1], src(e + k),
                                             start=True, stop=True, tile_position=(0, k * TAIL1))
                        return last

                    def down(n):
                        e, f = units[n]
                        w = W["w2"][:, e, f, :] if f is not None else W["w2_tail"][:, e // 2, :]
                        pe.wait_ge(s_hh, unit(i, b, n + 3))
                        mm = pe.matmul(acc[b][:, :], w, hh[n % 2][:, :], start=(n == 0), stop=(n == U - 1))
                        mm.then_inc(s_down, 1)
                        return mm

                    for n, (e, f) in enumerate(units):
                        pe.wait_ge(s_sa, unit(i, b, n + 1))
                        up(up_a[n % 2], W["w1"], lambda e: xg[b][:, 0, :], e, f).then_inc(s_a, 1)
                        pe.wait_ge(s_hh, unit(i, b, n + 1))
                        up(up_b[n % 2], W["w3"], lambda e: xg[b][:, 1 + e, :], e, f).then_inc(s_b, 1)
                        if n == 0:
                            pe.wait_ge(s_accc, i * BATCH + (b + 1))
                        else:
                            down(n - 1)
                    down(U - 1)
                    pe.wait_ge(s_accc, i * BATCH + (b + 3))
                    pe.wait_ge(s_gated, i * BATCH + (b + 1))
                    for k in range(TPG):
                        last = pe.transpose(back[b][:, k * P:(k + 1) * P], oT[b][:, k * P:(k + 1) * P], cst("ident"))
                    last.then_inc(s_back, 1)

        @block.scalar
        def _(act):
            act.sem_inc(s_down, 2)
            with act.Fori(0, TILES // TPG // BATCH) as i:
                for b in range(BATCH):
                    for n in range(U):
                        act.wait_ge(s_a, unit(i, b, n + 1))
                        act.wait_ge(s_hh, unit(i, b, n + 1))
                        act.activation(sa[n % 2][:, :], up_a[n % 2][:, :], ACT.Silu).then_inc(s_sa, 1)
                    act.wait_ge(s_down, unit(i, b, U + 2))
                    act.activation(oT[b][:, :], acc[b][:, :], ACT.Copy).then_inc(s_accc, 1)

        @block.vector
        def _(dve):
            with dve.Fori(0, TILES // TPG // BATCH) as i:
                for b in range(BATCH):
                    for n in range(U):
                        dve.wait_ge(s_sa, unit(i, b, n + 3))
                        dve.wait_ge(s_b, unit(i, b, n + 1))
                        dve.wait_ge(s_down, unit(i, b, n + 1))
                        dve.tensor_tensor(hh[n % 2][:, :], sa[n % 2][:, :], up_b[n % 2][:, :], ALU.mult)\
                            .then_inc(s_hh, 1)
                    dve.wait_ge(s_back, i * BATCH + (b + 1))
                    dve.wait_ge(s_x, i * BATCH + (b + 1))
                    dve.tensor_tensor(gated[b][:, :, :], back[b].rearrange("p (k n) -> p k n", k=TPG),
                                      mod_row[:, 1, 1, b, None, :].to_broadcast([P, TPG, C]), ALU.mult)\
                        .then_inc(s_gated, 1)

        @block.gpsimd
        def _(pool):
            def fetch(b, at):
                pool.tensor_copy(xg[b][:, 0, :].rearrange("p (k n) -> p k n", k=TPG),
                                 xT_all[:, bass.ds(at, TPG), :]).then_inc(s_xg, 1)
                pool.tensor_copy(xg[b][:, 1:, :].rearrange("p e (k n) -> p e k n", k=TPG),
                                 xsT_all[:, :, bass.ds(at, TPG), :]).then_inc(s_xg, 1)

            pool.sem_inc(s_x, 2)
            for b in range(BATCH):
                fetch(b, b * CHUNKS)

            def add(i, b):
                pool.wait_ge(s_gated, i * BATCH + (b + 3))
                xs = x_sb[:, bass.ds(i * TPG + b * CHUNKS, TPG), :]
                pool.tensor_tensor(xs, xs, gated[b][:, :, :], ALU.add).then_inc(s_x, 1)

            last = TILES // TPG // BATCH - 1
            with pool.Fori(0, last) as i:
                for b in range(BATCH):
                    add(i, b)
                    fetch(b, (i + 1) * TPG + b * CHUNKS)
            for b in range(BATCH):
                add(last, b)

        @block.sync
        def _(sp):
            with sp.Fori(0, TILES // TPG // BATCH) as i:
                for b in range(BATCH):
                    sp.wait_ge(s_x, i * BATCH + (b + 3))
                    sp.dma_start(out[b].rearrange("(c p) n -> p c n", p=P)[:, bass.ds(i * TPG, TPG), :],
                                 x_sb[:, bass.ds(i * TPG + b * CHUNKS, TPG), :]).then_inc(s_out, 16)
            sp.wait_ge(s_out, 16 * TILES // TPG)


def kernel(**inputs):
    import concourse.bacc as _bacc
    from concourse.bass_utils import run_bass_kernel_spmd as _run

    a = {k: np.asarray(v) for k, v in inputs.items()}
    A = {n: a["L0_attn_" + n] for n in ("miu_x", "lambda_", "A_lora", "B_lora", "td_miu", "td_A", "td_B", "u",
                                        "Wr", "Wk", "Wv", "Wg", "Wo", "gn_gamma", "gn_beta")}
    b_rows = np.zeros((MIXES, P, C), np.float32)
    for f in range(4):
        b_rows[f, f * LORA:(f + 1) * LORA] = A["B_lora"][f]
    b_rows[4, 0:LORA] = A["B_lora"][4]
    host = {
        "const": shape_constants()[1],
        "L0_attn_x": a["L0_attn_x"],
        "c_cols": np.stack([a["L0_c"].T, a["L1_c"].T], axis=1),
        "wmod": np.stack([a["L0_wmod"], a["L1_wmod"]]),
        "miu_col": A["miu_x"].reshape(C, 1),
        "lambda_cols": A["lambda_"].reshape(MIXES, C).T,
        "td_miu_col": A["td_miu"].reshape(C, 1),
        "u_col": A["u"].reshape(C, 1),
        "gn_gamma_col": A["gn_gamma"].reshape(C, 1),
        "gn_beta_col": A["gn_beta"].reshape(C, 1),
        "L0_attn_A_lora": A["A_lora"],
        "b_lora_rows": b_rows,
        "L0_attn_td_A": A["td_A"],
        "L0_attn_td_B": A["td_B"],
        "rwkv_wT": np.stack([A[n].T for n in ("Wk", "Wv", "Wr", "Wg", "Wo")]),
    }
    w1, b1, w2 = a["L0_ffn_w1"], a["L0_ffn_b1"], a["L0_ffn_w2"]
    host["experts0"] = np.concatenate([w1, w2.reshape(E0, 2, P, C).transpose(0, 2, 1, 3).reshape(E0, P, 2 * C),
                                       b1.reshape(E0, 2, P).transpose(0, 2, 1)], axis=2)
    host["L0_ffn_b2"] = a["L0_ffn_b2"]
    host["L0_ffn_router_w"] = a["L0_ffn_router_w"]
    for n in ("Wq", "Wk", "Wv", "Wo"):
        host["L1_attn_" + n] = a["L1_attn_" + n]
    host["gate_cols"] = a["L1_ffn_gate_w"][:E1_LIVE].T
    for n in ("w1", "w3", "w2"):
        host["moe_" + n] = a["L1_ffn_" + n][:E1_LIVE]
    nc = _bacc.Bacc("TRN2", target_bir_lowering=False, num_devices=1)
    arrays, t = {}, {}
    for name, v in host.items():
        v = np.ascontiguousarray(v)
        arrays[f"in_{name}_dram"] = v
        t[name] = nc.dram_tensor(f"in_{name}_dram", v.shape, mybir.dt.from_np(v.dtype), kind="ExternalInput").ap()
    for name in ("slots_in", "slots_out"):
        t[name] = nc.dram_tensor(name, (SLOTS, C), F32, kind="Internal").ap()
    out = nc.dram_tensor("out_0_dram", (BATCH, SEQ, C), F32, kind="ExternalOutput").ap()
    bass_adaln_stack(nc, t, out)
    r = _run(nc, [arrays], core_ids=[0])
    return r.results[0]["out_0_dram"]
```

```python
from contextlib import ExitStack

import numpy as np

import concourse.bass as bass
from concourse import mybir

F32 = mybir.dt.float32
I32 = mybir.dt.int32
U32 = mybir.dt.uint32
ALU = mybir.AluOpType
ACT = mybir.ActivationFunctionType
AX = mybir.AxisListType

P = 128
BATCH, SEQ, C = 2, 1024, 128
CHUNKS = SEQ // P
TILES = BATCH * CHUNKS
LN_EPS = 1e-5

RW_HEADS, RW_DIM = 2, 64
LORA = 32
MIXES = 5
TD_RANK = 64
LEAF = 32
GN_EPS = 1e-5 * RW_HEADS
LEVELS = 7

E0, F0 = 16, 256
SLOT_TILES = 32
SLOTS = SLOT_TILES * P
W0 = 2 * F0 + 3

HL_HEADS, HL_DIM = 16, 32
GROUPS = HL_HEADS * HL_DIM // P
HPG = P // HL_DIM
GAMMA = 0.99

E1, E1_LIVE, F1 = 8, 4, 704
FULL1 = F1 // P
TAIL1 = F1 - FULL1 * P


def shape_constants():
    i = np.arange(P)
    row, col = i[:, None], i[None, :]
    parts = {}
    parts["ident"] = (row == col)
    parts["before"] = (row < col)
    parts["ones"] = np.ones((P, P))
    parts["head2"] = (row // RW_DIM == col // RW_DIM)
    parts["head4"] = (row // HL_DIM == col // HL_DIM)
    lag = (col - row).astype(np.float64)
    parts["decay_incl"] = np.where(lag >= 0, GAMMA ** np.maximum(lag, 0), 0)
    parts["decay_excl"] = np.where(lag > 0, GAMMA ** np.maximum(lag, 0), 0)
    parts["decay_row"] = np.broadcast_to(GAMMA ** (col + 1.0), (P, P))
    parts["decay_col"] = GAMMA ** (P - 1.0 - row)
    s, t = row % LEAF, np.arange(LEAF)[None, :]
    leaf = [(s // 2 == t // 2) & (s <= t)]
    for m in (2, 4, 8, 16):
        leaf.append((s // (2 * m) == t // (2 * m)) & (s % (2 * m) < m) & (t % (2 * m) >= m))
    parts["leaf"] = np.concatenate(leaf, axis=1)
    parts["iota16"] = np.broadcast_to(np.arange(E0), (P, E0))
    parts["iota32"] = np.broadcast_to(np.arange(SLOT_TILES), (P, SLOT_TILES))
    parts["restart"] = np.broadcast_to(np.arange(E0 * TILES) % TILES != 0, (P, E0 * TILES))
    at, cols = {}, 0
    for name, a in parts.items():
        at[name] = (cols, cols + a.shape[1])
        cols += a.shape[1]
    return at, np.concatenate([np.asarray(a, np.float32) for a in parts.values()], axis=1)


CONST_AT, _ = shape_constants()
CONST_COLS = max(b for _, b in CONST_AT.values())


def bass_adaln_stack(nc, t, out):
    ctx = ExitStack()
    with ctx:
        def sb(name, shape, dt=F32):
            return ctx.enter_context(nc.sbuf_tensor(name, shape, dt))

        def sem(name):
            return ctx.enter_context(nc.semaphore(name))

        const = sb("const", [P, CONST_COLS])

        def cst(name):
            a, b = CONST_AT[name]
            return const[:, a:b]

        x_sb = sb("x_sb", [P, TILES, C])
        x_bc = x_sb[:, :, :].rearrange("p (b c) n -> p b c n", b=BATCH)
        eps_pow = sb("eps_pow", [P, 16])
        mod_col = sb("mod_col", [P, 2, 4, BATCH])
        mod_row = sb("mod_row", [P, 2, 2, BATCH, C])
        sbw = sb("sbw", [P, 2, 2, BATCH, C])

        bank = [ctx.enter_context(nc.psum_tensor(f"bank{i}", [P, 512], F32)) for i in range(4)]
        bank.append(None)
        pair = ctx.enter_context(nc.psum_tensor("pair", [P, 1024], F32))
        bank[4] = ctx.enter_context(nc.psum_tensor("bank6", [P, 512], F32))
        bank.append(ctx.enter_context(nc.psum_tensor("bank7", [P, 512], F32)))

        W1 = {n: sb(f"hla_w{n}", [P, HL_HEADS * HL_DIM]) for n in "qkv"}
        W1["o"] = sb("hla_wo", [P, GROUPS, C])
        s_w1 = sem("s_w1")
        W2 = {"w1": sb("moe_w1", [P, E1_LIVE, F1]), "w3": sb("moe_w3", [P, E1_LIVE, F1]),
              "w2": sb("moe_w2", [P, E1_LIVE, FULL1, C]), "w2_tail": sb("moe_w2_tail", [P, E1_LIVE // 2, C])}
        s_w2 = sem("s_w2")
        with nc.cleanup_on_exit():
            setup_phase(nc, t, const, x_sb, eps_pow, mod_col, mod_row, sbw, bank, cst, W1, s_w1, W2, s_w2)
        with nc.cleanup_on_exit():
            rwkv_phase(nc, t, x_bc, eps_pow, mod_col, mod_row, bank, pair, cst)
        mv_next = sb("mv_next", [P, TILES, 2])
        halves = [pair[:, 0:512], pair[:, 512:1024]]
        with nc.cleanup_on_exit():
            expert_phase(nc, t, x_sb, eps_pow, sbw[:, 0], mod_row, bank + halves, cst, mv_next)
        with nc.sbuf_tensor("hT_all", [P, TILES, P], F32) as hT_all:
            with nc.cleanup_on_exit():
                norm_transpose_phase(nc, x_sb, eps_pow, mod_col, bank, cst, mv_next, hT_all)
            with nc.cleanup_on_exit():
                hla_phase(nc, x_bc, mod_row, bank, pair, cst, hT_all, W1, s_w1)
        with nc.cleanup_on_exit():
            swiglu_phase(nc, t, x_sb, eps_pow, sbw[:, 1], mod_row, bank, pair, cst, W2, s_w2, out)


def setup_phase(nc, t, const, x_sb, eps_pow, mod_col, mod_row, sbw, bank, cst, W1, s_w1, W2, s_w2):
    with ExitStack() as ctx:
        def sb(name, shape, dt=F32):
            return ctx.enter_context(nc.sbuf_tensor(name, shape, dt))

        def sem(name):
            return nc.alloc_semaphore(name)

        cT = sb("cT", [P, 2, BATCH])
        eT = sb("eT", [P, 2, BATCH])
        silu_c = sb("silu_c", [P, 2, BATCH])
        wmod = sb("wmod", [P, 2, 6 * C])
        absr = sb("absr", [P, 2, 2, BATCH, C])
        sgn = sb("sgn", [P, 2, 2, BATCH, C])
        s_const = sem("s_const")
        s_x = sem("s_x")
        s_c = sem("s_c")
        s_wmod = sem("s_wmod")
        s_exp = sem("s_exp")
        s_silu = sem("s_silu")
        s_cols = sem("s_cols")
        s_rows = sem("s_rows")
        s_colv = sem("s_colv")
        s_clamp = sem("s_clamp")
        s_set = sem("s_set")
        block = ctx.enter_context(nc.Block())

        @block.sync
        def _(sp):
            sp.dma_start(cT[:, :, :], t["c_cols"]).then_inc(s_c, 16)
            sp.dma_start(wmod[:, :, :], t["wmod"].rearrange("l k n -> k l n")).then_inc(s_wmod, 16)
            sp.dma_start(const[:, :], t["const"]).then_inc(s_const, 16)
            for b in range(BATCH):
                sp.dma_start(x_sb[:, b * CHUNKS:(b + 1) * CHUNKS, :],
                             t["L0_attn_x"][b].rearrange("(c p) n -> p c n", p=P)).then_inc(s_x, 16)
            for n in "qkv":
                sp.dma_start(W1[n][:, :], t["L1_attn_W" + n]).then_inc(s_w1, 16)
            sp.dma_start(W1["o"][:, :, :], t["L1_attn_Wo"].rearrange("(j p) n -> p j n", p=P)).then_inc(s_w1, 16)
            for n in ("w1", "w3"):
                sp.dma_start(W2[n][:, :, :], t["moe_" + n].rearrange("e k n -> k e n")).then_inc(s_w2, 16)
            for e in range(E1_LIVE):
                sp.dma_start(W2["w2"][:, e, :, :], t["moe_w2"][e, 0:FULL1 * P, :].rearrange("(f p) n -> p f n", p=P))\
                    .then_inc(s_w2, 16)
                rows = slice((e % 2) * TAIL1, (e % 2 + 1) * TAIL1)
                sp.dma_start(W2["w2_tail"][rows, e // 2, :], t["moe_w2"][e, FULL1 * P:F1, :]).then_inc(s_w2, 16)
            sp.wait_ge(s_const, 16)
            sp.wait_ge(s_x, 32)

        @block.gpsimd
        def _(pool):
            pool.memset(eps_pow[:, :], -0.5).then_inc(s_set, 1)
            pool.wait_ge(s_set, 1)

        @block.scalar
        def _(act):
            act.wait_ge(s_c, 16)
            act.activation(eT[:, :, :], cT[:, :, :], ACT.Exp, scale=-1.0).then_inc(s_exp, 1)

        @block.vector
        def _(dve):
            dve.wait_ge(s_exp, 1)
            dve.tensor_scalar(eT[:, :, :], eT[:, :, :], 1.0, None, ALU.add).then_inc(s_silu, 1)
            dve.wait_ge(s_silu, 1)
            dve.reciprocal(eT[:, :, :], eT[:, :, :]).then_inc(s_silu, 1)
            dve.wait_ge(s_silu, 2)
            dve.tensor_tensor(silu_c[:, :, :], eT[:, :, :], cT[:, :, :], ALU.mult).then_inc(s_silu, 1)
            dve.wait_ge(s_cols, 1)
            for n, plus in enumerate((0.0, 1.0, 0.0, 1.0)):
                dve.tensor_scalar(mod_col[:, :, n, :],
                                  bank[0][:, 0:16].rearrange("p (l n b) -> p l n b", l=2, n=4)[:, :, n, :],
                                  plus, None, ALU.add).then_inc(s_colv, 1)
            dve.wait_ge(s_rows, 1)
            for layer in range(2):
                rows = bank[1 + layer][:, :].rearrange("p (g b n) -> p g b n", g=2, b=BATCH)
                flat_rows = bank[1 + layer][:, :]
                neg = absr[:, layer].rearrange("p g b n -> p (g b n)")
                dve.tensor_scalar(neg, flat_rows, -1.0, None, ALU.mult).then_inc(s_clamp, 1)
                dve.tensor_scalar(sgn[:, layer], rows, 0.0, 2.0, ALU.is_ge, ALU.mult).then_inc(s_clamp, 1)
                dve.wait_ge(s_clamp, 3 * layer + 1)
                dve.scalar_tensor_tensor(out=neg, in0=neg, scalar=0.25, in1=flat_rows, op0=ALU.max,
                                         op1=ALU.max).then_inc(s_clamp, 1)
            dve.wait_ge(s_clamp, 6)
            dve.scalar_tensor_tensor(out=mod_row[:, :, :, :, :].rearrange("p l g b n -> p (l g b n)"),
                                     in0=sgn[:, :, :, :, :].rearrange("p l g b n -> p (l g b n)"), scalar=-1.0,
                                     in1=absr[:, :, :, :, :].rearrange("p l g b n -> p (l g b n)"),
                                     op0=ALU.add, op1=ALU.mult).then_inc(s_clamp, 1)
            for layer in range(2):
                srows = bank[3 + layer][:, :].rearrange("p (k b n) -> p k b n", k=2, b=BATCH)
                dve.tensor_scalar(sbw[:, layer, 0], srows[:, 0], 0.0, None, ALU.add).then_inc(s_clamp, 1)
                dve.tensor_scalar(sbw[:, layer, 1], srows[:, 1], 1.0, None, ALU.add).then_inc(s_clamp, 1)
            dve.wait_ge(s_clamp, 11)
            dve.wait_ge(s_colv, 4)

        @block.tensor
        def _(pe):
            pe.wait_ge(s_silu, 3)
            pe.wait_ge(s_wmod, 16)
            for layer in range(2):
                for n, part in enumerate((0, 1, 3, 4)):
                    at = (layer * 4 + n) * 2
                    last = pe.matmul(bank[0][:, at:at + 2], wmod[:, layer, part * C:(part + 1) * C],
                                     silu_c[:, layer, :], start=True, stop=True)
            last.then_inc(s_cols, 1)
            for layer in range(2):
                for g, part in enumerate((2, 5)):
                    for b in range(BATCH):
                        at = (g * 2 + b) * C
                        pe.matmul(bank[1 + layer][:, at:at + C], silu_c[:, layer, b:b + 1].to_broadcast([P, P]),
                                  wmod[:, layer, part * C:(part + 1) * C], start=True, stop=True)
                for k, part in enumerate((3, 4)):
                    for b in range(BATCH):
                        at = (k * 2 + b) * C
                        last = pe.matmul(bank[3 + layer][:, at:at + C], silu_c[:, layer, b:b + 1].to_broadcast([P, P]),
                                         wmod[:, layer, part * C:(part + 1) * C], start=True, stop=True)
            last.then_inc(s_rows, 1)


def rwkv_phase(nc, t, x_bc, eps_pow, mod_col, mod_row, bank, pair, cst):
    with ExitStack() as ctx:
        def sb(name, shape, dt=F32):
            return ctx.enter_context(nc.sbuf_tensor(name, shape, dt))

        def sem(name):
            return nc.alloc_semaphore(name)

        N = BATCH * P
        lamb = sb("lamb", [P, MIXES])
        miu = sb("miu", [P, 1])
        td_miu = sb("td_miu", [P, 1])
        bonus = sb("bonus", [P, 1])
        gamma = sb("gamma", [P, 1])
        beta = sb("beta", [P, 1])
        a_lora = sb("a_lora", [P, MIXES * LORA])
        b_pad = sb("b_pad", [P, MIXES, C])
        td_a = sb("td_a", [P, TD_RANK])
        td_b = sb("td_b", [TD_RANK, C])
        wT = sb("wT", [P, 5, C])
        stats = sb("stats", [P, TILES, 6])
        mv = sb("mv", [P, TILES, 2])
        rstd = sb("rstd", [P, TILES])
        xn = sb("xn", [P, BATCH, C])
        hT = sb("hT", [P, BATCH, P + 1])
        dxa = sb("dxa", [P, BATCH, P])
        xm = sb("xm", [P, BATCH, P])
        lh = sb("lh", [P, N])
        lh4 = sb("lh4", [LORA, N])
        xx = sb("xx", [P, MIXES, BATCH, P])
        tw = sb("tw", [TD_RANK, N])
        ew = sb("ew", [P, N])
        rl = [sb(f"rl{m}", [P, N]) for m in range(LEVELS + 1)]
        kl = [sb(f"kl{m}", [P, N]) for m in range(LEVELS + 1)]
        tot = [sb(f"tot{m}", [P, N >> m]) for m in range(LEVELS + 1)]
        rd = sb("rd", [P, N])
        kd = sb("kd", [P, N])
        v_sb = sb("v_sb", [P, BATCH, C])
        eg = sb("eg", [P, N])
        gT = sb("gT", [P, N])
        prod = sb("prod", [P, 4, 160])
        leafs = sb("leafs", [P, 4, LEAF])
        att = sb("att", [P, 4, P])
        ktm = sb("ktm", [P, BATCH, P])
        state = sb("state", [P, BATCH, P])
        kv = sb("kv", [P, BATCH, P])
        gst = sb("gst", [P, 4, 6])
        gmv = sb("gmv", [P, 4, 2])
        grs = sb("grs", [P, 4])
        yn = sb("yn", [P, BATCH, C])
        zT = sb("zT", [P, BATCH, P])
        gated = sb("gated", [P, BATCH, C])

        s_w = sem("s_w")
        s_zero = sem("s_zero")
        s_stat = sem("s_stat")
        s_var = sem("s_var")
        s_rstd = sem("s_rstd")
        s_xn = sem("s_xn")
        s_xt = sem("s_xt")
        s_ht = sem("s_ht")
        s_dxa = sem("s_dxa")
        s_xm = sem("s_xm")
        s_lora = sem("s_lora")
        s_lh = sem("s_lh")
        s_mix = sem("s_mix")
        s_scaled = sem("s_scaled")
        s_xx = sem("s_xx")
        s_proj = sem("s_proj")
        s_td = sem("s_td")
        s_tw = sem("s_tw")
        s_ew = sem("s_ew")
        s_evac = sem("s_evac")
        s_diag = sem("s_diag")
        s_r = sem("s_r")
        s_k = sem("s_k")
        s_tot = sem("s_tot")
        s_rc = sem("s_rc")
        s_leafmm = sem("s_leafmm")
        s_prod = sem("s_prod")
        s_leaf = sem("s_leaf")
        s_att = sem("s_att")
        s_off = sem("s_off")
        s_ktT = sem("s_ktT")
        s_ktm = sem("s_ktm")
        s_y = sem("s_y")
        s_kv = sem("s_kv")
        s_state = sem("s_state")
        s_gn = sem("s_gn")
        s_grs = sem("s_grs")
        s_yn = sem("s_yn")
        s_zt = sem("s_zt")
        s_z = sem("s_z")
        s_zg = sem("s_zg")
        s_o = sem("s_o")
        s_gate = sem("s_gate")
        s_gated = sem("s_gated")
        s_gT = sem("s_gT")
        s_iter = sem("s_iter")
        block = ctx.enter_context(nc.Block())
        flat = "p b n -> p (b n)"
        lv = [mm for mm in range(LEVELS)]

        def halves(a, m):
            return a[:, :].rearrange("p (k h e) -> p k h e", h=2, e=1 << m)

        def per(a, m):
            return a[:, :].rearrange("p (k h) -> p k h", h=2)

        @block.sync
        def _(sp):
            sp.dma_start(lamb[:, :], t["lambda_cols"]).then_inc(s_w, 16)
            sp.dma_start(miu[:, :], t["miu_col"]).then_inc(s_w, 16)
            sp.dma_start(td_miu[:, :], t["td_miu_col"]).then_inc(s_w, 16)
            sp.dma_start(bonus[:, :], t["u_col"]).then_inc(s_w, 16)
            sp.dma_start(gamma[:, :], t["gn_gamma_col"]).then_inc(s_w, 16)
            sp.dma_start(beta[:, :], t["gn_beta_col"]).then_inc(s_w, 16)
            sp.dma_start(a_lora[:, :], t["L0_attn_A_lora"]).then_inc(s_w, 16)
            sp.dma_start(b_pad[:, :, :], t["b_lora_rows"].rearrange("f k n -> k f n")).then_inc(s_w, 16)
            sp.dma_start(td_a[:, :], t["L0_attn_td_A"]).then_inc(s_w, 16)
            sp.dma_start(td_b[:, :], t["L0_attn_td_B"]).then_inc(s_w, 16)
            sp.dma_start(wT[:, :, :], t["rwkv_wT"].rearrange("w k n -> k w n")).then_inc(s_w, 16)
        LOADS = 16 * 11

        def iteration_free(eng, i):
            eng.wait_ge(s_iter, i * 2 + 2)

        @block.vector
        def _(dve):
            dve.wait_ge(s_w, LOADS)
            dve.memset(state[:, :, :], 0.0).then_inc(s_zero, 1)
            dve.memset(att[:, :, :], 0.0).then_inc(s_zero, 1)
            dve.memset(hT[:, :, P:P + 1], 0.0).then_inc(s_zero, 1)
            for c in range(TILES):
                dve.bn_stats(stats[:, c, :], x_bc[:, c // CHUNKS, c % CHUNKS, :]).then_inc(s_stat, 1)
            dve.wait_ge(s_stat, TILES)
            for c in range(TILES):
                dve.bn_aggr(mv[:, c, :], stats[:, c, :]).then_inc(s_var, 1)
            dve.wait_ge(s_rstd, 2)
            dve.wait_ge(s_zero, 3)
            with dve.Fori(0, CHUNKS) as i:
                iteration_free(dve, i)
                dve.tensor_copy(hT[:, :, 0:1], hT[:, :, P:P + 1]).then_inc(s_xn, 1)
                for b in range(BATCH):
                    dve.tensor_scalar(xn[:, b, :], x_bc[:, b, bass.ds(i, 1), :],
                                      mv[:, bass.ds(i + b * CHUNKS, 1), 0:1], rstd[:, bass.ds(i + b * CHUNKS, 1)],
                                      ALU.subtract, ALU.mult).then_inc(s_xn, 1)
                dve.wait_ge(s_dxa, i + 1)
                dve.scalar_tensor_tensor(out=xm[:, :, :], in0=dxa[:, :, :], scalar=miu[:, 0:1], in1=hT[:, :, 1:],
                                         op0=ALU.mult, op1=ALU.add).then_inc(s_xm, 1)
                for f in range(MIXES):
                    if f % 2 == 0:
                        dve.wait_ge(s_mix, i * 3 + (f // 2 + 1))
                    src = bank[(2, 3, 4)[f // 2]][:, f % 2 * N:(f % 2 + 1) * N].rearrange("p (b n) -> p b n", b=BATCH)
                    dve.scalar_tensor_tensor(out=xx[:, f], in0=src, scalar=lamb[:, f:f + 1], in1=dxa[:, :, :],
                                             op0=ALU.add, op1=ALU.mult).then_inc(s_scaled, 1)
                dve.wait_ge(s_evac, i * 3 + 3)
                rh, kh = halves(rl[0], 0), halves(kl[0], 0)
                dve.tensor_scalar(halves(rd, 0)[:, :, 0], rh[:, :, 0], bonus[:, 0:1], None, ALU.mult).then_inc(s_diag, 1)
                dve.tensor_copy(halves(rd, 0)[:, :, 1], rh[:, :, 1]).then_inc(s_diag, 1)
                dve.tensor_copy(halves(kd, 0)[:, :, 0], kh[:, :, 0]).then_inc(s_diag, 1)
                dve.tensor_scalar(halves(kd, 0)[:, :, 1], kh[:, :, 1], bonus[:, 0:1], None, ALU.mult).then_inc(s_diag, 1)
                dve.wait_ge(s_ew, i * 2 + 2)
                for m in lv:
                    if m:
                        dve.wait_ge(s_tot, i * LEVELS + m)
                        dve.wait_ge(s_r, i * LEVELS + m)
                        dve.wait_ge(s_rc, i * 2 * LEVELS + 2 * m)
                    tp = per(tot[m], m)
                    dve.tensor_tensor(tot[m + 1][:, :], tp[:, :, 0], tp[:, :, 1], ALU.mult).then_inc(s_tot, 1)
                    dve.tensor_tensor(halves(rl[m + 1], m)[:, :, 1], halves(rl[m], m)[:, :, 1],
                                      tp[:, :, 0:1].to_broadcast([P, N >> (m + 1), 1 << m]), ALU.mult).then_inc(s_r, 1)
                dve.wait_ge(s_gT, i + 1)
                dve.tensor_scalar(eg[:, :], eg[:, :], 1.0, None, ALU.add).then_inc(s_gate, 1)
                dve.wait_ge(s_gate, i * 3 + 1)
                dve.reciprocal(eg[:, :], eg[:, :]).then_inc(s_gate, 1)
                dve.wait_ge(s_gate, i * 3 + 2)
                dve.tensor_tensor(gT[:, :], eg[:, :], bank[4][:, 0:N], ALU.mult).then_inc(s_gate, 1)
                scores = pair[:, :].rearrange("p (u n) -> p u n", u=4)
                dve.wait_ge(s_leafmm, i + 1)
                dve.tensor_tensor(prod[:, :, :], scores[:, :, 0:160],
                                  cst("leaf")[:, None, :].to_broadcast([P, 4, 160]), ALU.mult).then_inc(s_prod, 1)
                dve.wait_ge(s_prod, i + 1)
                dve.tensor_reduce(leafs[:, :, :], prod[:, :, :].rearrange("p u (l n) -> p u n l", n=LEAF), AX.X,
                                  ALU.add).then_inc(s_leaf, 1)
                dve.wait_ge(s_leaf, i + 1)
                for q in range(4):
                    rows = slice(q * LEAF, (q + 1) * LEAF)
                    dve.tensor_copy(att[rows, :, rows], leafs[rows, :, :]).then_inc(s_att, 1)
                dve.wait_ge(s_kv, i + 1)
                dve.tensor_tensor(kv[:, :, :], bank[5][:, N:2 * N].rearrange("p (b n) -> p b n", b=BATCH),
                                  cst("head2")[:, None, :].to_broadcast([P, BATCH, P]), ALU.mult).then_inc(s_state, 1)
                dve.wait_ge(s_state, i * 3 + 1)
                for b in range(BATCH):
                    dve.scalar_tensor_tensor(out=state[:, b, :], in0=state[:, b, :], scalar=tot[LEVELS][:, b:b + 1],
                                             in1=kv[:, b, :], op0=ALU.mult, op1=ALU.add).then_inc(s_state, 1)
                y = bank[5][:, 0:N].rearrange("p (u n) -> p u n", u=4)
                for u in range(4):
                    dve.bn_stats(gst[:, u, :], y[:, u, :]).then_inc(s_gn, 1)
                dve.wait_ge(s_gn, i * 8 + 4)
                dve.nop(nofuse=True)
                for u in range(4):
                    dve.bn_aggr(gmv[:, u, :], gst[:, u, :]).then_inc(s_gn, 1)
                dve.wait_ge(s_grs, i * 2 + 2)
                for u in range(4):
                    dve.tensor_scalar(yn[:, u // 2, (u % 2) * RW_DIM:(u % 2 + 1) * RW_DIM], y[:, u, :], gmv[:, u, 0:1],
                                      grs[:, u:u + 1], ALU.subtract, ALU.mult).then_inc(s_yn, 1)
                dve.wait_ge(s_state, i * 3 + 3)
                dve.sem_inc(s_iter, 1)
                dve.wait_ge(s_o, i + 1)
                dve.tensor_tensor(gated[:, :, :], bank[2][:, 0:N].rearrange("p (b n) -> p b n", b=BATCH),
                                  mod_row[:, 0, 0], ALU.mult).then_inc(s_gated, 1)

        @block.gpsimd
        def _(pool):
            pool.sem_inc(s_iter, 2)
            pool.wait_ge(s_var, TILES)
            pool.tensor_scalar(rstd[:, :], mv[:, :, 1], LN_EPS, None, ALU.add).then_inc(s_rstd, 1)
            pool.wait_ge(s_rstd, 1)
            pool.tensor_tensor(rstd[:, :], rstd[:, :], eps_pow[:, 0:TILES], ALU.pow).then_inc(s_rstd, 1)
            with pool.Fori(0, CHUNKS) as i:
                iteration_free(pool, i)
                pool.wait_ge(s_ht, i * 2 + 2)
                pool.wait_ge(s_xn, i * 3 + 1)
                pool.tensor_tensor(dxa[:, :, :], hT[:, :, 0:P], hT[:, :, 1:], ALU.subtract).then_inc(s_dxa, 1)
                for f in range(MIXES):
                    pool.wait_ge(s_scaled, i * MIXES + (f + 1))
                    pool.tensor_tensor(xx[:, f], xx[:, f], hT[:, :, 1:], ALU.add).then_inc(s_xx, 1)
                pool.wait_ge(s_evac, i * 3 + 3)
                pool.wait_ge(s_ew, i * 2 + 2)
                for m in lv:
                    if m:
                        pool.wait_ge(s_tot, i * LEVELS + m)
                        pool.wait_ge(s_k, i * LEVELS + m)
                        pool.wait_ge(s_rc, i * 2 * LEVELS + 2 * m)
                    pool.tensor_tensor(halves(kl[m + 1], m)[:, :, 0], halves(kl[m], m)[:, :, 0],
                                       per(tot[m], m)[:, :, 1:2].to_broadcast([P, N >> (m + 1), 1 << m]),
                                       ALU.mult).then_inc(s_k, 1)
                pool.wait_ge(s_gn, i * 8 + 8)
                pool.nop(nofuse=True)
                pool.tensor_scalar(grs[:, :], gmv[:, :, 1], GN_EPS, None, ALU.add).then_inc(s_grs, 1)
                pool.wait_ge(s_grs, i * 2 + 1)
                pool.tensor_tensor(grs[:, :], grs[:, :], eps_pow[:, 0:4], ALU.pow).then_inc(s_grs, 1)
                pool.wait_ge(s_z, i + 1)
                pool.wait_ge(s_gate, i * 3 + 3)
                pool.tensor_tensor(zT[:, :, :], zT[:, :, :], gT[:, :].rearrange("p (b n) -> p b n", b=BATCH),
                                   ALU.mult).then_inc(s_zg, 1)
                pool.wait_ge(s_gated, i + 1)
                pool.tensor_tensor(x_bc[:, :, bass.ds(i, 1), :], x_bc[:, :, bass.ds(i, 1), :],
                                   gated[:, :, None, :], ALU.add).then_inc(s_iter, 1)
            pool.wait_ge(s_iter, 2 * CHUNKS + 2)

        @block.scalar
        def _(act):
            act.wait_ge(s_w, LOADS)
            with act.Fori(0, CHUNKS) as i:
                iteration_free(act, i)
                act.wait_ge(s_xt, i + 1)
                act.wait_ge(s_xn, i * 3 + 1)
                for b in range(BATCH):
                    act.activation(hT[:, b, 1:], bank[0][:, b * P:(b + 1) * P], ACT.Identity,
                                   bias=mod_col[:, 0, 0, b:b + 1], scale=mod_col[:, 0, 1, b:b + 1]).then_inc(s_ht, 1)
                act.wait_ge(s_lora, i + 1)
                act.activation(lh[:, :], bank[1][:, 0:N], ACT.Tanh).then_inc(s_lh, 1)
                act.activation(lh4[:, :], bank[1][0:LORA, N:2 * N], ACT.Tanh).then_inc(s_lh, 1)
                act.wait_ge(s_td, i * 2 + 1)
                act.activation(tw[:, :], bank[1][0:TD_RANK, 0:N], ACT.Tanh).then_inc(s_tw, 1)
                act.wait_ge(s_proj, i * 4 + 1)
                act.activation(kl[0][:, :], bank[2][:, 0:N], ACT.Copy).then_inc(s_evac, 1)
                act.wait_ge(s_td, i * 2 + 2)
                act.activation(ew[:, :], bank[1][:, N:2 * N], ACT.Exp, bias=td_miu[:, 0:1]).then_inc(s_ew, 1)
                act.wait_ge(s_ew, i * 2 + 1)
                act.activation(tot[0][:, :], ew[:, :], ACT.Exp, scale=-1.0).then_inc(s_ew, 1)
                act.wait_ge(s_proj, i * 4 + 2)
                act.activation(v_sb[:, :, :], bank[0][:, 0:N].rearrange("p (b n) -> p b n", b=BATCH),
                               ACT.Copy).then_inc(s_evac, 1)
                act.wait_ge(s_proj, i * 4 + 3)
                act.activation(rl[0][:, :], bank[3][:, 0:N], ACT.Copy).then_inc(s_evac, 1)
                act.wait_ge(s_proj, i * 4 + 4)
                act.activation(eg[:, :], bank[4][:, 0:N], ACT.Exp, scale=-1.0).then_inc(s_gT, 1)
                act.wait_ge(s_evac, i * 3 + 3)
                for m in lv:
                    if m:
                        act.wait_ge(s_r, i * LEVELS + m)
                        act.wait_ge(s_k, i * LEVELS + m)
                        act.wait_ge(s_rc, i * 2 * LEVELS + 2 * m)
                    act.activation(halves(rl[m + 1], m)[:, :, 0], halves(rl[m], m)[:, :, 0],
                                   ACT.Copy).then_inc(s_rc, 1)
                    act.activation(halves(kl[m + 1], m)[:, :, 1], halves(kl[m], m)[:, :, 1],
                                   ACT.Copy).then_inc(s_rc, 1)
                scores = pair[:, :].rearrange("p (u n) -> p u n", u=4)
                act.wait_ge(s_leaf, i + 1)
                act.activation(att[0:64, :, 64:128], scores[0:64, :, 160:224], ACT.Copy).then_inc(s_off, 1)
                act.activation(att[0:32, :, 32:64], scores[0:32, :, 224:256], ACT.Copy).then_inc(s_off, 1)
                act.activation(att[64:96, :, 96:128], scores[64:96, :, 224:256], ACT.Copy).then_inc(s_off, 1)
                act.wait_ge(s_ktT, i + 1)
                act.activation(ktm[:, :, :], bank[1][:, 0:N].rearrange("p (b n) -> p b n", b=BATCH),
                               ACT.Copy).then_inc(s_ktm, 1)
                act.wait_ge(s_zt, i + 1)
                act.activation(zT[:, :, :], bank[0][:, 0:N].rearrange("p (b n) -> p b n", b=BATCH), ACT.Identity,
                               bias=beta[:, 0:1], scale=gamma[:, 0:1]).then_inc(s_z, 1)

        @block.tensor
        def _(pe):
            pe.wait_ge(s_w, LOADS)
            with pe.Fori(0, CHUNKS) as i:
                iteration_free(pe, i)
                pe.wait_ge(s_xn, i * 3 + 3)
                for b in range(BATCH):
                    last = pe.transpose(bank[0][:, b * P:(b + 1) * P], xn[:, b, :], cst("ident"))
                last.then_inc(s_xt, 1)
                pe.wait_ge(s_xm, i + 1)
                pe.matmul(bank[1][:, 0:N], a_lora[:, 0:P], xm[:, :, :].rearrange(flat), start=True, stop=True)
                pe.matmul(bank[1][0:LORA, N:2 * N], a_lora[:, P:P + LORA], xm[:, :, :].rearrange(flat),
                          start=True, stop=True).then_inc(s_lora, 1)
                pe.wait_ge(s_lh, i * 2 + 2)
                for f in range(4):
                    mm = pe.matmul(bank[2 + f // 2][:, f % 2 * N:(f % 2 + 1) * N], b_pad[:, f, :], lh[:, :],
                                   start=True, stop=True)
                    if f % 2:
                        mm.then_inc(s_mix, 1)
                pe.matmul(bank[4][:, 0:N], b_pad[0:LORA, 4, :], lh4[:, :], start=True, stop=True).then_inc(s_mix, 1)
                pe.wait_ge(s_xx, i * MIXES + 1)
                pe.matmul(bank[1][0:TD_RANK, 0:N], td_a[:, :], xx[:, 0].rearrange(flat), start=True,
                          stop=True).then_inc(s_td, 1)
                pe.wait_ge(s_xx, i * MIXES + 2)
                pe.matmul(bank[2][:, 0:N], wT[:, 0, :], xx[:, 1].rearrange(flat), start=True,
                          stop=True).then_inc(s_proj, 1)
                pe.wait_ge(s_tw, i + 1)
                pe.matmul(bank[1][:, N:2 * N], td_b[:, :], tw[:, :], start=True, stop=True).then_inc(s_td, 1)
                pe.wait_ge(s_xx, i * MIXES + 3)
                for b in range(BATCH):
                    last = pe.matmul(bank[0][:, b * P:(b + 1) * P], xx[:, 2, b, :], wT[:, 1, :], start=True, stop=True)
                last.then_inc(s_proj, 1)
                pe.wait_ge(s_xx, i * MIXES + 4)
                pe.matmul(bank[3][:, 0:N], wT[:, 2, :], xx[:, 3].rearrange(flat), start=True,
                          stop=True).then_inc(s_proj, 1)
                pe.wait_ge(s_xx, i * MIXES + 5)
                pe.matmul(bank[4][:, 0:N], wT[:, 3, :], xx[:, 4].rearrange(flat), start=True,
                          stop=True).then_inc(s_proj, 1)

                def leaf_scores(slot, k_op, r_op):
                    for u in range(4):
                        h, b = u // 2, u % 2
                        rows = slice(h * RW_DIM, (h + 1) * RW_DIM)
                        for q in range(4):
                            cols = slice(b * P + q * LEAF, b * P + (q + 1) * LEAF)
                            pe.matmul(pair[q * LEAF:(q + 1) * LEAF, u * 256 + slot * LEAF:u * 256 + (slot + 1) * LEAF],
                                      k_op[rows, cols], r_op[rows, cols], start=True, stop=True,
                                      tile_position=(h * RW_DIM, q * LEAF))

                pe.wait_ge(s_diag, i * 4 + 4)
                pe.nop(nofuse=True)
                leaf_scores(0, kd, rd)
                for m in (1, 2, 3, 4):
                    pe.wait_ge(s_r, i * LEVELS + m)
                    pe.wait_ge(s_k, i * LEVELS + m)
                    pe.wait_ge(s_rc, i * 2 * LEVELS + 2 * m)
                    pe.nop(nofuse=True)
                    leaf_scores(m, kl[m], rl[m])
                pe.wait_ge(s_r, i * LEVELS + 6)
                pe.wait_ge(s_k, i * LEVELS + 6)
                pe.wait_ge(s_rc, i * 2 * LEVELS + 12)
                pe.nop(nofuse=True)
                for u in range(4):
                    h, b = u // 2, u % 2
                    rows = slice(h * RW_DIM, (h + 1) * RW_DIM)
                    for q in (0, 2):
                        s0 = b * P + q * LEAF
                        pe.matmul(pair[q * LEAF:(q + 1) * LEAF, u * 256 + 224:u * 256 + 256],
                                  kl[5][rows, s0:s0 + LEAF], rl[5][rows, s0 + LEAF:s0 + 2 * LEAF], start=True,
                                  stop=True, tile_position=(h * RW_DIM, q * LEAF))
                    last = pe.matmul(pair[0:64, u * 256 + 160:u * 256 + 224], kl[6][rows, b * P:b * P + 64],
                                     rl[6][rows, b * P + 64:b * P + 128], start=True, stop=True,
                                     tile_position=(h * RW_DIM, 0))
                last.then_inc(s_leafmm, 1)
                pe.wait_ge(s_k, i * LEVELS + 7)
                pe.wait_ge(s_r, i * LEVELS + 7)
                pe.wait_ge(s_rc, i * 2 * LEVELS + 14)
                for b in range(BATCH):
                    last = pe.transpose(bank[1][:, b * P:(b + 1) * P], kl[7][:, b * P:(b + 1) * P], cst("ident"))
                last.then_inc(s_ktT, 1)
                pe.wait_ge(s_att, i * 4 + 4)
                pe.wait_ge(s_off, i * 3 + 3)
                pe.wait_ge(s_evac, i * 3 + 3)
                for b in range(BATCH):
                    pe.matmul(bank[5][:, b * P:(b + 1) * P], rl[7][:, b * P:(b + 1) * P], state[:, b, :],
                              start=True, stop=False, skip_group_check=True)
                    for h in range(RW_HEADS):
                        pe.matmul(bank[5][:, b * P + h * RW_DIM:b * P + (h + 1) * RW_DIM], att[:, h * BATCH + b, :],
                                  v_sb[:, b, h * RW_DIM:(h + 1) * RW_DIM], start=False, stop=True,
                                  skip_group_check=True)
                pe.wait_ge(s_ktm, i + 1)
                for b in range(BATCH):
                    last = pe.matmul(bank[5][:, N + b * P:N + (b + 1) * P], ktm[:, b, :], v_sb[:, b, :], start=True,
                                     stop=True, skip_group_check=True)
                last.then_inc(s_kv, 1)
                pe.wait_ge(s_yn, i * 4 + 4)
                for b in range(BATCH):
                    last = pe.transpose(bank[0][:, b * P:(b + 1) * P], yn[:, b, :], cst("ident"))
                last.then_inc(s_zt, 1)
                pe.wait_ge(s_zg, i + 1)
                for b in range(BATCH):
                    last = pe.matmul(bank[2][:, b * P:(b + 1) * P], zT[:, b, :], wT[:, 4, :], start=True, stop=True)
                last.then_inc(s_o, 1)


def expert_phase(nc, t, x_sb, eps_pow, sbw, mod_row, bank, cst, mv_next):
    with ExitStack() as ctx:
        def sb(name, shape, dt=F32):
            return ctx.enter_context(nc.sbuf_tensor(name, shape, dt))

        def sem(name):
            return nc.alloc_semaphore(name)

        GROUP = 4
        NG = TILES // GROUP
        DEPTH = len(bank)
        HALF = DEPTH // 2
        ROUNDS = SLOT_TILES // DEPTH
        FILLS = SLOTS * C // (P * 1024)

        router = sb("router", [P, E0])
        zero = sb("zero", [P, 1024])
        st = sb("r_st", [P, TILES, 6])
        mv = sb("r_mv", [P, TILES, 2])
        rstd = sb("r_rstd", [P, TILES])
        h_all = sb("r_h_all", [P, TILES, C])
        hT = [sb(f"r_hT{g}", [P, GROUP, P]) for g in range(NG)]
        lg = sb("r_lg", [P, TILES, E0])
        mx = sb("r_mx", [P, TILES, 8])
        idx = sb("r_idx", [P, TILES, 8], U32)
        idf = sb("r_idf", [P, TILES])
        weight = sb("router_weight", [P, TILES])
        oh = sb("r_oh", [P, E0, TILES])
        incl = sb("r_incl", [P, E0, TILES])
        excl = sb("r_excl", [P, E0, TILES])
        place = sb("r_place", [P, E0, TILES])
        place_of = sb("r_place_of", [P, TILES])
        slot = sb("slot_of_token", [P, TILES], U32)
        cnt_i = sb("r_cnt_i", [P, E0], I32)
        ntile = sb("r_ntile", [P, E0])
        ends = sb("r_ends", [P, E0])
        base = sb("r_base", [P, E0])
        le = sb("r_le", [1, SLOT_TILES, E0])
        te = sb("r_te", [1, SLOT_TILES])
        expert = sb("expert_of_tile", [1, SLOT_TILES], I32)

        weights = [sb(f"e_w{k}", [P, W0]) for k in range(DEPTH)]
        xg = [sb(f"e_xg{s}", [P, HALF, C]) for s in range(2)]
        xgT = [sb(f"e_xgT{k}", [P, P]) for k in range(DEPTH)]
        hid = [sb(f"e_hid{k}", [P, 2, P]) for k in range(DEPTH)]
        yg = [sb(f"e_yg{s}", [P, HALF, C]) for s in range(2)]
        yt = sb("e_yt", [P, TILES, C])

        s_in, s_zero, s_fill = sem("r_in"), sem("r_zero"), sem("r_fill")
        s_st, s_mv, s_rstd, s_mod, s_h = sem("r_s_st"), sem("r_s_mv"), sem("r_s_rstd"), sem("r_s_mod"), sem("r_s_h")
        s_xt, s_ht, s_logit, s_lg, s_mx = sem("r_s_xt"), sem("r_s_ht"), sem("r_s_logit"), sem("r_s_lg"), sem("r_s_mx")
        s_idx, s_oh, s_rank, s_cnt, s_step = (sem("r_s_idx"), sem("r_s_oh"), sem("r_s_rank"), sem("r_s_cnt"),
                                              sem("r_s_step"))
        s_exp, s_slot, s_tile, s_sent = sem("r_s_exp"), sem("r_s_slot"), sem("r_s_tile"), sem("r_s_sent")
        s_x = [sem(f"e_s_x{s}") for s in range(2)]
        s_wt = [sem(f"e_s_wt{k}") for k in range(DEPTH)]
        s_out = [sem(f"e_s_out{s}") for s in range(2)]
        e_xt, e_xc, e_up, e_gelu, e_down, e_y = (sem("e_s_xt"), sem("e_s_xc"), sem("e_s_up"), sem("e_s_gelu"),
                                                 sem("e_s_down"), sem("e_s_y"))
        s_back = [sem(f"e_s_back{g}") for g in range(NG)]
        s_scaled, s_added, s_nst = sem("e_s_scaled"), sem("e_s_added"), sem("e_s_nst")
        block = ctx.enter_context(nc.Block())

        def tr(k):
            return bank[k][:, 2 * P:3 * P]

        def down(k):
            return bank[k][:, 3 * P:4 * P]

        @block.sync
        def _(sp):
            sp.dma_start(router[:, :], t["L0_ffn_router_w"]).then_inc(s_in, 16)
            sp.wait_ge(s_zero, 1)
            slots = t["slots_in"].rearrange("(q p a) n -> q p (a n)", p=P, a=8)
            for q in range(FILLS):
                sp.dma_start(slots[q], zero[:, :]).then_inc(s_fill, 16)

            def experts_of(i):
                return [sp.value_load(expert[0:1, bass.ds(i * DEPTH + k, 1)], min_val=0, max_val=E0 - 1)
                        for k in range(DEPTH)]

            def load_weights(k, e):
                sp.dma_start(weights[k][:, :], t["experts0"][bass.ds(e, 1), :, :].rearrange("e p n -> p (e n)"))\
                    .then_inc(s_wt[k], 16)

            def load_x(s, i):
                sp.dma_start(xg[s][:, :, :], t["slots_in"][bass.ds((i * 2 + s) * HALF * P, HALF * P), :]
                             .rearrange("(k p) n -> p k n", p=P)).then_inc(s_x[s], 16)

            def store(s, i):
                sp.dma_start(t["slots_out"][bass.ds((i * 2 + s) * HALF * P, HALF * P), :]
                             .rearrange("(k p) n -> p k n", p=P), yg[s][:, :, :]).then_inc(s_out[s], 16)

            sp.wait_ge(s_tile, 1)
            for k, e in enumerate(experts_of(0)):
                load_weights(k, e)
            sp.wait_ge(s_sent, 16 * TILES)
            for s in range(2):
                load_x(s, 0)
            with sp.Fori(0, ROUNDS - 1) as i:
                experts = experts_of(i + 1)
                for s in range(2):
                    sp.wait_ge(e_xt, i * DEPTH + (s + 1) * HALF)
                    load_x(s, i + 1)
                    for k in range(s * HALF, (s + 1) * HALF):
                        sp.wait_ge(e_y, i * DEPTH + (k + 1 + DEPTH))
                        load_weights(k, experts[k])
                    store(s, i)
            for s in range(2):
                sp.wait_ge(e_y, ROUNDS * DEPTH + (s + 1) * HALF)
                store(s, ROUNDS - 1)
            for s in range(2):
                sp.wait_ge(s_out[s], 16 * (ROUNDS + 1))

        @block.gpsimd
        def _(pool):
            pool.memset(zero[:, :], 0.0).then_inc(s_zero, 1)
            for g in range(NG):
                part = slice(g * GROUP, (g + 1) * GROUP)
                pool.wait_ge(s_mv, (g + 1) * GROUP)
                pool.tensor_scalar(rstd[:, part], mv[:, part, 1], LN_EPS, None, ALU.add).then_inc(s_rstd, 1)
                pool.wait_ge(s_rstd, 2 * g + 1)
                pool.tensor_tensor(rstd[:, part], rstd[:, part], eps_pow[:, 0:GROUP], ALU.pow).then_inc(s_rstd, 1)
            pool.wait_ge(s_fill, 16 * FILLS)
            pool.wait_ge(s_h, TILES)
            pool.wait_ge(s_slot, 1)
            for c in range(TILES):
                pool.indirect_dma_start(out=t["slots_in"], out_offset=bass.IndirectOffsetOnAxis(
                    ap=slot[:, c:c + 1], axis=0), in_=h_all[:, c, :], in_offset=None).then_inc(s_sent, 16)
            pool.wait_ge(s_sent, 16 * TILES)
            for s in range(2):
                pool.wait_ge(s_out[s], 16 * (ROUNDS + 1))
            for c in range(TILES):
                pool.indirect_dma_start(out=yt[:, c, :], out_offset=None, in_=t["slots_out"],
                                        in_offset=bass.IndirectOffsetOnAxis(ap=slot[:, c:c + 1], axis=0))\
                    .then_inc(s_back[c // GROUP], 16)

        @block.scalar
        def _(act):
            for g in range(NG):
                act.wait_ge(s_xt, g + 1)
                act.activation(hT[g][:, :, :], bank[g][:, :].rearrange("p (k n) -> p k n", k=GROUP),
                               ACT.Copy).then_inc(s_ht, 1)
            act.wait_ge(s_mx, TILES)
            act.activation(weight[:, :], mx[:, :, 0], ACT.Exp, scale=-1.0).then_inc(s_exp, 1)
            for s in range(2):
                act.sem_inc(s_out[s], 16)
            with act.Fori(0, ROUNDS) as i:
                for half in (range(HALF), range(HALF, DEPTH)):
                    for k in half:
                        act.wait_ge(e_xt, i * DEPTH + (k + 1))
                        act.activation(xgT[k][:, :], tr(k), ACT.Copy).then_inc(e_xc, 1)
                    for k in half:
                        act.wait_ge(e_up, i * DEPTH + (k + 1))
                        for f in range(2):
                            act.activation(hid[k][:, f, :], bank[k][:, f * P:(f + 1) * P], ACT.Gelu,
                                           bias=weights[k][:, 2 * F0 + f:2 * F0 + f + 1]).then_inc(e_gelu, 1)

        @block.vector
        def _(dve):
            for g in range(NG):
                for c in range(g * GROUP, (g + 1) * GROUP):
                    dve.bn_stats(st[:, c, :], x_sb[:, c, :]).then_inc(s_st, 1)
                dve.wait_ge(s_st, (g + 1) * GROUP)
                for c in range(g * GROUP, (g + 1) * GROUP):
                    dve.bn_aggr(mv[:, c, :], st[:, c, :]).then_inc(s_mv, 1)
            dve.wait_ge(s_mv, TILES)
            for c in range(TILES):
                dve.scalar_tensor_tensor(out=h_all[:, c, :], in0=x_sb[:, c, :], scalar=mv[:, c, 0:1],
                                         in1=sbw[:, 1, c // CHUNKS, :], op0=ALU.subtract,
                                         op1=ALU.mult).then_inc(s_mod, 1)
            dve.wait_ge(s_rstd, 2 * NG)
            for c in range(TILES):
                dve.wait_ge(s_mod, c + 1)
                dve.scalar_tensor_tensor(out=h_all[:, c, :], in0=h_all[:, c, :], scalar=rstd[:, c:c + 1],
                                         in1=sbw[:, 0, c // CHUNKS, :], op0=ALU.mult, op1=ALU.add).then_inc(s_h, 1)
            dve.wait_ge(s_logit, 1)
            dve.tensor_copy(lg[:, :, :], bank[4][:, 0:TILES * E0].rearrange("p (c n) -> p c n", c=TILES))\
                .then_inc(s_lg, 1)
            dve.wait_ge(s_lg, 1)
            for c in range(TILES):
                dve.max(mx[:, c, :], lg[:, c, :]).then_inc(s_mx, 1)
            for c in range(TILES):
                dve.wait_ge(s_mx, c + 1)
                dve.max_index(idx[:, c, :], mx[:, c, :], lg[:, c, :]).then_inc(s_idx, 1)
            dve.wait_ge(s_idx, TILES)
            dve.tensor_copy(idf[:, :], idx[:, :, 0]).then_inc(s_idx, 1)
            dve.wait_ge(s_idx, TILES + 1)
            dve.tensor_tensor(oh[:, :, :], cst("iota16")[:, :, None].to_broadcast([P, E0, TILES]),
                              idf[:, None, :].to_broadcast([P, E0, TILES]), ALU.is_equal).then_inc(s_oh, 1)
            dve.wait_ge(s_oh, 1)
            flat = "p e c -> p (e c)"
            dve.tensor_tensor_scan(incl[:, :, :].rearrange(flat), cst("restart"), oh[:, :, :].rearrange(flat), 0.0,
                                   ALU.mult, ALU.add).then_inc(s_oh, 1)
            dve.wait_ge(s_oh, 2)
            dve.tensor_tensor(excl[:, :, :], incl[:, :, :], oh[:, :, :], ALU.subtract).then_inc(s_oh, 1)
            dve.wait_ge(s_cnt, 1)
            dve.tensor_scalar(cnt_i[:, :], bank[0][:, 0:E0], float(P - 1), None, ALU.add).then_inc(s_step, 1)
            dve.wait_ge(s_step, 1)
            dve.tensor_scalar(cnt_i[:, :], cnt_i[:, :], 7, None, ALU.logical_shift_right).then_inc(s_step, 1)
            dve.wait_ge(s_step, 2)
            dve.tensor_copy(ntile[:, :], cnt_i[:, :]).then_inc(s_step, 1)
            dve.wait_ge(s_step, 3)
            dve.tensor_tensor_scan(ends[:, :], cst("ones")[:, 0:E0], ntile[:, :], 0.0, ALU.mult,
                                   ALU.add).then_inc(s_step, 1)
            dve.wait_ge(s_step, 4)
            dve.tensor_tensor(base[:, :], ends[:, :], ntile[:, :], ALU.subtract).then_inc(s_step, 1)
            dve.wait_ge(s_step, 5)
            dve.wait_ge(s_rank, 1)
            dve.scalar_tensor_tensor(out=place[:, :, :], in0=base[:, :, None].to_broadcast([P, E0, TILES]),
                                     scalar=float(P), in1=bank[5][:, 0:E0 * TILES].rearrange("p (e c) -> p e c", e=E0),
                                     op0=ALU.mult, op1=ALU.add).then_inc(s_step, 1)
            dve.wait_ge(s_step, 6)
            dve.tensor_tensor(place[:, :, :], place[:, :, :], oh[:, :, :], ALU.mult).then_inc(s_step, 1)
            dve.wait_ge(s_step, 7)
            dve.tensor_reduce(place_of[:, :], place[:, :, :].rearrange("p e c -> p c e"), AX.X, ALU.add)\
                .then_inc(s_step, 1)
            dve.wait_ge(s_step, 8)
            dve.tensor_copy(slot[:, :], place_of[:, :]).then_inc(s_slot, 1)
            dve.tensor_tensor(le[:, :, :], ends[0:1, None, :].to_broadcast([1, SLOT_TILES, E0]),
                              cst("iota32")[0:1, :, None].to_broadcast([1, SLOT_TILES, E0]),
                              ALU.is_le).then_inc(s_step, 1)
            dve.wait_ge(s_step, 9)
            dve.tensor_reduce(te[:, :], le[:, :, :], AX.X, ALU.add).then_inc(s_step, 1)
            dve.wait_ge(s_step, 10)
            dve.tensor_scalar(expert[:, :], te[:, :], float(E0 - 1), None, ALU.min).then_inc(s_tile, 1)
            dve.wait_ge(s_exp, 1)
            dve.tensor_scalar(weight[:, :], weight[:, :], 1.0, None, ALU.add).then_inc(s_exp, 1)
            dve.wait_ge(s_exp, 2)
            dve.reciprocal(weight[:, :], weight[:, :]).then_inc(s_exp, 1)
            dve.wait_ge(s_exp, 3)
            with dve.Fori(0, ROUNDS) as i:
                for k in range(DEPTH):
                    dve.wait_ge(e_down, i * DEPTH + (k + 1))
                    dve.wait_ge(s_out[k // HALF], i * 16 + 16)
                    dve.tensor_copy(yg[k // HALF][:, k % HALF, :], down(k)).then_inc(e_y, 1)
            for g in range(NG):
                tiles = range(g * GROUP, (g + 1) * GROUP)
                dve.wait_ge(s_back[g], 16 * GROUP)
                for c in tiles:
                    dve.scalar_tensor_tensor(out=yt[:, c, :], in0=yt[:, c, :], scalar=weight[:, c:c + 1],
                                             in1=mod_row[:, 0, 1, c // CHUNKS, :], op0=ALU.mult,
                                             op1=ALU.mult).then_inc(s_scaled, 1)
                dve.wait_ge(s_scaled, (g + 1) * GROUP)
                part = slice(g * GROUP, (g + 1) * GROUP)
                dve.tensor_tensor(x_sb[:, part, :], x_sb[:, part, :], yt[:, part, :], ALU.add).then_inc(s_added, 1)
                dve.wait_ge(s_added, g + 1)
                for c in tiles:
                    dve.bn_stats(st[:, c, :], x_sb[:, c, :]).then_inc(s_nst, 1)
                dve.wait_ge(s_nst, g * 2 * GROUP + GROUP)
                for c in tiles:
                    dve.bn_aggr(mv_next[:, c, :], st[:, c, :]).then_inc(s_nst, 1)
            dve.wait_ge(s_nst, NG * 2 * GROUP)

        @block.tensor
        def _(pe):
            pe.sem_inc(e_y, DEPTH)
            pe.wait_ge(s_in, 16)
            for g in range(NG):
                pe.wait_ge(s_h, (g + 1) * GROUP)
                for k in range(GROUP):
                    last = pe.transpose(bank[g][:, k * P:(k + 1) * P], h_all[:, g * GROUP + k, :], cst("ident"))
                last.then_inc(s_xt, 1)
            for g in range(NG):
                pe.wait_ge(s_ht, g + 1)
                for k in range(GROUP):
                    c = g * GROUP + k
                    last = pe.matmul(bank[4][:, c * E0:(c + 1) * E0], hT[g][:, k, :], router[:, :], start=True,
                                     stop=True)
            last.then_inc(s_logit, 1)
            pe.wait_ge(s_oh, 2)
            pe.matmul(bank[0][:, 0:E0], cst("ones"), incl[:, :, TILES - 1], start=True, stop=True).then_inc(s_cnt, 1)
            pe.matmul(bank[5][:, 0:E0 * TILES], cst("before"), oh[:, :, :].rearrange("p e c -> p (e c)"), start=True,
                      stop=False)
            pe.wait_ge(s_oh, 3)
            pe.matmul(bank[5][:, 0:E0 * TILES], cst("ones"), excl[:, :, :].rearrange("p e c -> p (e c)"), start=False,
                      stop=True).then_inc(s_rank, 1)
            with pe.Fori(0, ROUNDS) as i:

                def transposes(half):
                    for k in half:
                        pe.wait_ge(s_x[k // HALF], i * 16 + 16)
                        pe.wait_ge(e_y, i * DEPTH + (k + 1))
                        pe.transpose(tr(k), xg[k // HALF][:, k % HALF, :], cst("ident")).then_inc(e_xt, 1)

                def ups(half):
                    for k in half:
                        pe.wait_ge(e_xc, i * DEPTH + (k + 1))
                        pe.wait_ge(s_wt[k], i * 16 + 16)
                        for f in range(2):
                            last = pe.matmul(bank[k][:, f * P:(f + 1) * P], weights[k][:, f * P:(f + 1) * P],
                                             xgT[k][:, :], start=True, stop=True)
                        last.then_inc(e_up, 1)

                def downs(half):
                    for k in half:
                        pe.wait_ge(e_gelu, i * (2 * DEPTH) + (2 * k + 2))
                        for f in range(2):
                            pe.matmul(down(k), hid[k][:, f, :], weights[k][:, F0 + f * P:F0 + (f + 1) * P],
                                      start=(f == 0), stop=False)
                        pe.matmul(down(k), weights[k][:, W0 - 1:W0].to_broadcast([P, P]), cst("ident"), start=False,
                                  stop=True)\
                            .then_inc(e_down, 1)

                first, second = range(HALF), range(HALF, DEPTH)
                transposes(first)
                ups(first)
                transposes(second)
                downs(first)
                ups(second)
                downs(second)


def norm_transpose_phase(nc, x_sb, eps_pow, mod_col, bank, cst, mv, hT_all):
    with ExitStack() as ctx:
        def sb(name, shape, dt=F32):
            return ctx.enter_context(nc.sbuf_tensor(name, shape, dt))

        def sem(name):
            return nc.alloc_semaphore(name)

        rstd = sb("n_rstd", [P, TILES])
        xn = sb("n_xn", [P, TILES, C])
        s_rstd, s_xn, s_xt, s_ht = sem("n_s_rstd"), sem("n_s_xn"), sem("n_s_xt"), sem("n_s_ht")
        GROUP = 4
        block = ctx.enter_context(nc.Block())

        @block.vector
        def _(dve):
            dve.wait_ge(s_rstd, 2)
            for c in range(TILES):
                dve.tensor_scalar(xn[:, c, :], x_sb[:, c, :], mv[:, c, 0:1], rstd[:, c:c + 1], ALU.subtract,
                                  ALU.mult).then_inc(s_xn, 1)

        @block.gpsimd
        def _(pool):
            pool.tensor_scalar(rstd[:, :], mv[:, :, 1], LN_EPS, None, ALU.add).then_inc(s_rstd, 1)
            pool.wait_ge(s_rstd, 1)
            pool.tensor_tensor(rstd[:, :], rstd[:, :], eps_pow[:, 0:TILES], ALU.pow).then_inc(s_rstd, 1)

        @block.tensor
        def _(pe):
            for g in range(TILES // GROUP):
                pe.wait_ge(s_xn, (g + 1) * GROUP)
                for k in range(GROUP):
                    last = pe.transpose(bank[g][:, k * P:(k + 1) * P], xn[:, g * GROUP + k, :], cst("ident"))
                last.then_inc(s_xt, 1)

        @block.scalar
        def _(act):
            for g in range(TILES // GROUP):
                b = g * GROUP // CHUNKS
                act.wait_ge(s_xt, g + 1)
                act.activation(hT_all[:, g * GROUP:(g + 1) * GROUP, :],
                               bank[g][:, :].rearrange("p (k n) -> p k n", k=GROUP), ACT.Identity,
                               bias=mod_col[:, 1, 0, b:b + 1], scale=mod_col[:, 1, 1, b:b + 1]).then_inc(s_ht, 1)


def hla_phase(nc, x_bc, mod_row, bank, pair, cst, hT_all, W, s_weights):
    with ExitStack() as ctx:
        def sb(name, shape, dt=F32):
            return ctx.enter_context(nc.sbuf_tensor(name, shape, dt))

        def sem(name):
            return nc.alloc_semaphore(name)

        J = range(GROUPS)
        hT = [sb(f"h_hT{b}", [P, P]) for b in range(BATCH)]
        v_sb = [sb(f"h_v{b}", [P, HL_HEADS * HL_DIM]) for b in range(BATCH)]
        qk = [[sb(f"h_qk{b}{j}", [P, 2, P]) for j in J] for b in range(BATCH)]
        qkd = [[sb(f"h_qkd{b}{j}", [P, 2, P]) for j in J] for b in range(BATCH)]
        qB = [[sb(f"h_qB{b}{j}", [P, HPG, P]) for j in J] for b in range(BATCH)]
        kB = [[sb(f"h_kB{b}{j}", [P, HPG, P]) for j in J] for b in range(BATCH)]
        kg = [sb(f"h_kg{j}", [P, 2, P]) for j in J]
        kqd = [sb(f"h_kqd{j}", [P, 2, P]) for j in J]
        m1 = [sb(f"h_m1{j}", [P, HPG, P]) for j in J]
        m2 = [sb(f"h_m2{j}", [P, HPG, P]) for j in J]
        m3 = [sb(f"h_m3{j}", [P, HPG, P]) for j in J]
        aT = [sb(f"h_aT{j}", [P, P]) for j in J]
        aTd = [sb(f"h_aTd{j}", [P, P]) for j in J]
        oT = [sb(f"h_oT{j}", [P, P]) for j in J]
        states = [[sb(f"h_state{b}{j}", [P, 3, P]) for j in J] for b in range(BATCH)]
        fresh = [sb(f"h_fresh{k}", [P, 3, P]) for k in range(2)]
        gated = sb("h_gated", [P, C])

        X = [k[:, :] for k in bank[0:4]]
        ring = [pair[:, 0:512], pair[:, 512:1024]]
        front = bank[4]
        upd = bank[5]
        s_zero, s_hT, s_v, s_vc = sem("h_s_zero"), sem("h_s_hT"), sem("h_s_v"), sem("h_s_vc")
        s_qk, s_qkc, s_qkd, s_bd = sem("h_s_qk"), sem("h_s_qkc"), sem("h_s_qkd"), sem("h_s_bd")
        s_tm, s_tmc, s_sc, s_mask = sem("h_s_tm"), sem("h_s_tmc"), sem("h_s_sc"), sem("h_s_mask")
        s_ga, s_gac, s_aTd, s_o, s_oc = sem("h_s_ga"), sem("h_s_gac"), sem("h_s_aTd"), sem("h_s_o"), sem("h_s_oc")
        s_upd, s_new, s_st, s_out = sem("h_s_upd"), sem("h_s_new"), sem("h_s_st"), sem("h_s_out")
        s_gated, s_x = sem("h_s_gated"), sem("h_s_x")
        block = ctx.enter_context(nc.Block())

        def nth(i, b, per_tile, k):
            return i * (BATCH * per_tile) + (b * per_tile + k + 1)

        hT_bc = hT_all[:, :, :].rearrange("p (b c) n -> p b c n", b=BATCH)
        heads = cst("head4")

        def following(i, b):
            return (i, 1) if b == 0 else (i + 1, 0)

        @block.gpsimd
        def _(pool):
            def fetch(i, b):
                pool.tensor_tensor(hT[b][:, None, :], hT_all[:, bass.ds(i + b * CHUNKS, 1), :],
                                   cst("ones")[:, None, :], ALU.mult).then_inc(s_hT, 1)

            def expand(i, b):
                for j in J:
                    pool.wait_ge(s_qkc, nth(i, b, GROUPS, j))
                    pool.wait_ge(s_o, nth(i, b, GROUPS, j))
                    for k, full in ((1, kB[b]), (0, qB[b])):
                        pool.tensor_tensor(full[j][:, :, :], qk[b][j][:, k, None, :].to_broadcast([P, HPG, P]),
                                           heads[:, 0::HL_DIM, None].to_broadcast([P, HPG, P]),
                                           ALU.mult).then_inc(s_bd, 1)
                    pool.tensor_tensor(qkd[b][j][:, :, :], qk[b][j][:, :, :],
                                       cst("decay_row")[:, None, :].to_broadcast([P, 2, P]),
                                       ALU.mult).then_inc(s_qkd, 1)

            fetch(0, 0)
            expand(0, 0)
            with pool.Fori(0, CHUNKS) as i:
                for b in range(BATCH):
                    fetch(*following(i, b))
                    expand(*following(i, b))
                    pool.wait_ge(s_gated, nth(i, b, 1, 1))
                    pool.tensor_tensor(x_bc[:, b, bass.ds(i, 1), :], x_bc[:, b, bass.ds(i, 1), :],
                                       gated[:, None, :], ALU.add).then_inc(s_x, 1)
            pool.wait_ge(s_x, TILES + 1)

        @block.scalar
        def _(act):
            def copy_v(i, b):
                act.wait_ge(s_v, nth(i, b, 1, 0))
                act.wait_ge(s_upd, nth(i, b, GROUPS, GROUPS - 1))
                act.activation(v_sb[b][:, :], front[:, :], ACT.Copy).then_inc(s_vc, 1)

            def copy_qk(i, b, j):
                act.wait_ge(s_qk, nth(i, b, GROUPS, j))
                act.activation(qk[b][j][:, :, :], front[:, 0:2 * P].rearrange("p (k n) -> p k n", k=2),
                               ACT.Copy).then_inc(s_qkc, 1)

            copy_v(0, 0)
            for j in J:
                copy_qk(0, 0, j)
            with act.Fori(0, CHUNKS) as i:
                for b in range(BATCH):
                    for j in J:
                        act.wait_ge(s_tm, nth(i, b, GROUPS, j))
                        act.activation(kg[j][:, 0, :], X[j][:, 2 * P:3 * P], ACT.Copy).then_inc(s_tmc, 1)
                        act.activation(kqd[j][:, :, :], X[j][:, 2 * P:4 * P].rearrange("p (k n) -> p k n", k=2),
                                       ACT.Copy, scale=cst("decay_col")[:, 0:1]).then_inc(s_tmc, 1)
                    copy_v(*following(i, b))
                    copy_qk(*following(i, b), 0)
                    for j in J:
                        act.wait_ge(s_ga, nth(i, b, GROUPS, j))
                        act.activation(aT[j][:, :], X[j][:, P:2 * P], ACT.Copy).then_inc(s_gac, 1)
                        act.activation(kg[j][:, 1, :], X[j][:, 0:P], ACT.Copy, scale=-1.0).then_inc(s_gac, 1)
                        if j == 1:
                            copy_qk(*following(i, b), 1)
                    copy_qk(*following(i, b), 2)
                    for j in J:
                        act.wait_ge(s_o, nth(i, b, GROUPS, j + 2 * GROUPS))
                        act.activation(oT[j][:, :], X[j][:, 2 * P:3 * P], ACT.Copy).then_inc(s_oc, 1)
                    copy_qk(*following(i, b), 3)

        @block.vector
        def _(dve):
            for b in range(BATCH):
                for j in J:
                    dve.memset(states[b][j][:, :, :], 0.0).then_inc(s_zero, 1)
            dve.wait_ge(s_zero, BATCH * GROUPS)
            dve.sem_inc(s_x, 1)
            dve.sem_inc(s_st, 2 * GROUPS)
            incl = cst("decay_incl")[:, None, :].to_broadcast([P, HPG, P])
            excl = cst("decay_excl")[:, None, :].to_broadcast([P, HPG, P])
            with dve.Fori(0, CHUNKS) as i:
                for b in range(BATCH):
                    n = 0
                    for kind, dsts, mask in ((0, (m1, m2), (incl, excl)), (1, (m3,), (incl,))):
                        for j in J:
                            for dst, msk in zip(dsts, mask):
                                dve.wait_ge(s_sc, nth(i, b, 12, n))
                                dve.tensor_tensor(dst[j][:, :, :], ring[n % 2].rearrange("p (h n) -> p h n", h=HPG),
                                                  msk, ALU.mult).then_inc(s_mask, 1)
                                n += 1
                        if kind == 0:
                            for j in J:
                                dve.wait_ge(s_gac, nth(i, b, 2 * GROUPS, 2 * j + 1))
                                dve.tensor_tensor(aTd[j][:, :], X[j][:, P:2 * P], cst("decay_row"),
                                                  ALU.mult).then_inc(s_aTd, 1)
                    for j in J:
                        dve.wait_ge(s_upd, nth(i, b, GROUPS, j + 2 * GROUPS))
                        dve.wait_ge(s_st, nth(i, b, GROUPS, j + 2 * GROUPS - 2))
                        dve.tensor_tensor(fresh[j % 2][:, :, :], upd[:, 0:3 * P].rearrange("p (k n) -> p k n", k=3),
                                          heads[:, None, :].to_broadcast([P, 3, P]), ALU.mult).then_inc(s_new, 1)
                        dve.wait_ge(s_new, nth(i, b, GROUPS, j + 1))
                        flat = "p k n -> p (k n)"
                        dve.scalar_tensor_tensor(out=states[b][j][:, :, :].rearrange(flat),
                                                 in0=states[b][j][:, :, :].rearrange(flat), scalar=GAMMA ** P,
                                                 in1=fresh[j % 2][:, :, :].rearrange(flat), op0=ALU.mult,
                                                 op1=ALU.add).then_inc(s_st, 1)
                    dve.wait_ge(s_out, nth(i, b, 1, 0))
                    dve.wait_ge(s_x, nth(i, b, 1, 0))
                    dve.tensor_tensor(gated[:, :], X[0][:, 3 * P:4 * P], mod_row[:, 1, 0, b, :],
                                      ALU.mult).then_inc(s_gated, 1)

        @block.tensor
        def _(pe):
            pe.wait_ge(s_weights, 16 * 4)
            pe.sem_inc(s_gated, 1)
            pe.sem_inc(s_o, 2 * GROUPS)
            pe.sem_inc(s_mask, 2)
            pe.sem_inc(s_new, 1)
            pe.sem_inc(s_upd, 2 * GROUPS)

            def project_v(i, b):
                pe.wait_ge(s_hT, nth(i, b, 1, 0))
                pe.matmul(front[:, :], hT[b][:, :], W["v"][:, :], start=True, stop=True).then_inc(s_v, 1)

            def project_qk(i, b, j):
                if j == 0:
                    pe.wait_ge(s_vc, nth(i, b, 1, 0))
                else:
                    pe.wait_ge(s_qkc, nth(i, b, GROUPS, j - 1))
                cols = slice(j * P, (j + 1) * P)
                pe.matmul(front[:, 0:P], W["q"][:, cols], hT[b][:, :], start=True, stop=True)
                pe.matmul(front[:, P:2 * P], W["k"][:, cols], hT[b][:, :], start=True, stop=True).then_inc(s_qk, 1)

            project_v(0, 0)
            for j in J:
                project_qk(0, 0, j)
            with pe.Fori(0, CHUNKS) as i:
                for b in range(BATCH):

                    def scores(lhs, rhs, n):
                        pe.wait_ge(s_mask, nth(i, b, 12, n))
                        for h in range(HPG):
                            last = pe.matmul(ring[n % 2][:, h * P:(h + 1) * P], lhs[:, h, :], rhs, start=True,
                                             stop=True)
                        last.then_inc(s_sc, 1)

                    def first_scores(j):
                        pe.wait_ge(s_bd, nth(i, b, 2 * GROUPS, 2 * j))
                        scores(kB[b][j], qk[b][j][:, 0, :], 2 * j)
                        pe.wait_ge(s_bd, nth(i, b, 2 * GROUPS, 2 * j + 1))
                        scores(qB[b][j], qk[b][j][:, 1, :], 2 * j + 1)

                    first_scores(0)
                    for j in J:
                        if j == 0:
                            pe.wait_ge(s_qkc, nth(i, b, GROUPS, GROUPS - 1))
                            pe.wait_ge(s_gated, nth(i, b, 1, 0))
                        pe.transpose(X[j][:, 2 * P:3 * P], qk[b][j][:, 1, :], cst("ident"))
                        pe.transpose(X[j][:, 3 * P:4 * P], qk[b][j][:, 0, :], cst("ident")).then_inc(s_tm, 1)
                    first_scores(1)
                    project_v(*following(i, b))
                    first_scores(2)
                    project_qk(*following(i, b), 0)
                    first_scores(3)
                    for j in J:
                        pe.wait_ge(s_tmc, nth(i, b, 2 * GROUPS, 2 * j + 1))
                        pe.wait_ge(s_qkd, nth(i, b, GROUPS, j))
                        pe.wait_ge(s_st, nth(i, b, GROUPS, j))
                        pe.wait_ge(s_mask, nth(i, b, 12, 2 * j + 1 + 2))
                        if j == 0:
                            pe.wait_ge(s_vc, nth(i, b, 1, 0))
                        g, a = X[j][:, 0:P], X[j][:, P:2 * P]
                        pe.matmul(g, qkd[b][j][:, 1, :], states[b][j][:, 2, :], start=True, stop=False,
                                  skip_group_check=True)
                        for h in range(HPG):
                            rows = slice(h * HL_DIM, (h + 1) * HL_DIM)
                            pe.matmul(g[:, rows], m2[j][:, h, :],
                                      v_sb[b][:, j * P + h * HL_DIM:j * P + (h + 1) * HL_DIM], start=False,
                                      stop=True, skip_group_check=True)
                        pe.matmul(a, states[b][j][:, 0, :], qkd[b][j][:, 0, :], start=True, stop=False,
                                  skip_group_check=True)
                        for h in range(HPG):
                            rows = slice(h * HL_DIM, (h + 1) * HL_DIM)
                            last = pe.matmul(a[rows, :], kg[j][:, 0, rows], m1[j][:, h, :], start=False, stop=True,
                                             skip_group_check=True, tile_position=(0, h * HL_DIM))
                        last.then_inc(s_ga, 1)
                        if j == 1:
                            project_qk(*following(i, b), 1)
                    for j in J:
                        pe.wait_ge(s_gac, nth(i, b, 2 * GROUPS, 2 * j))
                        scores(qB[b][j], aT[j][:, :], 8 + j)
                        if j == 1:
                            project_qk(*following(i, b), 2)
                    for j in J:
                        pe.wait_ge(s_gac, nth(i, b, 2 * GROUPS, 2 * j + 1))
                        pe.wait_ge(s_aTd, nth(i, b, GROUPS, j))
                        pe.wait_ge(s_mask, nth(i, b, 12, 8 + j + 2))
                        o = X[j][:, 2 * P:3 * P]
                        pe.matmul(o, states[b][j][:, 2, :], aTd[j][:, :], start=True, stop=False,
                                  skip_group_check=True)
                        pe.matmul(o, states[b][j][:, 1, :], qkd[b][j][:, 0, :], start=False, stop=False,
                                  skip_group_check=True)
                        for h in range(HPG):
                            rows = slice(h * HL_DIM, (h + 1) * HL_DIM)
                            pe.matmul(o[rows, :], v_sb[b][:, j * P + h * HL_DIM:j * P + (h + 1) * HL_DIM],
                                      m3[j][:, h, :], start=False, stop=False, skip_group_check=True,
                                      tile_position=(0, h * HL_DIM))
                        for h in range(HPG):
                            rows = slice(h * HL_DIM, (h + 1) * HL_DIM)
                            last = pe.matmul(o[rows, :], kg[j][:, 1, rows], m1[j][:, h, :], start=False, stop=True,
                                             skip_group_check=True, tile_position=(0, h * HL_DIM))
                        last.then_inc(s_o, 1)
                        pe.wait_ge(s_new, nth(i, b, GROUPS, j))
                        pe.matmul(upd[:, 0:2 * P], kqd[j][:, 0, :], kg[j][:, :, :].rearrange("p k n -> p (k n)"),
                                  start=True, stop=True)
                        pe.matmul(upd[:, 2 * P:3 * P], kqd[j][:, 1, :], v_sb[b][:, j * P:(j + 1) * P], start=True,
                                  stop=True).then_inc(s_upd, 1)
                    project_qk(*following(i, b), 3)
                    for j in J:
                        pe.wait_ge(s_oc, nth(i, b, GROUPS, j))
                        last = pe.matmul(X[0][:, 3 * P:4 * P], oT[j][:, :], W["o"][:, j, :], start=(j == 0),
                                         stop=(j == GROUPS - 1))
                    last.then_inc(s_out, 1)


def swiglu_phase(nc, t, x_sb, eps_pow, sbw, mod_row, bank, pair, cst, W, s_weights, out):
    with ExitStack() as ctx:
        def sb(name, shape, dt=F32):
            return ctx.enter_context(nc.sbuf_tensor(name, shape, dt))

        def sem(name):
            return nc.alloc_semaphore(name)

        N = 512
        TPG = N // P
        NG = TILES // TPG
        ROUNDS = NG // BATCH
        E = E1_LIVE
        gate = sb("g_gate", [P, E])
        st = sb("g_st", [P, TILES, 6])
        mv = sb("g_mv", [P, TILES, 2])
        rstd = sb("g_rstd", [P, TILES])
        h_all = sb("g_h_all", [P, TILES, C])
        xT_all = sb("g_xT_all", [P, TILES, P])
        best = sb("g_best", [P, TILES])
        shifted = sb("g_shifted", [P, TILES, E])
        prob = sb("g_prob", [P, TILES, 8])
        mx = sb("g_mx", [P, TILES, 8])
        idx = sb("g_idx", [P, TILES, 8], U32)
        idf = sb("g_idf", [P, TILES, 2])
        den = sb("g_den", [P, TILES])
        cw = sb("g_cw", [P, 2, TILES, E])
        hs = [sb(f"g_hs{k}", [P, E, C]) for k in range(2)]
        xg = [sb(f"f_xg{b}", [P, 1 + E, N]) for b in range(BATCH)]
        sa = [sb(f"f_sa{k}", [P, N]) for k in range(2)]
        hh = [sb(f"f_h{k}", [P, N]) for k in range(2)]
        oT = [sb(f"f_oT{b}", [P, N]) for b in range(BATCH)]
        gated = [sb(f"f_gated{b}", [P, TPG, C]) for b in range(BATCH)]
        up_a = [bank[0], bank[1]]
        up_b = [bank[2], bank[3]]
        acc = [bank[4], bank[5]]
        back, scaled = pair[:, 0:512], pair[:, 512:1024]
        units = []
        for e in range(0, E, 2):
            units += [(e, f) for f in range(FULL1)] + [(e + 1, f) for f in range(FULL1)] + [(e, None)]
        U = len(units)
        assert U % 2 == 0
        prepare_at = {3 + 4 * k: k for k in range(TPG)}
        assert max(prepare_at) < U

        s_gate, s_pad, s_st, s_mv, s_rstd = (sem("g_s_gate"), sem("g_s_pad"), sem("g_s_st"), sem("g_s_mv"),
                                             sem("g_s_rstd"))
        s_mod, s_h, s_xt, s_keep, s_logit = (sem("g_s_mod"), sem("g_s_h"), sem("g_s_xt"), sem("g_s_keep"),
                                             sem("g_s_logit"))
        s_shift, s_prob, s_mx, s_idx, s_cw = (sem("g_s_shift"), sem("g_s_prob"), sem("g_s_mx"), sem("g_s_idx"),
                                              sem("g_s_cw"))
        s_hs, s_hst, s_hsc, s_xg = sem("g_s_hs"), sem("g_s_hst"), sem("g_s_hsc"), sem("f_s_xg")
        s_a, s_b, s_sa, s_hh = sem("f_s_a"), sem("f_s_b"), sem("f_s_sa"), sem("f_s_hh")
        s_down, s_accc, s_back = sem("f_s_down"), sem("f_s_accc"), sem("f_s_back")
        s_gated, s_x, s_out = sem("f_s_gated"), sem("f_s_x"), sem("f_s_out")
        block = ctx.enter_context(nc.Block())

        def unit(i, b, n):
            return i * (BATCH * U) + (b * U + n)

        def group(i, b):
            return i * BATCH + b

        def following(i, b):
            return (i, 1) if b == 0 else (i + 1, 0)

        @block.tensor
        def _(pe):
            pe.wait_ge(s_gate, 16)
            for g in range(NG):
                pe.wait_ge(s_h, (g + 1) * TPG)
                for k in range(TPG):
                    last = pe.transpose(bank[g][:, k * P:(k + 1) * P], h_all[:, g * TPG + k, :], cst("ident"))
                last.then_inc(s_xt, 1)
            for g in range(NG):
                pe.wait_ge(s_keep, g + 1)
                for c in range(g * TPG, (g + 1) * TPG):
                    last = pe.matmul(bank[4][:, c * E:(c + 1) * E], xT_all[:, c, :], gate[:, :], start=True, stop=True)
            last.then_inc(s_logit, 1)
            pe.wait_ge(s_shift, 1)
            pe.sem_inc(s_sa, 2)
            pe.sem_inc(s_hh, 2)
            pe.sem_inc(s_accc, 2)
            pe.sem_inc(s_gated, 2)
            pe.sem_inc(s_hsc, 1)

            def prepare(i, b, k):
                pe.wait_ge(s_hs, group(i, b) * TPG + (k + 1))
                pe.wait_ge(s_hsc, group(i, b) * TPG + (k + 1))
                for e in range(E):
                    last = pe.transpose(scaled[:, e * P:(e + 1) * P], hs[k % 2][:, e, :], cst("ident"))
                last.then_inc(s_hst, 1)

            for k in range(TPG):
                prepare(0, 0, k)
            pe.wait_ge(s_weights, 16 * (2 + 2 * E))
            with pe.Fori(0, ROUNDS) as i:
                for b in range(BATCH):
                    pe.wait_ge(s_xg, group(i, b) + 1)
                    pe.wait_ge(s_hsc, group(i, b) * TPG + (TPG + 1))

                    def up(dst, w, src, e, f):
                        if f is not None:
                            return pe.matmul(dst[:, :], w[:, e, f * P:(f + 1) * P], src(e), start=True, stop=True)
                        for k in range(2):
                            last = pe.matmul(dst[k * TAIL1:(k + 1) * TAIL1, :], w[:, e + k, FULL1 * P:F1], src(e + k),
                                             start=True, stop=True, tile_position=(0, k * TAIL1))
                        return last

                    def down(n):
                        e, f = units[n]
                        w = W["w2"][:, e, f, :] if f is not None else W["w2_tail"][:, e // 2, :]
                        pe.wait_ge(s_hh, unit(i, b, n + 3))
                        pe.matmul(acc[b][:, :], w, hh[n % 2][:, :], start=(n == 0), stop=(n == U - 1))\
                            .then_inc(s_down, 1)

                    for n, (e, f) in enumerate(units):
                        pe.wait_ge(s_sa, unit(i, b, n + 1))
                        up(up_a[n % 2], W["w1"], lambda e: xg[b][:, 0, :], e, f).then_inc(s_a, 1)
                        pe.wait_ge(s_hh, unit(i, b, n + 1))
                        up(up_b[n % 2], W["w3"], lambda e: xg[b][:, 1 + e, :], e, f).then_inc(s_b, 1)
                        if n == 0:
                            pe.wait_ge(s_accc, group(i, b) + 1)
                        else:
                            down(n - 1)
                        if n in prepare_at:
                            prepare(*following(i, b), prepare_at[n])
                    down(U - 1)
                    pe.wait_ge(s_accc, group(i, b) + 3)
                    pe.wait_ge(s_gated, group(i, b) + 2)
                    for k in range(TPG):
                        last = pe.transpose(back[:, k * P:(k + 1) * P], oT[b][:, k * P:(k + 1) * P], cst("ident"))
                    last.then_inc(s_back, 1)

        @block.scalar
        def _(act):
            for g in range(NG):
                act.wait_ge(s_xt, g + 1)
                act.activation(xT_all[:, g * TPG:(g + 1) * TPG, :], bank[g][:, :].rearrange("p (k n) -> p k n", k=TPG),
                               ACT.Copy).then_inc(s_keep, 1)
            act.wait_ge(s_pad, 1)
            act.wait_ge(s_shift, 1)
            act.activation(prob[:, :, 0:E], shifted[:, :, :], ACT.Exp).then_inc(s_prob, 1)

            def prepare(i, b, k):
                act.wait_ge(s_hst, group(i, b) * TPG + (k + 3))
                act.activation(xg[b][:, 1:, k * P:(k + 1) * P], scaled.rearrange("p (e n) -> p e n", e=E),
                               ACT.Copy).then_inc(s_hsc, 1)

            for k in range(TPG):
                prepare(0, 0, k)
            act.sem_inc(s_down, 2)
            with act.Fori(0, ROUNDS) as i:
                for b in range(BATCH):
                    for n in range(U):
                        act.wait_ge(s_a, unit(i, b, n + 1))
                        act.wait_ge(s_hh, unit(i, b, n + 1))
                        act.activation(sa[n % 2][:, :], up_a[n % 2][:, :], ACT.Silu).then_inc(s_sa, 1)
                        if n in prepare_at:
                            prepare(*following(i, b), prepare_at[n])
                    act.wait_ge(s_down, unit(i, b, U + 2))
                    act.activation(oT[b][:, :], acc[b][:, :], ACT.Copy).then_inc(s_accc, 1)

        @block.vector
        def _(dve):
            for g in range(NG):
                tiles = range(g * TPG, (g + 1) * TPG)
                for c in tiles:
                    dve.bn_stats(st[:, c, :], x_sb[:, c, :]).then_inc(s_st, 1)
                dve.wait_ge(s_st, (g + 1) * TPG)
                for c in tiles:
                    dve.bn_aggr(mv[:, c, :], st[:, c, :]).then_inc(s_mv, 1)
            dve.wait_ge(s_mv, TILES)
            for c in range(TILES):
                dve.scalar_tensor_tensor(out=h_all[:, c, :], in0=x_sb[:, c, :], scalar=mv[:, c, 0:1],
                                         in1=sbw[:, 1, c // CHUNKS, :], op0=ALU.subtract,
                                         op1=ALU.mult).then_inc(s_mod, 1)
            dve.wait_ge(s_rstd, 2 * NG)
            for c in range(TILES):
                dve.wait_ge(s_mod, c + 1)
                dve.scalar_tensor_tensor(out=h_all[:, c, :], in0=h_all[:, c, :], scalar=rstd[:, c:c + 1],
                                         in1=sbw[:, 0, c // CHUNKS, :], op0=ALU.mult, op1=ALU.add).then_inc(s_h, 1)
            dve.memset(prob[:, :, :], -1.0).then_inc(s_pad, 1)
            logits = bank[4][:, 0:TILES * E].rearrange("p (c e) -> p c e", e=E)
            dve.wait_ge(s_logit, 1)
            dve.tensor_reduce(best[:, :], logits, AX.X, ALU.max).then_inc(s_cw, 1)
            dve.wait_ge(s_cw, 1)
            dve.tensor_tensor(shifted[:, :, :], logits, best[:, :, None].to_broadcast([P, TILES, E]),
                              ALU.subtract).then_inc(s_shift, 1)
            dve.wait_ge(s_prob, 1)
            for c in range(TILES):
                dve.max(mx[:, c, :], prob[:, c, :]).then_inc(s_mx, 1)
            for c in range(TILES):
                dve.wait_ge(s_mx, c + 1)
                dve.max_index(idx[:, c, :], mx[:, c, :], prob[:, c, :]).then_inc(s_idx, 1)
            dve.tensor_tensor(den[:, :], mx[:, :, 0], mx[:, :, 1], ALU.add).then_inc(s_cw, 1)
            dve.wait_ge(s_cw, 2)
            dve.reciprocal(den[:, :], den[:, :]).then_inc(s_cw, 1)
            dve.wait_ge(s_idx, TILES)
            dve.tensor_copy(idf[:, :, :], idx[:, :, 0:2]).then_inc(s_cw, 1)
            dve.wait_ge(s_cw, 4)
            experts = cst("iota16")[:, None, 0:E].to_broadcast([P, TILES, E])
            for k in range(2):
                dve.tensor_tensor(cw[:, k], experts, idf[:, :, k:k + 1].to_broadcast([P, TILES, E]),
                                  ALU.is_equal).then_inc(s_cw, 1)
            for k in range(2):
                dve.wait_ge(s_cw, 5 + k)
                dve.tensor_tensor(cw[:, k], cw[:, k], mx[:, :, k:k + 1].to_broadcast([P, TILES, E]),
                                  ALU.mult).then_inc(s_cw, 1)
            dve.wait_ge(s_cw, 8)
            dve.tensor_tensor(cw[:, 0], cw[:, 0], cw[:, 1], ALU.add).then_inc(s_cw, 1)
            dve.wait_ge(s_cw, 9)
            dve.tensor_tensor(cw[:, 0], cw[:, 0], den[:, :, None].to_broadcast([P, TILES, E]),
                              ALU.mult).then_inc(s_cw, 1)
            with dve.Fori(0, ROUNDS) as i:
                for b in range(BATCH):
                    for n in range(U):
                        dve.wait_ge(s_sa, unit(i, b, n + 3))
                        dve.wait_ge(s_b, unit(i, b, n + 1))
                        dve.wait_ge(s_down, unit(i, b, n + 1))
                        dve.tensor_tensor(hh[n % 2][:, :], sa[n % 2][:, :], up_b[n % 2][:, :], ALU.mult)\
                            .then_inc(s_hh, 1)
                    dve.wait_ge(s_back, group(i, b) + 1)
                    dve.wait_ge(s_x, group(i, b) + 1)
                    dve.tensor_tensor(gated[b][:, :, :], back.rearrange("p (k n) -> p k n", k=TPG),
                                      mod_row[:, 1, 1, b, None, :].to_broadcast([P, TPG, C]), ALU.mult)\
                        .then_inc(s_gated, 1)

        @block.gpsimd
        def _(pool):
            for g in range(NG):
                part = slice(g * TPG, (g + 1) * TPG)
                pool.wait_ge(s_mv, (g + 1) * TPG)
                pool.tensor_scalar(rstd[:, part], mv[:, part, 1], LN_EPS, None, ALU.add).then_inc(s_rstd, 1)
                pool.wait_ge(s_rstd, 2 * g + 1)
                pool.tensor_tensor(rstd[:, part], rstd[:, part], eps_pow[:, 0:TPG], ALU.pow).then_inc(s_rstd, 1)
            pool.wait_ge(s_keep, NG)
            pool.wait_ge(s_h, TILES)
            pool.wait_ge(s_cw, 10)
            pool.sem_inc(s_hst, 2)

            def prepare(i, b):
                at = i * TPG + b * CHUNKS
                for k in range(TPG):
                    pool.wait_ge(s_hst, group(i, b) * TPG + (k + 1))
                    pool.tensor_tensor(hs[k % 2][:, :, :],
                                       h_all[:, bass.ds(at + k, 1), :].to_broadcast([P, E, C]),
                                       cw[:, 0, bass.ds(at + k, 1), :].rearrange("p k e -> p e k")
                                       .to_broadcast([P, E, C]), ALU.mult).then_inc(s_hs, 1)
                pool.tensor_copy(xg[b][:, 0, :].rearrange("p (k n) -> p k n", k=TPG),
                                 xT_all[:, bass.ds(at, TPG), :]).then_inc(s_xg, 1)

            prepare(0, 0)
            pool.sem_inc(s_x, 2)
            with pool.Fori(0, ROUNDS) as i:
                for b in range(BATCH):
                    prepare(*following(i, b))
                    pool.wait_ge(s_gated, group(i, b) + 3)
                    xs = x_sb[:, bass.ds(i * TPG + b * CHUNKS, TPG), :]
                    pool.tensor_tensor(xs, xs, gated[b][:, :, :], ALU.add).then_inc(s_x, 1)

        @block.sync
        def _(sp):
            sp.dma_start(gate[:, :], t["gate_cols"]).then_inc(s_gate, 16)
            with sp.Fori(0, ROUNDS) as i:
                for b in range(BATCH):
                    sp.wait_ge(s_x, group(i, b) + 3)
                    sp.dma_start(out[b].rearrange("(c p) n -> p c n", p=P)[:, bass.ds(i * TPG, TPG), :],
                                 x_sb[:, bass.ds(i * TPG + b * CHUNKS, TPG), :]).then_inc(s_out, 16)
            sp.wait_ge(s_out, 16 * NG)


def kernel(**inputs):
    import concourse.bacc as _bacc
    from concourse.bass_utils import run_bass_kernel_spmd as _run

    a = {k: np.asarray(v) for k, v in inputs.items()}
    A = {n: a["L0_attn_" + n] for n in ("miu_x", "lambda_", "A_lora", "B_lora", "td_miu", "td_A", "td_B", "u",
                                        "Wr", "Wk", "Wv", "Wg", "Wo", "gn_gamma", "gn_beta")}
    b_rows = np.zeros((MIXES, P, C), np.float32)
    for f in range(4):
        b_rows[f, f * LORA:(f + 1) * LORA] = A["B_lora"][f]
    b_rows[4, 0:LORA] = A["B_lora"][4]
    host = {
        "const": shape_constants()[1],
        "L0_attn_x": a["L0_attn_x"],
        "c_cols": np.stack([a["L0_c"].T, a["L1_c"].T], axis=1),
        "wmod": np.stack([a["L0_wmod"], a["L1_wmod"]]),
        "miu_col": A["miu_x"].reshape(C, 1),
        "lambda_cols": A["lambda_"].reshape(MIXES, C).T,
        "td_miu_col": A["td_miu"].reshape(C, 1),
        "u_col": A["u"].reshape(C, 1),
        "gn_gamma_col": A["gn_gamma"].reshape(C, 1),
        "gn_beta_col": A["gn_beta"].reshape(C, 1),
        "L0_attn_A_lora": A["A_lora"],
        "b_lora_rows": b_rows,
        "L0_attn_td_A": A["td_A"],
        "L0_attn_td_B": A["td_B"],
        "rwkv_wT": np.stack([A[n].T for n in ("Wk", "Wv", "Wr", "Wg", "Wo")]),
    }
    w1, b1, w2 = a["L0_ffn_w1"], a["L0_ffn_b1"], a["L0_ffn_w2"]
    host["experts0"] = np.concatenate([w1, w2.reshape(E0, 2, P, C).transpose(0, 2, 1, 3).reshape(E0, P, 2 * C),
                                       b1.reshape(E0, 2, P).transpose(0, 2, 1), a["L0_ffn_b2"][:, :, None]], axis=2)
    host["L0_ffn_router_w"] = a["L0_ffn_router_w"]
    for n in ("Wq", "Wk", "Wv", "Wo"):
        host["L1_attn_" + n] = a["L1_attn_" + n]
    host["gate_cols"] = a["L1_ffn_gate_w"][:E1_LIVE].T
    for n in ("w1", "w3", "w2"):
        host["moe_" + n] = a["L1_ffn_" + n][:E1_LIVE]
    nc = _bacc.Bacc("TRN2", target_bir_lowering=False, num_devices=1)
    arrays, t = {}, {}
    for name, v in host.items():
        v = np.ascontiguousarray(v)
        arrays[f"in_{name}_dram"] = v
        t[name] = nc.dram_tensor(f"in_{name}_dram", v.shape, mybir.dt.from_np(v.dtype), kind="ExternalInput").ap()
    for name in ("slots_in", "slots_out"):
        t[name] = nc.dram_tensor(name, (SLOTS, C), F32, kind="Internal").ap()
    out = nc.dram_tensor("out_0_dram", (BATCH, SEQ, C), F32, kind="ExternalOutput").ap()
    bass_adaln_stack(nc, t, out)
    r = _run(nc, [arrays], core_ids=[0])
    return r.results[0]["out_0_dram"]
```

```python
from contextlib import ExitStack

import numpy as np

import concourse.bass as bass
from concourse import mybir

F32 = mybir.dt.float32
I32 = mybir.dt.int32
U32 = mybir.dt.uint32
ALU = mybir.AluOpType
ACT = mybir.ActivationFunctionType
AX = mybir.AxisListType

P = 128
BATCH, SEQ, C = 2, 1024, 128
CHUNKS = SEQ // P
TILES = BATCH * CHUNKS
LN_EPS = 1e-5

RW_HEADS, RW_DIM = 2, 64
LORA = 32
MIXES = 5
TD_RANK = 64
LEAF = 32
GN_EPS = 1e-5 * RW_HEADS
LEVELS = 7

E0, F0 = 16, 256
SLOT_TILES = 32
SLOTS = SLOT_TILES * P
W0 = 2 * F0 + 3

HL_HEADS, HL_DIM = 16, 32
GROUPS = HL_HEADS * HL_DIM // P
HPG = P // HL_DIM
GAMMA = 0.99

E1, E1_LIVE, F1 = 8, 4, 704
FULL1 = F1 // P
TAIL1 = F1 - FULL1 * P


def shape_constants():
    i = np.arange(P)
    row, col = i[:, None], i[None, :]
    parts = {}
    parts["ident"] = (row == col)
    parts["before"] = (row < col)
    parts["ones"] = np.ones((P, P))
    parts["head2"] = (row // RW_DIM == col // RW_DIM)
    parts["head4"] = (row // HL_DIM == col // HL_DIM)
    lag = (col - row).astype(np.float64)
    parts["decay_incl"] = np.where(lag >= 0, GAMMA ** np.maximum(lag, 0), 0)
    parts["decay_excl"] = np.where(lag > 0, GAMMA ** np.maximum(lag, 0), 0)
    parts["decay_row"] = np.broadcast_to(GAMMA ** (col + 1.0), (P, P))
    parts["decay_col"] = GAMMA ** (P - 1.0 - row)
    s, t = row % LEAF, np.arange(LEAF)[None, :]
    leaf = [(s // 2 == t // 2) & (s <= t)]
    for m in (2, 4, 8, 16):
        leaf.append((s // (2 * m) == t // (2 * m)) & (s % (2 * m) < m) & (t % (2 * m) >= m))
    parts["leaf"] = np.concatenate(leaf, axis=1)
    parts["iota16"] = np.broadcast_to(np.arange(E0), (P, E0))
    parts["iota32"] = np.broadcast_to(np.arange(SLOT_TILES), (P, SLOT_TILES))
    parts["restart"] = np.broadcast_to(np.arange(E0 * TILES) % TILES != 0, (P, E0 * TILES))
    at, cols = {}, 0
    for name, a in parts.items():
        at[name] = (cols, cols + a.shape[1])
        cols += a.shape[1]
    return at, np.concatenate([np.asarray(a, np.float32) for a in parts.values()], axis=1)


CONST_AT, _ = shape_constants()
CONST_COLS = max(b for _, b in CONST_AT.values())


def bass_adaln_stack(nc, t, out):
    ctx = ExitStack()
    with ctx:
        def sb(name, shape, dt=F32):
            return ctx.enter_context(nc.sbuf_tensor(name, shape, dt))

        def sem(name):
            return ctx.enter_context(nc.semaphore(name))

        const = sb("const", [P, CONST_COLS])

        def cst(name):
            a, b = CONST_AT[name]
            return const[:, a:b]

        x_sb = sb("x_sb", [P, TILES, C])
        x_bc = x_sb[:, :, :].rearrange("p (b c) n -> p b c n", b=BATCH)
        eps_pow = sb("eps_pow", [P, 16])
        mod_col = sb("mod_col", [P, 2, 4, BATCH])
        mod_row = sb("mod_row", [P, 2, 2, BATCH, C])
        sbw = sb("sbw", [P, 2, 2, BATCH, C])

        bank = [ctx.enter_context(nc.psum_tensor(f"bank{i}", [P, 512], F32)) for i in range(4)]
        bank.append(None)
        pair = ctx.enter_context(nc.psum_tensor("pair", [P, 1024], F32))
        bank[4] = ctx.enter_context(nc.psum_tensor("bank6", [P, 512], F32))
        bank.append(ctx.enter_context(nc.psum_tensor("bank7", [P, 512], F32)))

        W1 = {n: sb(f"hla_w{n}", [P, HL_HEADS * HL_DIM]) for n in "qkv"}
        W1["o"] = sb("hla_wo", [P, GROUPS, C])
        s_w1 = sem("s_w1")
        W2 = {"w1": sb("moe_w1", [P, E1_LIVE, F1]), "w3": sb("moe_w3", [P, E1_LIVE, F1]),
              "w2": sb("moe_w2", [P, E1_LIVE, FULL1, C]), "w2_tail": sb("moe_w2_tail", [P, E1_LIVE // 2, C])}
        s_w2 = sem("s_w2")
        s_w0 = sem("s_w0")
        mv0 = sb("mv0", [P, TILES, 2])
        rstd0 = sb("rstd0", [P, TILES])
        h_all = sb("h_all", [P, TILES, C])
        W0T = {n: sb(n, shape) for n, (shape, _) in rwkv_parameters(t).items()}
        with nc.cleanup_on_exit():
            setup_phase(nc, t, const, x_sb, eps_pow, mod_col, mod_row, sbw, bank, cst, W0T, s_w0, mv0, rstd0)
        with nc.cleanup_on_exit():
            rwkv_phase(nc, t, x_bc, eps_pow, mod_col, mod_row, bank, pair, cst, W0T, s_w0, mv0, rstd0, W1, s_w1, W2,
                       s_w2, sbw[:, 0], h_all)
        halves = [pair[:, 0:512], pair[:, 512:1024]]
        with nc.sbuf_tensor("hT_all", [P, TILES, P], F32) as hT_all:
            with nc.cleanup_on_exit():
                expert_phase(nc, t, x_sb, h_all, eps_pow, mod_row, mod_col, bank + halves, cst, hT_all)
            with nc.cleanup_on_exit():
                hla_phase(nc, x_bc, mod_row, bank, pair, cst, hT_all, W1, s_w1)
        with nc.cleanup_on_exit():
            swiglu_phase(nc, t, x_sb, eps_pow, sbw[:, 1], mod_row, bank, pair, cst, W2, s_w2, out)


def rwkv_parameters(t):
    return {
        "lamb": ([P, MIXES], t["lambda_cols"]),
        "miu": ([P, 1], t["miu_col"]),
        "td_miu": ([P, 1], t["td_miu_col"]),
        "bonus": ([P, 1], t["u_col"]),
        "gamma": ([P, 1], t["gn_gamma_col"]),
        "beta": ([P, 1], t["gn_beta_col"]),
        "a_lora": ([P, MIXES * LORA], t["L0_attn_A_lora"]),
        "b_pad": ([P, MIXES, C], t["b_lora_rows"].rearrange("f k n -> k f n")),
        "td_a": ([P, TD_RANK], t["L0_attn_td_A"]),
        "td_b": ([TD_RANK, C], t["L0_attn_td_B"]),
        "wT": ([P, 5, C], t["rwkv_wT"].rearrange("w k n -> k w n")),
    }


def setup_phase(nc, t, const, x_sb, eps_pow, mod_col, mod_row, sbw, bank, cst, W0T, s_w0, mv, rstd):
    with ExitStack() as ctx:
        def sb(name, shape, dt=F32):
            return ctx.enter_context(nc.sbuf_tensor(name, shape, dt))

        def sem(name):
            return nc.alloc_semaphore(name)

        cT = sb("cT", [P, 2, BATCH])
        eT = sb("eT", [P, 2, BATCH])
        silu_c = sb("silu_c", [P, 2, BATCH])
        wmod = sb("wmod", [P, 2, 6 * C])
        absr = sb("absr", [P, 2, 2, BATCH, C])
        sgn = sb("sgn", [P, 2, 2, BATCH, C])
        s_const = sem("s_const")
        s_x = sem("s_x")
        s_c = sem("s_c")
        s_wmod = sem("s_wmod")
        s_exp = sem("s_exp")
        s_silu = sem("s_silu")
        s_cols = sem("s_cols")
        s_rows = sem("s_rows")
        s_colv = sem("s_colv")
        s_clamp = sem("s_clamp")
        s_set = sem("s_set")
        s_stat, s_var, s_rstd = sem("s_stat"), sem("s_var"), sem("s_rstd")
        stats = sb("stats", [P, TILES, 6])
        block = ctx.enter_context(nc.Block())

        @block.sync
        def _(sp):
            sp.dma_start(cT[:, :, :], t["c_cols"]).then_inc(s_c, 16)
            sp.dma_start(wmod[:, :, :], t["wmod"].rearrange("l k n -> k l n")).then_inc(s_wmod, 16)
            sp.dma_start(const[:, :], t["const"]).then_inc(s_const, 16)
            for b in range(BATCH):
                sp.dma_start(x_sb[:, b * CHUNKS:(b + 1) * CHUNKS, :],
                             t["L0_attn_x"][b].rearrange("(c p) n -> p c n", p=P)).then_inc(s_x, 16)
            for n, (_, source) in rwkv_parameters(t).items():
                sp.dma_start(W0T[n][:], source).then_inc(s_w0, 16)
            sp.wait_ge(s_const, 16)
            sp.wait_ge(s_x, 32)

        @block.gpsimd
        def _(pool):
            pool.memset(eps_pow[:, :], -0.5).then_inc(s_set, 1)
            pool.wait_ge(s_set, 1)
            pool.wait_ge(s_var, TILES)
            pool.tensor_scalar(rstd[:, :], mv[:, :, 1], LN_EPS, None, ALU.add).then_inc(s_rstd, 1)
            pool.wait_ge(s_rstd, 1)
            pool.tensor_tensor(rstd[:, :], rstd[:, :], eps_pow[:, 0:TILES], ALU.pow).then_inc(s_rstd, 1)

        @block.scalar
        def _(act):
            act.wait_ge(s_c, 16)
            act.activation(eT[:, :, :], cT[:, :, :], ACT.Exp, scale=-1.0).then_inc(s_exp, 1)

        @block.vector
        def _(dve):
            dve.wait_ge(s_exp, 1)
            dve.tensor_scalar(eT[:, :, :], eT[:, :, :], 1.0, None, ALU.add).then_inc(s_silu, 1)
            dve.wait_ge(s_silu, 1)
            dve.reciprocal(eT[:, :, :], eT[:, :, :]).then_inc(s_silu, 1)
            dve.wait_ge(s_silu, 2)
            dve.tensor_tensor(silu_c[:, :, :], eT[:, :, :], cT[:, :, :], ALU.mult).then_inc(s_silu, 1)
            dve.wait_ge(s_x, 32)
            for c in range(TILES):
                dve.bn_stats(stats[:, c, :], x_sb[:, c, :]).then_inc(s_stat, 1)
            dve.wait_ge(s_stat, TILES)
            for c in range(TILES):
                dve.bn_aggr(mv[:, c, :], stats[:, c, :]).then_inc(s_var, 1)
            dve.wait_ge(s_cols, 1)
            for n, plus in enumerate((0.0, 1.0, 0.0, 1.0)):
                dve.tensor_scalar(mod_col[:, :, n, :],
                                  bank[0][:, 0:16].rearrange("p (l n b) -> p l n b", l=2, n=4)[:, :, n, :],
                                  plus, None, ALU.add).then_inc(s_colv, 1)
            for layer in range(2):
                dve.wait_ge(s_rows, layer + 1)
                rows = bank[1 + layer][:, :].rearrange("p (g b n) -> p g b n", g=2, b=BATCH)
                flat_rows = bank[1 + layer][:, :]
                neg = absr[:, layer].rearrange("p g b n -> p (g b n)")
                dve.tensor_scalar(neg, flat_rows, -1.0, None, ALU.mult).then_inc(s_clamp, 1)
                dve.tensor_scalar(sgn[:, layer], rows, 0.0, 2.0, ALU.is_ge, ALU.mult).then_inc(s_clamp, 1)
                dve.wait_ge(s_clamp, 3 * layer + 1)
                dve.scalar_tensor_tensor(out=neg, in0=neg, scalar=0.25, in1=flat_rows, op0=ALU.max,
                                         op1=ALU.max).then_inc(s_clamp, 1)
            dve.wait_ge(s_clamp, 6)
            dve.scalar_tensor_tensor(out=mod_row[:, :, :, :, :].rearrange("p l g b n -> p (l g b n)"),
                                     in0=sgn[:, :, :, :, :].rearrange("p l g b n -> p (l g b n)"), scalar=-1.0,
                                     in1=absr[:, :, :, :, :].rearrange("p l g b n -> p (l g b n)"),
                                     op0=ALU.add, op1=ALU.mult).then_inc(s_clamp, 1)
            for layer in range(2):
                srows = bank[3 + layer][:, :].rearrange("p (k b n) -> p k b n", k=2, b=BATCH)
                dve.tensor_scalar(sbw[:, layer, 0], srows[:, 0], 0.0, None, ALU.add).then_inc(s_clamp, 1)
                dve.tensor_scalar(sbw[:, layer, 1], srows[:, 1], 1.0, None, ALU.add).then_inc(s_clamp, 1)
            dve.wait_ge(s_clamp, 11)
            dve.wait_ge(s_colv, 4)

        @block.tensor
        def _(pe):
            pe.wait_ge(s_silu, 3)
            pe.wait_ge(s_wmod, 16)
            for layer in range(2):
                for n, part in enumerate((0, 1, 3, 4)):
                    at = (layer * 4 + n) * 2
                    last = pe.matmul(bank[0][:, at:at + 2], wmod[:, layer, part * C:(part + 1) * C],
                                     silu_c[:, layer, :], start=True, stop=True)
            last.then_inc(s_cols, 1)
            for layer in range(2):
                for g, part in enumerate((2, 5)):
                    for b in range(BATCH):
                        at = (g * 2 + b) * C
                        pe.matmul(bank[1 + layer][:, at:at + C], silu_c[:, layer, b:b + 1].to_broadcast([P, P]),
                                  wmod[:, layer, part * C:(part + 1) * C], start=True, stop=True)
                for k, part in enumerate((3, 4)):
                    for b in range(BATCH):
                        at = (k * 2 + b) * C
                        last = pe.matmul(bank[3 + layer][:, at:at + C], silu_c[:, layer, b:b + 1].to_broadcast([P, P]),
                                         wmod[:, layer, part * C:(part + 1) * C], start=True, stop=True)
                last.then_inc(s_rows, 1)


def rwkv_phase(nc, t, x_bc, eps_pow, mod_col, mod_row, bank, pair, cst, W0T, s_w0, mv, rstd, W1, s_w1, W2, s_w2, sbw,
               h_all):
    with ExitStack() as ctx:
        def sb(name, shape, dt=F32):
            return ctx.enter_context(nc.sbuf_tensor(name, shape, dt))

        def sem(name):
            return nc.alloc_semaphore(name)

        N = BATCH * P
        lamb, miu, td_miu, bonus, gamma, beta = (W0T[n] for n in ("lamb", "miu", "td_miu", "bonus", "gamma", "beta"))
        a_lora, b_pad, td_a, td_b, wT = (W0T[n] for n in ("a_lora", "b_pad", "td_a", "td_b", "wT"))
        xn = sb("xn", [P, BATCH, C])
        hT = sb("hT", [P, BATCH, P + 1])
        dxa = sb("dxa", [P, BATCH, P])
        xm = sb("xm", [P, BATCH, P])
        lh = sb("lh", [P, N])
        lh4 = sb("lh4", [LORA, N])
        xx = sb("xx", [P, MIXES, BATCH, P])
        tw = sb("tw", [TD_RANK, N])
        ew = sb("ew", [P, N])
        rl1 = [sb(f"rl{m}", [P, N]) for m in range(1, LEVELS + 1)]
        kl1 = [sb(f"kl{m}", [P, N]) for m in range(1, LEVELS + 1)]
        tot1 = [sb(f"tot{m}", [P, N >> m]) for m in range(1, LEVELS + 1)]
        rls = [[sb(f"rl0_{q}", [P, N])] + rl1 for q in range(2)]
        kls = [[sb(f"kl0_{q}", [P, N])] + kl1 for q in range(2)]
        tots = [[sb(f"tot0_{q}", [P, N])] + tot1 for q in range(2)]
        rd = sb("rd", [P, N])
        kd = sb("kd", [P, N])
        vs = [sb(f"v_sb{q}", [P, BATCH, C]) for q in range(2)]
        eg = sb("eg", [P, N])
        gT = sb("gT", [P, N])
        prod = sb("prod", [P, 4, 160])
        leafs = sb("leafs", [P, 4, LEAF])
        att = sb("att", [P, 4, P])
        ktm = sb("ktm", [P, BATCH, P])
        state = sb("state", [P, BATCH, P])
        kv = sb("kv", [P, BATCH, P])
        gst = sb("gst", [P, 4, 6])
        gmv = sb("gmv", [P, 4, 2])
        grs = sb("grs", [P, 4])
        yn = sb("yn", [P, BATCH, C])
        zT = sb("zT", [P, BATCH, P])
        gated = sb("gated", [P, BATCH, C])

        s_zero = sem("s_zero")
        s_xn = sem("s_xn")
        s_xt = sem("s_xt")
        s_ht = sem("s_ht")
        s_dxa = sem("s_dxa")
        s_xm = sem("s_xm")
        s_lora = sem("s_lora")
        s_lh = sem("s_lh")
        s_mix = sem("s_mix")
        s_scaled = sem("s_scaled")
        s_xx = sem("s_xx")
        s_proj = sem("s_proj")
        s_td = sem("s_td")
        s_tw = sem("s_tw")
        s_ew = sem("s_ew")
        s_evac = sem("s_evac")
        s_diag = sem("s_diag")
        s_r = sem("s_r")
        s_k = sem("s_k")
        s_tot = sem("s_tot")
        s_rc = sem("s_rc")
        s_leafmm = sem("s_leafmm")
        s_prod = sem("s_prod")
        s_leaf = sem("s_leaf")
        s_att = sem("s_att")
        s_off = sem("s_off")
        s_ktT = sem("s_ktT")
        s_ktm = sem("s_ktm")
        s_kv = sem("s_kv")
        s_state = sem("s_state")
        s_gn = sem("s_gn")
        s_grs = sem("s_grs")
        s_yn = sem("s_yn")
        s_zt = sem("s_zt")
        s_z = sem("s_z")
        s_zg = sem("s_zg")
        s_o = sem("s_o")
        s_gate = sem("s_gate")
        s_gated = sem("s_gated")
        s_gT = sem("s_gT")
        s_iter = sem("s_iter")
        h_bc = h_all[:, :, :].rearrange("p (b c) n -> p b c n", b=BATCH)
        nst = sb("nst", [P, BATCH, 6])
        nmv = sb("nmv", [P, BATCH, 2])
        nrstd = sb("nrstd", [P, BATCH])
        s_nst, s_nrstd, s_nmod = sem("s_nst"), sem("s_nrstd"), sem("s_nmod")
        block = ctx.enter_context(nc.Block())
        flat = "p b n -> p (b n)"
        lv = [mm for mm in range(LEVELS)]

        def halves(a, m):
            return a[:, :].rearrange("p (k h e) -> p k h e", h=2, e=1 << m)

        def per(a, m):
            return a[:, :].rearrange("p (k h) -> p k h", h=2)

        @block.sync
        def _(sp):
            for n in "qkv":
                sp.dma_start(W1[n][:, :], t["L1_attn_W" + n]).then_inc(s_w1, 16)
            sp.dma_start(W1["o"][:, :, :], t["L1_attn_Wo"].rearrange("(j p) n -> p j n", p=P)).then_inc(s_w1, 16)
            for n in ("w1", "w3"):
                sp.dma_start(W2[n][:, :, :], t["moe_" + n].rearrange("e k n -> k e n")).then_inc(s_w2, 16)
            for e in range(E1_LIVE):
                sp.dma_start(W2["w2"][:, e, :, :], t["moe_w2"][e, 0:FULL1 * P, :].rearrange("(f p) n -> p f n", p=P))\
                    .then_inc(s_w2, 16)
                rows = slice((e % 2) * TAIL1, (e % 2 + 1) * TAIL1)
                sp.dma_start(W2["w2_tail"][rows, e // 2, :], t["moe_w2"][e, FULL1 * P:F1, :]).then_inc(s_w2, 16)

        LOADS = 16 * len(W0T)

        def start(eng, i):
            if not isinstance(i, int) or i:
                eng.wait_ge(s_state, i * 3)
            eng.wait_ge(s_gT, i + 1)

        def steps(eng, front, step, tail):
            front()
            step(0, 0, True, False)
            with eng.Fori(0, CHUNKS // 2 - 1) as j:
                step(j * 2 + 1, 1, True, True)
                step(j * 2 + 2, 0, True, True)
            step(CHUNKS - 1, 1, False, True)
            for part in tail:
                part(CHUNKS - 1, 1)

        @block.vector
        def _(dve):
            dve.wait_ge(s_w0, LOADS)
            dve.memset(state[:, :, :], 0.0).then_inc(s_zero, 1)
            dve.memset(att[:, :, :], 0.0).then_inc(s_zero, 1)
            dve.memset(hT[:, :, P:P + 1], 0.0).then_inc(s_zero, 1)
            dve.wait_ge(s_zero, 3)

            def norm(n):
                dve.tensor_copy(hT[:, :, 0:1], hT[:, :, P:P + 1]).then_inc(s_xn, 1)
                for b in range(BATCH):
                    dve.tensor_scalar(xn[:, b, :], x_bc[:, b, bass.ds(n, 1), :],
                                      mv[:, bass.ds(n + b * CHUNKS, 1), 0:1], rstd[:, bass.ds(n + b * CHUNKS, 1)],
                                      ALU.subtract, ALU.mult).then_inc(s_xn, 1)

            def lora_input(n):
                dve.wait_ge(s_dxa, n + 1)
                dve.scalar_tensor_tensor(out=xm[:, :, :], in0=dxa[:, :, :], scalar=miu[:, 0:1], in1=hT[:, :, 1:],
                                         op0=ALU.mult, op1=ALU.add).then_inc(s_xm, 1)

            def mix(n):
                for f in range(MIXES):
                    if f % 2 == 0:
                        dve.wait_ge(s_mix, n * 3 + (f // 2 + 1))
                    at = N if f == 4 else f % 2 * N
                    src = bank[(2, 3, 0)[f // 2]][:, at:at + N].rearrange("p (b n) -> p b n", b=BATCH)
                    dve.scalar_tensor_tensor(out=xx[:, f], in0=src, scalar=lamb[:, f:f + 1], in1=dxa[:, :, :],
                                             op0=ALU.add, op1=ALU.mult).then_inc(s_scaled, 1)

            def gate(n):
                dve.tensor_scalar(eg[:, :], eg[:, :], 1.0, None, ALU.add).then_inc(s_gate, 1)
                dve.wait_ge(s_gate, n * 3 + 1)
                dve.reciprocal(eg[:, :], eg[:, :]).then_inc(s_gate, 1)
                dve.wait_ge(s_gate, n * 3 + 2)
                dve.tensor_tensor(gT[:, :], eg[:, :], bank[0][:, N:2 * N], ALU.mult).then_inc(s_gate, 1)

            def front():
                norm(0)
                lora_input(0)
                mix(0)

            y = bank[5][:, 0:N].rearrange("p (u n) -> p u n", u=4)

            def statistics(n, q):
                for u in range(4):
                    dve.bn_stats(gst[:, u, :], y[:, u, :]).then_inc(s_gn, 1)
                dve.wait_ge(s_gn, n * 8 + 4)
                dve.nop(nofuse=True)
                for u in range(4):
                    dve.bn_aggr(gmv[:, u, :], gst[:, u, :]).then_inc(s_gn, 1)

            def normalise(n, q):
                dve.wait_ge(s_grs, n * 2 + 2)
                for u in range(4):
                    dve.tensor_scalar(yn[:, u // 2, (u % 2) * RW_DIM:(u % 2 + 1) * RW_DIM], y[:, u, :], gmv[:, u, 0:1],
                                      grs[:, u:u + 1], ALU.subtract, ALU.mult).then_inc(s_yn, 1)

            def output(n, q):
                dve.wait_ge(s_o, n + 1)
                dve.wait_ge(s_iter, n + 1)
                dve.tensor_tensor(gated[:, :, :], bank[4][:, 0:N].rearrange("p (b n) -> p b n", b=BATCH),
                                  mod_row[:, 0, 0], ALU.mult).then_inc(s_gated, 1)

            def moe_input(n, q):
                dve.wait_ge(s_iter, n + 2)
                for b in range(BATCH):
                    dve.bn_stats(nst[:, b, :], x_bc[:, b, bass.ds(n, 1), :]).then_inc(s_nst, 1)
                dve.wait_ge(s_nst, n * 4 + 2)
                dve.nop(nofuse=True)
                for b in range(BATCH):
                    dve.bn_aggr(nmv[:, b, :], nst[:, b, :]).then_inc(s_nst, 1)
                dve.wait_ge(s_nst, n * 4 + 4)
                for b in range(BATCH):
                    dve.scalar_tensor_tensor(out=h_bc[:, b, bass.ds(n, 1), :], in0=x_bc[:, b, bass.ds(n, 1), :],
                                             scalar=nmv[:, b, 0:1], in1=sbw[:, 1, b:b + 1, :], op0=ALU.subtract,
                                             op1=ALU.mult).then_inc(s_nmod, 1)
                dve.wait_ge(s_nrstd, n * 2 + 2)
                dve.wait_ge(s_nmod, n * 4 + 2)
                for b in range(BATCH):
                    hn = h_bc[:, b, bass.ds(n, 1), :]
                    dve.scalar_tensor_tensor(out=hn, in0=hn, scalar=nrstd[:, b:b + 1], in1=sbw[:, 0, b:b + 1, :],
                                             op0=ALU.mult, op1=ALU.add).then_inc(s_nmod, 1)

            def step(i, q, prepare, tail):
                rl, kl, tot = rls[q], kls[q], tots[q]
                start(dve, i)
                if prepare:
                    norm(i + 1)
                if tail:
                    statistics(i - 1, 1 - q)
                rh, kh = halves(rl[0], 0), halves(kl[0], 0)
                dve.tensor_scalar(halves(rd, 0)[:, :, 0], rh[:, :, 0], bonus[:, 0:1], None, ALU.mult).then_inc(s_diag, 1)
                dve.tensor_copy(halves(rd, 0)[:, :, 1], rh[:, :, 1]).then_inc(s_diag, 1)
                dve.tensor_copy(halves(kd, 0)[:, :, 0], kh[:, :, 0]).then_inc(s_diag, 1)
                dve.tensor_scalar(halves(kd, 0)[:, :, 1], kh[:, :, 1], bonus[:, 0:1], None, ALU.mult).then_inc(s_diag, 1)
                for m in lv:
                    if m:
                        dve.wait_ge(s_tot, i * LEVELS + m)
                        dve.wait_ge(s_r, i * LEVELS + m)
                        dve.wait_ge(s_rc, i * 2 * LEVELS + 2 * m)
                    tp = per(tot[m], m)
                    dve.tensor_tensor(tot[m + 1][:, :], tp[:, :, 0], tp[:, :, 1], ALU.mult).then_inc(s_tot, 1)
                    dve.tensor_tensor(halves(rl[m + 1], m)[:, :, 1], halves(rl[m], m)[:, :, 1],
                                      tp[:, :, 0:1].to_broadcast([P, N >> (m + 1), 1 << m]), ALU.mult).then_inc(s_r, 1)
                    if tail and m == 0:
                        normalise(i - 1, 1 - q)
                    if prepare and m == 1:
                        lora_input(i + 1)
                    if m == 4:
                        if tail:
                            output(i - 1, 1 - q)
                            dve.wait_ge(s_zg, i)
                        gate(i)
                if prepare:
                    mix(i + 1)
                scores = pair[:, :].rearrange("p (u n) -> p u n", u=4)
                dve.wait_ge(s_leafmm, i + 1)
                dve.tensor_tensor(prod[:, :, :], scores[:, :, 0:160],
                                  cst("leaf")[:, None, :].to_broadcast([P, 4, 160]), ALU.mult).then_inc(s_prod, 1)
                dve.wait_ge(s_prod, i + 1)
                dve.tensor_reduce(leafs[:, :, :], prod[:, :, :].rearrange("p u (l n) -> p u n l", n=LEAF), AX.X,
                                  ALU.add).then_inc(s_leaf, 1)
                dve.wait_ge(s_leaf, i + 1)
                for k in range(4):
                    rows = slice(k * LEAF, (k + 1) * LEAF)
                    dve.tensor_copy(att[rows, :, rows], leafs[rows, :, :]).then_inc(s_att, 1)
                if tail:
                    moe_input(i - 1, 1 - q)
                dve.wait_ge(s_kv, i + 1)
                dve.tensor_tensor(kv[:, :, :], bank[5][:, N:2 * N].rearrange("p (b n) -> p b n", b=BATCH),
                                  cst("head2")[:, None, :].to_broadcast([P, BATCH, P]), ALU.mult).then_inc(s_state, 1)
                dve.wait_ge(s_state, i * 3 + 1)
                for b in range(BATCH):
                    dve.scalar_tensor_tensor(out=state[:, b, :], in0=state[:, b, :], scalar=tot[LEVELS][:, b:b + 1],
                                             in1=kv[:, b, :], op0=ALU.mult, op1=ALU.add).then_inc(s_state, 1)

            steps(dve, front, step, (statistics, normalise, output, moe_input))

        @block.gpsimd
        def _(pool):
            pool.sem_inc(s_iter, 1)
            def difference(n):
                pool.wait_ge(s_ht, n * 2 + 2)
                pool.wait_ge(s_xn, n * 3 + 1)
                pool.tensor_tensor(dxa[:, :, :], hT[:, :, 0:P], hT[:, :, 1:], ALU.subtract).then_inc(s_dxa, 1)

            def mix(n):
                for f in range(MIXES):
                    pool.wait_ge(s_scaled, n * MIXES + (f + 1))
                    pool.tensor_tensor(xx[:, f], xx[:, f], hT[:, :, 1:], ALU.add).then_inc(s_xx, 1)

            def front():
                difference(0)
                mix(0)

            def deviation(n, q):
                pool.wait_ge(s_gn, n * 8 + 8)
                pool.nop(nofuse=True)
                pool.tensor_scalar(grs[:, :], gmv[:, :, 1], GN_EPS, None, ALU.add).then_inc(s_grs, 1)
                pool.wait_ge(s_grs, n * 2 + 1)
                pool.tensor_tensor(grs[:, :], grs[:, :], eps_pow[:, 0:4], ALU.pow).then_inc(s_grs, 1)

            def gated_heads(n, q):
                pool.wait_ge(s_z, n + 1)
                pool.wait_ge(s_gate, n * 3 + 3)
                pool.tensor_tensor(zT[:, :, :], zT[:, :, :], gT[:, :].rearrange("p (b n) -> p b n", b=BATCH),
                                   ALU.mult).then_inc(s_zg, 1)

            def add(n, q):
                pool.wait_ge(s_gated, n + 1)
                pool.tensor_tensor(x_bc[:, :, bass.ds(n, 1), :], x_bc[:, :, bass.ds(n, 1), :],
                                   gated[:, :, None, :], ALU.add).then_inc(s_iter, 1)

            def moe_deviation(n, q):
                pool.wait_ge(s_nst, n * 4 + 4)
                pool.nop(nofuse=True)
                pool.tensor_scalar(nrstd[:, :], nmv[:, :, 1], LN_EPS, None, ALU.add).then_inc(s_nrstd, 1)
                pool.wait_ge(s_nrstd, n * 2 + 1)
                pool.tensor_tensor(nrstd[:, :], nrstd[:, :], eps_pow[:, 0:BATCH], ALU.pow).then_inc(s_nrstd, 1)

            def step(i, q, prepare, tail):
                kl, tot = kls[q], tots[q]
                start(pool, i)
                for m in lv:
                    if m:
                        pool.wait_ge(s_tot, i * LEVELS + m)
                        pool.wait_ge(s_k, i * LEVELS + m)
                        pool.wait_ge(s_rc, i * 2 * LEVELS + 2 * m)
                    pool.tensor_tensor(halves(kl[m + 1], m)[:, :, 0], halves(kl[m], m)[:, :, 0],
                                       per(tot[m], m)[:, :, 1:2].to_broadcast([P, N >> (m + 1), 1 << m]),
                                       ALU.mult).then_inc(s_k, 1)
                    if prepare and m == 1:
                        difference(i + 1)
                    if tail and m == 0:
                        deviation(i - 1, 1 - q)
                    if tail and m == 2:
                        gated_heads(i - 1, 1 - q)
                if tail:
                    add(i - 1, 1 - q)
                if prepare:
                    mix(i + 1)
                if tail:
                    moe_deviation(i - 1, 1 - q)

            steps(pool, front, step, (deviation, gated_heads, add, moe_deviation))
            pool.wait_ge(s_iter, CHUNKS + 1)

        @block.scalar
        def _(act):
            act.wait_ge(s_w0, LOADS)

            def modulate(n):
                act.wait_ge(s_xt, n + 1)
                act.wait_ge(s_xn, n * 3 + 1)
                for b in range(BATCH):
                    act.activation(hT[:, b, 1:], bank[1][:, b * P:(b + 1) * P], ACT.Identity,
                                   bias=mod_col[:, 0, 0, b:b + 1], scale=mod_col[:, 0, 1, b:b + 1]).then_inc(s_ht, 1)

            def lora_tanh(n):
                act.wait_ge(s_lora, n + 1)
                act.activation(lh[:, :], bank[1][:, 0:N], ACT.Tanh).then_inc(s_lh, 1)
                act.activation(lh4[:, :], bank[1][0:LORA, N:2 * N], ACT.Tanh).then_inc(s_lh, 1)

            def decay_tanh(n):
                act.wait_ge(s_td, n * 2 + 1)
                act.activation(tw[:, :], bank[1][0:TD_RANK, 0:N], ACT.Tanh).then_inc(s_tw, 1)

            def take_k_v(n, q):
                act.wait_ge(s_proj, n * 3 + 1)
                act.activation(kls[q][0][:, :], bank[2][:, 0:N], ACT.Copy).then_inc(s_evac, 1)
                act.activation(vs[q][:, :, :], bank[2][:, N:2 * N].rearrange("p (b n) -> p b n", b=BATCH),
                               ACT.Copy).then_inc(s_evac, 1)

            def take_decay_r_g(n, q):
                act.wait_ge(s_td, n * 2 + 2)
                act.activation(ew[:, :], bank[1][:, N:2 * N], ACT.Exp, bias=td_miu[:, 0:1]).then_inc(s_ew, 1)
                act.wait_ge(s_ew, n * 2 + 1)
                act.activation(tots[q][0][:, :], ew[:, :], ACT.Exp, scale=-1.0).then_inc(s_ew, 1)
                act.wait_ge(s_proj, n * 3 + 2)
                act.activation(rls[q][0][:, :], bank[3][:, 0:N], ACT.Copy).then_inc(s_evac, 1)
                act.wait_ge(s_proj, n * 3 + 3)
                act.activation(eg[:, :], bank[0][:, N:2 * N], ACT.Exp, scale=-1.0).then_inc(s_gT, 1)

            def front():
                modulate(0)
                lora_tanh(0)
                decay_tanh(0)
                take_k_v(0, 0)
                take_decay_r_g(0, 0)

            def scale_heads(n, q):
                act.wait_ge(s_zt, n + 1)
                act.activation(zT[:, :, :], bank[4][:, N:2 * N].rearrange("p (b n) -> p b n", b=BATCH), ACT.Identity,
                               bias=beta[:, 0:1], scale=gamma[:, 0:1]).then_inc(s_z, 1)

            def step(i, q, prepare, tail):
                rl, kl = rls[q], kls[q]
                start(act, i)
                for m in lv:
                    if m:
                        act.wait_ge(s_r, i * LEVELS + m)
                        act.wait_ge(s_k, i * LEVELS + m)
                        act.wait_ge(s_rc, i * 2 * LEVELS + 2 * m)
                    act.activation(halves(rl[m + 1], m)[:, :, 0], halves(rl[m], m)[:, :, 0],
                                   ACT.Copy).then_inc(s_rc, 1)
                    act.activation(halves(kl[m + 1], m)[:, :, 1], halves(kl[m], m)[:, :, 1],
                                   ACT.Copy).then_inc(s_rc, 1)
                    if prepare and m == 0:
                        modulate(i + 1)
                    if tail and m == 1:
                        scale_heads(i - 1, 1 - q)
                    if prepare and m == 3:
                        lora_tanh(i + 1)
                act.wait_ge(s_ktT, i + 1)
                act.activation(ktm[:, :, :], bank[4][:, 0:N].rearrange("p (b n) -> p b n", b=BATCH),
                               ACT.Copy).then_inc(s_ktm, 1)
                if prepare:
                    decay_tanh(i + 1)
                    take_k_v(i + 1, 1 - q)
                scores = pair[:, :].rearrange("p (u n) -> p u n", u=4)
                act.wait_ge(s_leaf, i + 1)
                act.activation(att[0:64, :, 64:128], scores[0:64, :, 160:224], ACT.Copy).then_inc(s_off, 1)
                act.activation(att[0:32, :, 32:64], scores[0:32, :, 224:256], ACT.Copy).then_inc(s_off, 1)
                act.activation(att[64:96, :, 96:128], scores[64:96, :, 224:256], ACT.Copy).then_inc(s_off, 1)
                if prepare:
                    take_decay_r_g(i + 1, 1 - q)

            steps(act, front, step, (scale_heads,))

        @block.tensor
        def _(pe):
            pe.wait_ge(s_w0, LOADS)

            def transpose_x(n):
                pe.wait_ge(s_xn, n * 3 + 3)
                for b in range(BATCH):
                    last = pe.transpose(bank[1][:, b * P:(b + 1) * P], xn[:, b, :], cst("ident"))
                last.then_inc(s_xt, 1)

            def lora(n):
                pe.wait_ge(s_xm, n + 1)
                pe.matmul(bank[1][:, 0:N], a_lora[:, 0:P], xm[:, :, :].rearrange(flat), start=True, stop=True)
                pe.matmul(bank[1][0:LORA, N:2 * N], a_lora[:, P:P + LORA], xm[:, :, :].rearrange(flat),
                          start=True, stop=True).then_inc(s_lora, 1)

            def mix(n):
                pe.wait_ge(s_lh, n * 2 + 2)
                for f in range(4):
                    mm = pe.matmul(bank[2 + f // 2][:, f % 2 * N:(f % 2 + 1) * N], b_pad[:, f, :], lh[:, :],
                                   start=True, stop=True)
                    if f % 2:
                        mm.then_inc(s_mix, 1)
                if not isinstance(n, int) or n:
                    pe.wait_ge(s_gate, n * 3)
                pe.matmul(bank[0][:, N:2 * N], b_pad[0:LORA, 4, :], lh4[:, :], start=True, stop=True).then_inc(s_mix, 1)

            def project(n):
                pe.wait_ge(s_xx, n * MIXES + 1)
                pe.matmul(bank[1][0:TD_RANK, 0:N], td_a[:, :], xx[:, 0].rearrange(flat), start=True,
                          stop=True).then_inc(s_td, 1)
                pe.wait_ge(s_xx, n * MIXES + 3)
                pe.matmul(bank[2][:, 0:N], wT[:, 0, :], xx[:, 1].rearrange(flat), start=True, stop=True)
                for b in range(BATCH):
                    last = pe.matmul(bank[2][:, N + b * P:N + (b + 1) * P], xx[:, 2, b, :], wT[:, 1, :], start=True,
                                     stop=True)
                last.then_inc(s_proj, 1)
                pe.wait_ge(s_tw, n + 1)
                pe.matmul(bank[1][:, N:2 * N], td_b[:, :], tw[:, :], start=True, stop=True).then_inc(s_td, 1)
                pe.wait_ge(s_xx, n * MIXES + 4)
                pe.matmul(bank[3][:, 0:N], wT[:, 2, :], xx[:, 3].rearrange(flat), start=True,
                          stop=True).then_inc(s_proj, 1)
                pe.wait_ge(s_xx, n * MIXES + 5)
                pe.matmul(bank[0][:, N:2 * N], wT[:, 3, :], xx[:, 4].rearrange(flat), start=True,
                          stop=True).then_inc(s_proj, 1)

            def front():
                transpose_x(0)
                lora(0)
                mix(0)
                project(0)

            def leaf_scores(slot, k_op, r_op):
                for u in range(4):
                    h, b = u // 2, u % 2
                    rows = slice(h * RW_DIM, (h + 1) * RW_DIM)
                    for k in range(4):
                        cols = slice(b * P + k * LEAF, b * P + (k + 1) * LEAF)
                        pe.matmul(pair[k * LEAF:(k + 1) * LEAF, u * 256 + slot * LEAF:u * 256 + (slot + 1) * LEAF],
                                  k_op[rows, cols], r_op[rows, cols], start=True, stop=True,
                                  tile_position=(h * RW_DIM, k * LEAF))

            def transpose_heads(n, q):
                pe.wait_ge(s_yn, n * 4 + 4)
                for b in range(BATCH):
                    last = pe.transpose(bank[4][:, N + b * P:N + (b + 1) * P], yn[:, b, :], cst("ident"))
                last.then_inc(s_zt, 1)

            def output(n, q):
                pe.wait_ge(s_zg, n + 1)
                for b in range(BATCH):
                    last = pe.matmul(bank[4][:, b * P:(b + 1) * P], zT[:, b, :], wT[:, 4, :], start=True, stop=True)
                last.then_inc(s_o, 1)

            def step(i, q, prepare, tail):
                rl, kl, v_sb = rls[q], kls[q], vs[q]
                start(pe, i)
                if prepare:
                    transpose_x(i + 1)
                pe.wait_ge(s_diag, i * 4 + 4)
                pe.nop(nofuse=True)
                leaf_scores(0, kd, rd)
                for m in (1, 2, 3, 4):
                    pe.wait_ge(s_r, i * LEVELS + m)
                    pe.wait_ge(s_k, i * LEVELS + m)
                    pe.wait_ge(s_rc, i * 2 * LEVELS + 2 * m)
                    pe.nop(nofuse=True)
                    leaf_scores(m, kl[m], rl[m])
                    if tail and m == 1:
                        transpose_heads(i - 1, 1 - q)
                    if prepare and m == 2:
                        lora(i + 1)
                    if tail and m == 3:
                        output(i - 1, 1 - q)
                if prepare:
                    mix(i + 1)
                pe.wait_ge(s_r, i * LEVELS + 6)
                pe.wait_ge(s_k, i * LEVELS + 6)
                pe.wait_ge(s_rc, i * 2 * LEVELS + 12)
                pe.nop(nofuse=True)
                for u in range(4):
                    h, b = u // 2, u % 2
                    rows = slice(h * RW_DIM, (h + 1) * RW_DIM)
                    for k in (0, 2):
                        s0 = b * P + k * LEAF
                        pe.matmul(pair[k * LEAF:(k + 1) * LEAF, u * 256 + 224:u * 256 + 256],
                                  kl[5][rows, s0:s0 + LEAF], rl[5][rows, s0 + LEAF:s0 + 2 * LEAF], start=True,
                                  stop=True, tile_position=(h * RW_DIM, k * LEAF))
                    last = pe.matmul(pair[0:64, u * 256 + 160:u * 256 + 224], kl[6][rows, b * P:b * P + 64],
                                     rl[6][rows, b * P + 64:b * P + 128], start=True, stop=True,
                                     tile_position=(h * RW_DIM, 0))
                last.then_inc(s_leafmm, 1)
                pe.wait_ge(s_k, i * LEVELS + 7)
                pe.wait_ge(s_r, i * LEVELS + 7)
                pe.wait_ge(s_rc, i * 2 * LEVELS + 14)
                if tail:
                    pe.wait_ge(s_gated, i)
                for b in range(BATCH):
                    last = pe.transpose(bank[4][:, b * P:(b + 1) * P], kl[7][:, b * P:(b + 1) * P], cst("ident"))
                last.then_inc(s_ktT, 1)
                if prepare:
                    project(i + 1)
                pe.wait_ge(s_att, i * 4 + 4)
                pe.wait_ge(s_off, i * 3 + 3)
                for b in range(BATCH):
                    pe.matmul(bank[5][:, b * P:(b + 1) * P], rl[7][:, b * P:(b + 1) * P], state[:, b, :],
                              start=True, stop=False, skip_group_check=True)
                    for h in range(RW_HEADS):
                        pe.matmul(bank[5][:, b * P + h * RW_DIM:b * P + (h + 1) * RW_DIM], att[:, h * BATCH + b, :],
                                  v_sb[:, b, h * RW_DIM:(h + 1) * RW_DIM], start=False, stop=True,
                                  skip_group_check=True)
                pe.wait_ge(s_ktm, i + 1)
                for b in range(BATCH):
                    last = pe.matmul(bank[5][:, N + b * P:N + (b + 1) * P], ktm[:, b, :], v_sb[:, b, :], start=True,
                                     stop=True, skip_group_check=True)
                last.then_inc(s_kv, 1)

            steps(pe, front, step, (transpose_heads, output))


def expert_phase(nc, t, x_sb, h_all, eps_pow, mod_row, mod_col, bank, cst, hT_all):
    with ExitStack() as ctx:
        def sb(name, shape, dt=F32):
            return ctx.enter_context(nc.sbuf_tensor(name, shape, dt))

        def sem(name):
            return nc.alloc_semaphore(name)

        GROUP = 4
        NG = TILES // GROUP
        DEPTH = len(bank)
        HALF = DEPTH // 2
        ROUNDS = SLOT_TILES // DEPTH
        FILLS = SLOTS * C // (P * 1024)

        router = sb("router", [P, E0])
        zero = sb("zero", [P, 1024])
        st = sb("r_st", [P, TILES, 6])
        mv = sb("r_mv", [P, TILES, 2])
        rstd = sb("r_rstd", [P, TILES])
        hT = [sb(f"r_hT{g}", [P, GROUP, P]) for g in range(NG)]
        lg = sb("r_lg", [P, TILES, E0])
        mx = sb("r_mx", [P, TILES, 8])
        idx = sb("r_idx", [P, TILES, 8], U32)
        idf = sb("r_idf", [P, TILES])
        weight = sb("router_weight", [P, TILES])
        oh = sb("r_oh", [P, E0, TILES])
        incl = sb("r_incl", [P, E0, TILES])
        excl = sb("r_excl", [P, E0, TILES])
        place = sb("r_place", [P, E0, TILES])
        place_of = sb("r_place_of", [P, TILES])
        slot = sb("slot_of_token", [P, TILES], U32)
        cnt_i = sb("r_cnt_i", [P, E0], I32)
        ntile = sb("r_ntile", [P, E0])
        ends = sb("r_ends", [P, E0])
        base = sb("r_base", [P, E0])
        le = sb("r_le", [1, SLOT_TILES, E0])
        te = sb("r_te", [1, SLOT_TILES])
        expert = sb("expert_of_tile", [1, SLOT_TILES], I32)

        weights = [sb(f"e_w{k}", [P, W0]) for k in range(DEPTH)]
        xg = [sb(f"e_xg{s}", [P, HALF, C]) for s in range(2)]
        xgT = [sb(f"e_xgT{k}", [P, P]) for k in range(DEPTH)]
        hid = [sb(f"e_hid{k}", [P, 2, P]) for k in range(DEPTH)]
        yg = [sb(f"e_yg{s}", [P, HALF, C]) for s in range(2)]
        yt = sb("e_yt", [P, TILES, C])

        s_in, s_zero, s_fill = sem("r_in"), sem("r_zero"), sem("r_fill")
        s_xt, s_ht, s_logit, s_lg, s_mx = sem("r_s_xt"), sem("r_s_ht"), sem("r_s_logit"), sem("r_s_lg"), sem("r_s_mx")
        s_idx, s_oh, s_rank, s_cnt, s_step = (sem("r_s_idx"), sem("r_s_oh"), sem("r_s_rank"), sem("r_s_cnt"),
                                              sem("r_s_step"))
        s_exp, s_slot, s_tile, s_sent = sem("r_s_exp"), sem("r_s_slot"), sem("r_s_tile"), sem("r_s_sent")
        s_x = [sem(f"e_s_x{s}") for s in range(2)]
        s_wt = [sem(f"e_s_wt{k}") for k in range(DEPTH)]
        s_out = [sem(f"e_s_out{s}") for s in range(2)]
        e_xt, e_xc, e_up, e_gelu, e_down, e_y = (sem("e_s_xt"), sem("e_s_xc"), sem("e_s_up"), sem("e_s_gelu"),
                                                 sem("e_s_down"), sem("e_s_y"))
        s_back = [sem(f"e_s_back{g}") for g in range(NG)]
        s_scaled, s_added, s_nst = sem("e_s_scaled"), sem("e_s_added"), sem("e_s_nst")
        s_nrstd, s_nxn, s_nxt, s_nht = sem("e_s_nrstd"), sem("e_s_nxn"), sem("e_s_nxt"), sem("e_s_nht")
        block = ctx.enter_context(nc.Block())

        def tr(k):
            return bank[k][:, 2 * P:3 * P]

        def down(k):
            return bank[k][:, 3 * P:4 * P]

        @block.sync
        def _(sp):
            sp.dma_start(router[:, :], t["L0_ffn_router_w"]).then_inc(s_in, 16)
            sp.wait_ge(s_zero, 1)
            slots = t["slots_in"].rearrange("(q p a) n -> q p (a n)", p=P, a=8)
            for q in range(FILLS):
                sp.dma_start(slots[q], zero[:, :]).then_inc(s_fill, 16)

            def experts_of(i):
                return [sp.value_load(expert[0:1, bass.ds(i * DEPTH + k, 1)], min_val=0, max_val=E0 - 1)
                        for k in range(DEPTH)]

            def load_weights(k, e):
                sp.dma_start(weights[k][:, :], t["experts0"][bass.ds(e, 1), :, :].rearrange("e p n -> p (e n)"))\
                    .then_inc(s_wt[k], 16)

            def load_x(s, i):
                sp.dma_start(xg[s][:, :, :], t["slots_in"][bass.ds((i * 2 + s) * HALF * P, HALF * P), :]
                             .rearrange("(k p) n -> p k n", p=P)).then_inc(s_x[s], 16)

            def store(s, i):
                sp.dma_start(t["slots_out"][bass.ds((i * 2 + s) * HALF * P, HALF * P), :]
                             .rearrange("(k p) n -> p k n", p=P), yg[s][:, :, :]).then_inc(s_out[s], 16)

            sp.wait_ge(s_tile, 1)
            for k, e in enumerate(experts_of(0)):
                load_weights(k, e)
            sp.wait_ge(s_sent, 16 * TILES)
            for s in range(2):
                load_x(s, 0)
            with sp.Fori(0, ROUNDS - 1) as i:
                experts = experts_of(i + 1)
                for s in range(2):
                    sp.wait_ge(e_xt, i * DEPTH + (s + 1) * HALF)
                    load_x(s, i + 1)
                    for k in range(s * HALF, (s + 1) * HALF):
                        sp.wait_ge(e_y, i * DEPTH + (k + 1 + DEPTH))
                        load_weights(k, experts[k])
                    store(s, i)
            for s in range(2):
                sp.wait_ge(e_y, ROUNDS * DEPTH + (s + 1) * HALF)
                store(s, ROUNDS - 1)
            for s in range(2):
                sp.wait_ge(s_out[s], 16 * (ROUNDS + 1))

        @block.gpsimd
        def _(pool):
            pool.memset(zero[:, :], 0.0).then_inc(s_zero, 1)
            pool.wait_ge(s_fill, 16 * FILLS)
            pool.wait_ge(s_slot, 1)
            for c in range(TILES):
                pool.indirect_dma_start(out=t["slots_in"], out_offset=bass.IndirectOffsetOnAxis(
                    ap=slot[:, c:c + 1], axis=0), in_=h_all[:, c, :], in_offset=None).then_inc(s_sent, 16)
            pool.wait_ge(s_sent, 16 * TILES)
            for s in range(2):
                pool.wait_ge(s_out[s], 16 * (ROUNDS + 1))
            for c in range(TILES):
                pool.indirect_dma_start(out=yt[:, c, :], out_offset=None, in_=t["slots_out"],
                                        in_offset=bass.IndirectOffsetOnAxis(ap=slot[:, c:c + 1], axis=0))\
                    .then_inc(s_back[c // GROUP], 16)
            for g in range(NG):
                part = slice(g * GROUP, (g + 1) * GROUP)
                pool.wait_ge(s_nst, (g + 1) * 2 * GROUP)
                pool.tensor_scalar(rstd[:, part], mv[:, part, 1], LN_EPS, None, ALU.add).then_inc(s_nrstd, 1)
                pool.wait_ge(s_nrstd, 2 * g + 1)
                pool.tensor_tensor(rstd[:, part], rstd[:, part], eps_pow[:, 0:GROUP], ALU.pow).then_inc(s_nrstd, 1)

        @block.scalar
        def _(act):
            for g in range(NG):
                act.wait_ge(s_xt, g + 1)
                act.activation(hT[g][:, :, :], bank[g][:, :].rearrange("p (k n) -> p k n", k=GROUP),
                               ACT.Copy).then_inc(s_ht, 1)
            act.wait_ge(s_mx, TILES)
            act.activation(weight[:, :], mx[:, :, 0], ACT.Exp, scale=-1.0).then_inc(s_exp, 1)
            for s in range(2):
                act.sem_inc(s_out[s], 16)
            with act.Fori(0, ROUNDS) as i:
                for k in range(DEPTH):
                    act.wait_ge(e_up, i * DEPTH + (k + 1))
                    for f in range(2):
                        act.activation(hid[k][:, f, :], bank[k][:, f * P:(f + 1) * P], ACT.Gelu,
                                       bias=weights[k][:, 2 * F0 + f:2 * F0 + f + 1]).then_inc(e_gelu, 1)

            for g in range(NG):
                b = g * GROUP // CHUNKS
                act.wait_ge(s_nxt, g + 1)
                act.activation(hT_all[:, g * GROUP:(g + 1) * GROUP, :],
                               bank[g][:, :].rearrange("p (k n) -> p k n", k=GROUP), ACT.Identity,
                               bias=mod_col[:, 1, 0, b:b + 1], scale=mod_col[:, 1, 1, b:b + 1]).then_inc(s_nht, 1)

        @block.vector
        def _(dve):
            dve.wait_ge(s_logit, 1)
            dve.tensor_copy(lg[:, :, :], bank[4][:, 0:TILES * E0].rearrange("p (c n) -> p c n", c=TILES))\
                .then_inc(s_lg, 1)
            dve.wait_ge(s_lg, 1)
            for c in range(TILES):
                dve.max(mx[:, c, :], lg[:, c, :]).then_inc(s_mx, 1)
            for c in range(TILES):
                dve.wait_ge(s_mx, c + 1)
                dve.max_index(idx[:, c, :], mx[:, c, :], lg[:, c, :]).then_inc(s_idx, 1)
            dve.wait_ge(s_idx, TILES)
            dve.tensor_copy(idf[:, :], idx[:, :, 0]).then_inc(s_idx, 1)
            dve.wait_ge(s_idx, TILES + 1)
            dve.tensor_tensor(oh[:, :, :], cst("iota16")[:, :, None].to_broadcast([P, E0, TILES]),
                              idf[:, None, :].to_broadcast([P, E0, TILES]), ALU.is_equal).then_inc(s_oh, 1)
            dve.wait_ge(s_oh, 1)
            flat = "p e c -> p (e c)"
            dve.tensor_tensor_scan(incl[:, :, :].rearrange(flat), cst("restart"), oh[:, :, :].rearrange(flat), 0.0,
                                   ALU.mult, ALU.add).then_inc(s_oh, 1)
            dve.wait_ge(s_oh, 2)
            dve.tensor_tensor(excl[:, :, :], incl[:, :, :], oh[:, :, :], ALU.subtract).then_inc(s_oh, 1)
            dve.wait_ge(s_cnt, 1)
            dve.tensor_scalar(cnt_i[:, :], bank[0][:, 0:E0], float(P - 1), None, ALU.add).then_inc(s_step, 1)
            dve.wait_ge(s_step, 1)
            dve.tensor_scalar(cnt_i[:, :], cnt_i[:, :], 7, None, ALU.logical_shift_right).then_inc(s_step, 1)
            dve.wait_ge(s_step, 2)
            dve.tensor_copy(ntile[:, :], cnt_i[:, :]).then_inc(s_step, 1)
            dve.wait_ge(s_step, 3)
            dve.tensor_tensor_scan(ends[:, :], cst("ones")[:, 0:E0], ntile[:, :], 0.0, ALU.mult,
                                   ALU.add).then_inc(s_step, 1)
            dve.wait_ge(s_step, 4)
            dve.tensor_tensor(base[:, :], ends[:, :], ntile[:, :], ALU.subtract).then_inc(s_step, 1)
            dve.wait_ge(s_step, 5)
            dve.wait_ge(s_rank, 1)
            dve.scalar_tensor_tensor(out=place[:, :, :], in0=base[:, :, None].to_broadcast([P, E0, TILES]),
                                     scalar=float(P), in1=bank[5][:, 0:E0 * TILES].rearrange("p (e c) -> p e c", e=E0),
                                     op0=ALU.mult, op1=ALU.add).then_inc(s_step, 1)
            dve.wait_ge(s_step, 6)
            dve.tensor_tensor(place[:, :, :], place[:, :, :], oh[:, :, :], ALU.mult).then_inc(s_step, 1)
            dve.wait_ge(s_step, 7)
            dve.tensor_reduce(place_of[:, :], place[:, :, :].rearrange("p e c -> p c e"), AX.X, ALU.add)\
                .then_inc(s_step, 1)
            dve.wait_ge(s_step, 8)
            dve.tensor_copy(slot[:, :], place_of[:, :]).then_inc(s_slot, 1)
            dve.tensor_tensor(le[:, :, :], ends[0:1, None, :].to_broadcast([1, SLOT_TILES, E0]),
                              cst("iota32")[0:1, :, None].to_broadcast([1, SLOT_TILES, E0]),
                              ALU.is_le).then_inc(s_step, 1)
            dve.wait_ge(s_step, 9)
            dve.tensor_reduce(te[:, :], le[:, :, :], AX.X, ALU.add).then_inc(s_step, 1)
            dve.wait_ge(s_step, 10)
            dve.tensor_scalar(expert[:, :], te[:, :], float(E0 - 1), None, ALU.min).then_inc(s_tile, 1)
            dve.wait_ge(s_exp, 1)
            dve.tensor_scalar(weight[:, :], weight[:, :], 1.0, None, ALU.add).then_inc(s_exp, 1)
            dve.wait_ge(s_exp, 2)
            dve.reciprocal(weight[:, :], weight[:, :]).then_inc(s_exp, 1)
            dve.wait_ge(s_exp, 3)
            with dve.Fori(0, ROUNDS) as i:

                def inputs(half):
                    for k in half:
                        dve.wait_ge(e_xt, i * DEPTH + (k + 1))
                        dve.tensor_copy(xgT[k][:, :], tr(k)).then_inc(e_xc, 1)

                def results(half):
                    for k in half:
                        dve.wait_ge(e_down, i * DEPTH + (k + 1))
                        dve.wait_ge(s_out[k // HALF], i * 16 + 16)
                        dve.tensor_copy(yg[k // HALF][:, k % HALF, :], down(k)).then_inc(e_y, 1)

                first, second = range(HALF), range(HALF, DEPTH)
                inputs(first)
                inputs(second)
                results(first)
                results(second)
            for g in range(NG):
                tiles = range(g * GROUP, (g + 1) * GROUP)
                dve.wait_ge(s_back[g], 16 * GROUP)
                for c in tiles:
                    dve.scalar_tensor_tensor(out=yt[:, c, :], in0=yt[:, c, :], scalar=weight[:, c:c + 1],
                                             in1=mod_row[:, 0, 1, c // CHUNKS, :], op0=ALU.mult,
                                             op1=ALU.mult).then_inc(s_scaled, 1)
                dve.wait_ge(s_scaled, (g + 1) * GROUP)
                part = slice(g * GROUP, (g + 1) * GROUP)
                dve.tensor_tensor(x_sb[:, part, :], x_sb[:, part, :], yt[:, part, :], ALU.add).then_inc(s_added, 1)
                dve.wait_ge(s_added, g + 1)
                for c in tiles:
                    dve.bn_stats(st[:, c, :], x_sb[:, c, :]).then_inc(s_nst, 1)
                dve.wait_ge(s_nst, g * 2 * GROUP + GROUP)
                for c in tiles:
                    dve.bn_aggr(mv[:, c, :], st[:, c, :]).then_inc(s_nst, 1)
            for g in range(NG):
                dve.wait_ge(s_nrstd, 2 * g + 2)
                for c in range(g * GROUP, (g + 1) * GROUP):
                    dve.tensor_scalar(h_all[:, c, :], x_sb[:, c, :], mv[:, c, 0:1], rstd[:, c:c + 1], ALU.subtract,
                                      ALU.mult).then_inc(s_nxn, 1)

        @block.tensor
        def _(pe):
            pe.sem_inc(e_y, DEPTH)
            pe.wait_ge(s_in, 16)

            def logits(g):
                pe.wait_ge(s_ht, g + 1)
                for k in range(GROUP):
                    c = g * GROUP + k
                    last = pe.matmul(bank[4][:, c * E0:(c + 1) * E0], hT[g][:, k, :], router[:, :], start=True,
                                     stop=True)
                return last

            for g in range(NG):
                for k in range(GROUP):
                    last = pe.transpose(bank[g][:, k * P:(k + 1) * P], h_all[:, g * GROUP + k, :], cst("ident"))
                last.then_inc(s_xt, 1)
                if g:
                    logits(g - 1)
            logits(NG - 1).then_inc(s_logit, 1)
            pe.wait_ge(s_oh, 2)
            pe.matmul(bank[0][:, 0:E0], cst("ones"), incl[:, :, TILES - 1], start=True, stop=True).then_inc(s_cnt, 1)
            pe.matmul(bank[5][:, 0:E0 * TILES], cst("before"), oh[:, :, :].rearrange("p e c -> p (e c)"), start=True,
                      stop=False)
            pe.wait_ge(s_oh, 3)
            pe.matmul(bank[5][:, 0:E0 * TILES], cst("ones"), excl[:, :, :].rearrange("p e c -> p (e c)"), start=False,
                      stop=True).then_inc(s_rank, 1)
            with pe.Fori(0, ROUNDS) as i:

                def transposes(half):
                    for k in half:
                        pe.wait_ge(s_x[k // HALF], i * 16 + 16)
                        pe.wait_ge(e_y, i * DEPTH + (k + 1))
                        pe.transpose(tr(k), xg[k // HALF][:, k % HALF, :], cst("ident")).then_inc(e_xt, 1)

                def ups(half):
                    for k in half:
                        pe.wait_ge(e_xc, i * DEPTH + (k + 1))
                        pe.wait_ge(s_wt[k], i * 16 + 16)
                        for f in range(2):
                            last = pe.matmul(bank[k][:, f * P:(f + 1) * P], weights[k][:, f * P:(f + 1) * P],
                                             xgT[k][:, :], start=True, stop=True)
                        last.then_inc(e_up, 1)

                def downs(half):
                    for k in half:
                        pe.wait_ge(e_gelu, i * (2 * DEPTH) + (2 * k + 2))
                        for f in range(2):
                            pe.matmul(down(k), hid[k][:, f, :], weights[k][:, F0 + f * P:F0 + (f + 1) * P],
                                      start=(f == 0), stop=False)
                        pe.matmul(down(k), weights[k][:, W0 - 1:W0].to_broadcast([P, P]), cst("ident"), start=False,
                                  stop=True)\
                            .then_inc(e_down, 1)

                first, second = range(HALF), range(HALF, DEPTH)
                transposes(first)
                ups(first)
                transposes(second)
                downs(first)
                ups(second)
                downs(second)
            for g in range(NG):
                pe.wait_ge(s_nxn, (g + 1) * GROUP)
                for k in range(GROUP):
                    last = pe.transpose(bank[g][:, k * P:(k + 1) * P], h_all[:, g * GROUP + k, :], cst("ident"))
                last.then_inc(s_nxt, 1)


def hla_phase(nc, x_bc, mod_row, bank, pair, cst, hT_all, W, s_weights):
    with ExitStack() as ctx:
        def sb(name, shape, dt=F32):
            return ctx.enter_context(nc.sbuf_tensor(name, shape, dt))

        def sem(name):
            return nc.alloc_semaphore(name)

        J = range(GROUPS)
        hT = [sb(f"h_hT{b}", [P, P]) for b in range(BATCH)]
        v_sb = [sb(f"h_v{b}", [P, HL_HEADS * HL_DIM]) for b in range(BATCH)]
        qk = [[sb(f"h_qk{b}{j}", [P, 2, P]) for j in J] for b in range(BATCH)]
        qkd = [[sb(f"h_qkd{b}{j}", [P, 2, P]) for j in J] for b in range(BATCH)]
        qB = [[sb(f"h_qB{b}{j}", [P, HPG, P]) for j in J] for b in range(BATCH)]
        raw = [sb(f"h_raw{j}", [P, HPG, P]) for j in J]
        kg = [sb(f"h_kg{j}", [P, 2, P]) for j in J]
        kqd = [sb(f"h_kqd{j}", [P, 2, P]) for j in J]
        m1 = [sb(f"h_m1{j}", [P, HPG, P]) for j in J]
        m2 = [sb(f"h_m2{j}", [P, HPG, P]) for j in J]
        m3 = [sb(f"h_m3{j}", [P, HPG, P]) for j in J]
        aT = [sb(f"h_aT{j}", [P, P]) for j in J]
        gT = [sb(f"h_gT{j}", [P, P]) for j in J]
        aTd = [sb(f"h_aTd{j}", [P, P]) for j in J]
        oT = [sb(f"h_oT{j}", [P, P]) for j in J]
        states = [[sb(f"h_state{b}{j}", [P, 3, P]) for j in J] for b in range(BATCH)]
        fresh = [sb(f"h_fresh{k}", [P, 3, P]) for k in range(2)]
        gated = sb("h_gated", [P, C])

        X = [k[:, :] for k in bank[0:4]]
        ring = [pair[:, 0:512], pair[:, 512:1024]]
        front = bank[4]
        A_AT, T_AT, M_AT = (0, 1, 3, 5), (2, 4, 6, 7), (8, 9, 10, 11)
        upd = bank[5]
        s_zero, s_hT, s_v, s_vc = sem("h_s_zero"), sem("h_s_hT"), sem("h_s_v"), sem("h_s_vc")
        s_qk, s_qkc, s_qkd, s_bd = sem("h_s_qk"), sem("h_s_qkc"), sem("h_s_qkd"), sem("h_s_bd")
        s_tm, s_tmc, s_sc, s_mask = sem("h_s_tm"), sem("h_s_tmc"), sem("h_s_sc"), sem("h_s_mask")
        s_gt, s_gtc = sem("h_s_gt"), sem("h_s_gtc")
        s_kq, s_raw, s_m1 = sem("h_s_kq"), sem("h_s_raw"), sem("h_s_m1")
        s_ga, s_gac, s_aTd, s_o, s_oc = sem("h_s_ga"), sem("h_s_gac"), sem("h_s_aTd"), sem("h_s_o"), sem("h_s_oc")
        s_upd, s_new, s_st, s_out = sem("h_s_upd"), sem("h_s_new"), sem("h_s_st"), sem("h_s_out")
        s_gated, s_x = sem("h_s_gated"), sem("h_s_x")
        block = ctx.enter_context(nc.Block())

        def nth(i, b, per_tile, k):
            return i * (BATCH * per_tile) + (b * per_tile + k + 1)

        hT_bc = hT_all[:, :, :].rearrange("p (b c) n -> p b c n", b=BATCH)
        heads = cst("head4")

        def slot(use):
            return ring[use % 2]

        def following(i, b):
            return (i, 1) if b == 0 else (i + 1, 0)

        @block.gpsimd
        def _(pool):
            def fetch(i, b):
                pool.tensor_tensor(hT[b][:, None, :], hT_all[:, bass.ds(i + b * CHUNKS, 1), :],
                                   cst("ones")[:, None, :], ALU.mult).then_inc(s_hT, 1)

            def expand(i, b):
                for j in J:
                    pool.wait_ge(s_qkc, nth(i, b, GROUPS, j))
                    pool.wait_ge(s_o, nth(i, b, GROUPS, j))
                    pool.tensor_tensor(qB[b][j][:, :, :], qk[b][j][:, 0, None, :].to_broadcast([P, HPG, P]),
                                       heads[:, 0::HL_DIM, None].to_broadcast([P, HPG, P]),
                                       ALU.mult).then_inc(s_bd, 1)
                    pool.tensor_tensor(qkd[b][j][:, :, :], qk[b][j][:, :, :],
                                       cst("decay_row")[:, None, :].to_broadcast([P, 2, P]),
                                       ALU.mult).then_inc(s_qkd, 1)

            fetch(0, 0)
            expand(0, 0)
            with pool.Fori(0, CHUNKS) as i:
                for b in range(BATCH):
                    fetch(*following(i, b))
                    expand(*following(i, b))
                    pool.wait_ge(s_gated, nth(i, b, 1, 1))
                    pool.tensor_tensor(x_bc[:, b, bass.ds(i, 1), :], x_bc[:, b, bass.ds(i, 1), :],
                                       gated[:, None, :], ALU.add).then_inc(s_x, 1)
            pool.wait_ge(s_x, TILES + 1)

        @block.scalar
        def _(act):
            def copy_v(i, b):
                act.wait_ge(s_v, nth(i, b, 1, 0))
                act.wait_ge(s_upd, nth(i, b, GROUPS, GROUPS - 1))
                act.activation(v_sb[b][:, :], front[:, :], ACT.Copy).then_inc(s_vc, 1)

            def copy_qk(i, b, j):
                act.wait_ge(s_qk, nth(i, b, GROUPS, j))
                act.activation(qk[b][j][:, :, :], front[:, 0:2 * P].rearrange("p (k n) -> p k n", k=2),
                               ACT.Copy).then_inc(s_qkc, 1)

            def copy_raw(i, b, j):
                act.wait_ge(s_kq, nth(i, b, GROUPS, j))
                act.activation(raw[j][:, :, :], slot(A_AT[j]).rearrange("p (h n) -> p h n", h=HPG),
                               ACT.Copy).then_inc(s_raw, 1)

            copy_v(0, 0)
            for j in J:
                copy_qk(0, 0, j)
            with act.Fori(0, CHUNKS) as i:
                for b in range(BATCH):
                    copy_raw(i, b, 0)
                    for j in J:
                        act.wait_ge(s_tm, nth(i, b, GROUPS, j))
                        act.activation(kg[j][:, 0, :], X[j][:, 2 * P:3 * P], ACT.Copy).then_inc(s_tmc, 1)
                        act.activation(kqd[j][:, :, :], X[j][:, 2 * P:4 * P].rearrange("p (k n) -> p k n", k=2),
                                       ACT.Copy, scale=cst("decay_col")[:, 0:1]).then_inc(s_tmc, 1)
                        if j == 1:
                            copy_raw(i, b, 1)
                    copy_v(*following(i, b))
                    copy_raw(i, b, 2)
                    copy_raw(i, b, 3)
                    copy_qk(*following(i, b), 0)
                    for j in J:
                        act.wait_ge(s_ga, nth(i, b, GROUPS, j))
                        act.activation(aT[j][:, :], X[j][:, P:2 * P], ACT.Copy).then_inc(s_gac, 1)
                        act.activation(gT[j][:, :], X[j][:, 0:P], ACT.Copy).then_inc(s_gac, 1)
                        if j == 1:
                            copy_qk(*following(i, b), 1)
                    for j in J:
                        act.wait_ge(s_gt, nth(i, b, GROUPS, j))
                        act.activation(kg[j][:, 1, :], X[j][:, 0:P], ACT.Copy, scale=-1.0).then_inc(s_gtc, 1)
                        if j == 1:
                            copy_qk(*following(i, b), 2)
                    for j in J:
                        act.wait_ge(s_o, nth(i, b, GROUPS, j + 2 * GROUPS))
                        act.activation(oT[j][:, :], X[j][:, 2 * P:3 * P], ACT.Copy).then_inc(s_oc, 1)
                    copy_qk(*following(i, b), 3)

        @block.vector
        def _(dve):
            for b in range(BATCH):
                for j in J:
                    dve.memset(states[b][j][:, :, :], 0.0).then_inc(s_zero, 1)
            dve.wait_ge(s_zero, BATCH * GROUPS)
            dve.sem_inc(s_x, 1)
            dve.sem_inc(s_st, 2 * GROUPS)
            incl = cst("decay_incl")[:, None, :].to_broadcast([P, HPG, P])
            excl = cst("decay_excl")[:, None, :].to_broadcast([P, HPG, P])
            with dve.Fori(0, CHUNKS) as i:
                for b in range(BATCH):

                    def mask(dst, src, m, done):
                        dve.tensor_tensor(dst[:, :, :], src, m, ALU.mult).then_inc(done, 1)

                    def scores(use):
                        return slot(use).rearrange("p (h n) -> p h n", h=HPG)

                    for j in J:
                        dve.wait_ge(s_raw, nth(i, b, GROUPS, j))
                        mask(m1[j], raw[j][:, :, :], incl, s_m1)
                        dve.wait_ge(s_sc, nth(i, b, 2 * GROUPS, j))
                        mask(m2[j], scores(T_AT[j]), excl, s_mask)
                    for j in J:
                        dve.wait_ge(s_gac, nth(i, b, 2 * GROUPS, 2 * j + 1))
                        dve.tensor_tensor(aTd[j][:, :], X[j][:, P:2 * P], cst("decay_row"),
                                          ALU.mult).then_inc(s_aTd, 1)
                    for j in J:
                        dve.wait_ge(s_sc, nth(i, b, 2 * GROUPS, GROUPS + j))
                        mask(m3[j], scores(M_AT[j]), incl, s_mask)
                    for j in J:
                        dve.wait_ge(s_upd, nth(i, b, GROUPS, j + 2 * GROUPS))
                        dve.wait_ge(s_st, nth(i, b, GROUPS, j + 2 * GROUPS - 2))
                        dve.tensor_tensor(fresh[j % 2][:, :, :], upd[:, 0:3 * P].rearrange("p (k n) -> p k n", k=3),
                                          heads[:, None, :].to_broadcast([P, 3, P]), ALU.mult).then_inc(s_new, 1)
                        dve.wait_ge(s_new, nth(i, b, GROUPS, j + 1))
                        flat = "p k n -> p (k n)"
                        dve.scalar_tensor_tensor(out=states[b][j][:, :, :].rearrange(flat),
                                                 in0=states[b][j][:, :, :].rearrange(flat), scalar=GAMMA ** P,
                                                 in1=fresh[j % 2][:, :, :].rearrange(flat), op0=ALU.mult,
                                                 op1=ALU.add).then_inc(s_st, 1)
                    dve.wait_ge(s_out, nth(i, b, 1, 0))
                    dve.wait_ge(s_x, nth(i, b, 1, 0))
                    dve.tensor_tensor(gated[:, :], X[0][:, 3 * P:4 * P], mod_row[:, 1, 0, b, :],
                                      ALU.mult).then_inc(s_gated, 1)

        @block.tensor
        def _(pe):
            pe.wait_ge(s_weights, 16 * 4)
            pe.sem_inc(s_gated, 1)
            pe.sem_inc(s_o, 2 * GROUPS)
            pe.sem_inc(s_mask, 2)
            pe.sem_inc(s_new, 1)
            pe.sem_inc(s_upd, 2 * GROUPS)

            def project_v(i, b):
                pe.wait_ge(s_hT, nth(i, b, 1, 0))
                pe.matmul(front[:, :], hT[b][:, :], W["v"][:, :], start=True, stop=True).then_inc(s_v, 1)

            def project_qk(i, b, j):
                if j == 0:
                    pe.wait_ge(s_vc, nth(i, b, 1, 0))
                else:
                    pe.wait_ge(s_qkc, nth(i, b, GROUPS, j - 1))
                cols = slice(j * P, (j + 1) * P)
                pe.matmul(front[:, 0:P], W["q"][:, cols], hT[b][:, :], start=True, stop=True)
                pe.matmul(front[:, P:2 * P], W["k"][:, cols], hT[b][:, :], start=True, stop=True).then_inc(s_qk, 1)

            project_v(0, 0)
            for j in J:
                project_qk(0, 0, j)
            with pe.Fori(0, CHUNKS) as i:
                for b in range(BATCH):

                    def products(j):
                        pe.wait_ge(s_bd, nth(i, b, GROUPS, j))
                        if j < 2:
                            pe.wait_ge(s_mask, nth(i, b, 2 * GROUPS, j))
                        else:
                            pe.wait_ge(s_raw, nth(i, b, GROUPS, j - 1))
                        pe.matmul(slot(A_AT[j]), qk[b][j][:, 1, :], qB[b][j][:, :, :].rearrange("p h n -> p (h n)"),
                                  start=True, stop=True).then_inc(s_kq, 1)

                    def transposed(j):
                        pe.wait_ge(s_raw, nth(i, b, GROUPS, j))
                        if j in (1, 2):
                            pe.wait_ge(s_mask, nth(i, b, 2 * GROUPS, j - 1 + 2))
                        for h in range(HPG):
                            last = pe.transpose(slot(T_AT[j])[:, h * P:(h + 1) * P], raw[j][:, h, :], cst("ident"))
                        last.then_inc(s_sc, 1)

                    products(0)
                    for j in J:
                        if j == 0:
                            pe.wait_ge(s_gated, nth(i, b, 1, 0))
                            pe.wait_ge(s_qkc, nth(i, b, GROUPS, GROUPS - 1))
                        pe.transpose(X[j][:, 2 * P:3 * P], qk[b][j][:, 1, :], cst("ident"))
                        pe.transpose(X[j][:, 3 * P:4 * P], qk[b][j][:, 0, :], cst("ident")).then_inc(s_tm, 1)
                    products(1)
                    transposed(0)
                    project_v(*following(i, b))
                    products(2)
                    transposed(1)
                    products(3)
                    project_qk(*following(i, b), 0)
                    transposed(2)
                    transposed(3)
                    for j in J:
                        pe.wait_ge(s_tmc, nth(i, b, 2 * GROUPS, 2 * j + 1))
                        pe.wait_ge(s_qkd, nth(i, b, GROUPS, j))
                        pe.wait_ge(s_st, nth(i, b, GROUPS, j))
                        pe.wait_ge(s_m1, nth(i, b, GROUPS, j))
                        pe.wait_ge(s_mask, nth(i, b, 2 * GROUPS, j + 2))
                        if j == 0:
                            pe.wait_ge(s_vc, nth(i, b, 1, 0))
                        g, a = X[j][:, 0:P], X[j][:, P:2 * P]
                        pe.matmul(g, states[b][j][:, 2, :], qkd[b][j][:, 1, :], start=True, stop=False,
                                  skip_group_check=True)
                        for h in range(HPG):
                            rows = slice(h * HL_DIM, (h + 1) * HL_DIM)
                            pe.matmul(g[rows, :], v_sb[b][:, j * P + h * HL_DIM:j * P + (h + 1) * HL_DIM],
                                      m2[j][:, h, :], start=False, stop=True, skip_group_check=True,
                                      tile_position=(0, h * HL_DIM))
                        pe.matmul(a, states[b][j][:, 0, :], qkd[b][j][:, 0, :], start=True, stop=False,
                                  skip_group_check=True)
                        for h in range(HPG):
                            rows = slice(h * HL_DIM, (h + 1) * HL_DIM)
                            last = pe.matmul(a[rows, :], kg[j][:, 0, rows], m1[j][:, h, :], start=False, stop=True,
                                             skip_group_check=True, tile_position=(0, h * HL_DIM))
                        last.then_inc(s_ga, 1)
                        if j == 1:
                            project_qk(*following(i, b), 1)
                    for j in J:
                        pe.wait_ge(s_gac, nth(i, b, 2 * GROUPS, 2 * j))
                        pe.wait_ge(s_mask, nth(i, b, 2 * GROUPS, j + 4))
                        for h in range(HPG):
                            last = pe.matmul(slot(M_AT[j])[:, h * P:(h + 1) * P], qB[b][j][:, h, :], aT[j][:, :],
                                             start=True, stop=True)
                        last.then_inc(s_sc, 1)
                        pe.wait_ge(s_gac, nth(i, b, 2 * GROUPS, 2 * j + 1))
                        pe.wait_ge(s_aTd, nth(i, b, GROUPS, j))
                        pe.transpose(X[j][:, 0:P], gT[j][:, :], cst("ident")).then_inc(s_gt, 1)
                        if j == 1:
                            project_qk(*following(i, b), 2)
                    for j in J:
                        pe.wait_ge(s_gac, nth(i, b, 2 * GROUPS, 2 * j + 1))
                        pe.wait_ge(s_aTd, nth(i, b, GROUPS, j))
                        pe.wait_ge(s_mask, nth(i, b, 2 * GROUPS, GROUPS + j + 2))
                        pe.wait_ge(s_gtc, nth(i, b, GROUPS, j))
                        o = X[j][:, 2 * P:3 * P]
                        pe.matmul(o, states[b][j][:, 2, :], aTd[j][:, :], start=True, stop=False,
                                  skip_group_check=True)
                        pe.matmul(o, states[b][j][:, 1, :], qkd[b][j][:, 0, :], start=False, stop=False,
                                  skip_group_check=True)
                        for h in range(HPG):
                            rows = slice(h * HL_DIM, (h + 1) * HL_DIM)
                            pe.matmul(o[rows, :], v_sb[b][:, j * P + h * HL_DIM:j * P + (h + 1) * HL_DIM],
                                      m3[j][:, h, :], start=False, stop=False, skip_group_check=True,
                                      tile_position=(0, h * HL_DIM))
                        for h in range(HPG):
                            rows = slice(h * HL_DIM, (h + 1) * HL_DIM)
                            last = pe.matmul(o[rows, :], kg[j][:, 1, rows], m1[j][:, h, :], start=False, stop=True,
                                             skip_group_check=True, tile_position=(0, h * HL_DIM))
                        last.then_inc(s_o, 1)
                        pe.wait_ge(s_new, nth(i, b, GROUPS, j))
                        pe.matmul(upd[:, 0:2 * P], kqd[j][:, 0, :], kg[j][:, :, :].rearrange("p k n -> p (k n)"),
                                  start=True, stop=True)
                        pe.matmul(upd[:, 2 * P:3 * P], kqd[j][:, 1, :], v_sb[b][:, j * P:(j + 1) * P], start=True,
                                  stop=True).then_inc(s_upd, 1)
                    project_qk(*following(i, b), 3)
                    for j in J:
                        pe.wait_ge(s_oc, nth(i, b, GROUPS, j))
                        last = pe.matmul(X[0][:, 3 * P:4 * P], oT[j][:, :], W["o"][:, j, :], start=(j == 0),
                                         stop=(j == GROUPS - 1))
                    last.then_inc(s_out, 1)


def swiglu_phase(nc, t, x_sb, eps_pow, sbw, mod_row, bank, pair, cst, W, s_weights, out):
    with ExitStack() as ctx:
        def sb(name, shape, dt=F32):
            return ctx.enter_context(nc.sbuf_tensor(name, shape, dt))

        def sem(name):
            return nc.alloc_semaphore(name)

        N = 512
        TPG = N // P
        NG = TILES // TPG
        ROUNDS = NG // BATCH
        E = E1_LIVE
        gate = sb("g_gate", [P, E])
        st = sb("g_st", [P, TILES, 6])
        mv = sb("g_mv", [P, TILES, 2])
        rstd = sb("g_rstd", [P, TILES])
        h_all = sb("g_h_all", [P, TILES, C])
        xT_all = sb("g_xT_all", [P, TILES, P])
        best = sb("g_best", [P, TILES])
        shifted = sb("g_shifted", [P, TILES, E])
        prob = sb("g_prob", [P, TILES, 8])
        mx = sb("g_mx", [P, TILES, 8])
        idx = sb("g_idx", [P, TILES, 8], U32)
        idf = sb("g_idf", [P, TILES, 2])
        den = sb("g_den", [P, TILES])
        cw = sb("g_cw", [P, 2, TILES, E])
        hs = [sb(f"g_hs{k}", [P, E, C]) for k in range(2)]
        xg = [sb(f"f_xg{b}", [P, 1 + E, N]) for b in range(BATCH)]
        sa = [sb(f"f_sa{k}", [P, N]) for k in range(2)]
        hh = [sb(f"f_h{k}", [P, N]) for k in range(2)]
        oT = [sb(f"f_oT{b}", [P, N]) for b in range(BATCH)]
        gated = [sb(f"f_gated{b}", [P, TPG, C]) for b in range(BATCH)]
        up_a = [bank[0], bank[1]]
        up_b = [bank[2], bank[3]]
        acc = [bank[4], bank[5]]
        back, scaled = pair[:, 0:512], pair[:, 512:1024]
        units = []
        for e in range(0, E, 2):
            units += [(e, f) for f in range(FULL1)] + [(e + 1, f) for f in range(FULL1)] + [(e, None)]
        U = len(units)
        assert U % 2 == 0
        prepare_at = {3 + 4 * k: k for k in range(TPG)}
        assert max(prepare_at) < U

        s_gate, s_pad, s_st, s_mv, s_rstd = (sem("g_s_gate"), sem("g_s_pad"), sem("g_s_st"), sem("g_s_mv"),
                                             sem("g_s_rstd"))
        s_mod, s_h, s_xt, s_keep, s_logit = (sem("g_s_mod"), sem("g_s_h"), sem("g_s_xt"), sem("g_s_keep"),
                                             sem("g_s_logit"))
        s_shift, s_prob, s_mx, s_idx, s_cw = (sem("g_s_shift"), sem("g_s_prob"), sem("g_s_mx"), sem("g_s_idx"),
                                              sem("g_s_cw"))
        s_hs, s_hst, s_hsc, s_xg = sem("g_s_hs"), sem("g_s_hst"), sem("g_s_hsc"), sem("f_s_xg")
        s_a, s_b, s_sa, s_hh = sem("f_s_a"), sem("f_s_b"), sem("f_s_sa"), sem("f_s_hh")
        s_down, s_accc, s_back = sem("f_s_down"), sem("f_s_accc"), sem("f_s_back")
        s_gated, s_x, s_out = sem("f_s_gated"), sem("f_s_x"), sem("f_s_out")
        block = ctx.enter_context(nc.Block())

        def unit(i, b, n):
            return i * (BATCH * U) + (b * U + n)

        def group(i, b):
            return i * BATCH + b

        def following(i, b):
            return (i, 1) if b == 0 else (i + 1, 0)

        @block.tensor
        def _(pe):
            pe.wait_ge(s_gate, 16)
            def logits(g):
                pe.wait_ge(s_keep, g + 1)
                for c in range(g * TPG, (g + 1) * TPG):
                    last = pe.matmul(bank[4][:, c * E:(c + 1) * E], xT_all[:, c, :], gate[:, :], start=True, stop=True)
                return last

            for g in range(NG):
                pe.wait_ge(s_h, (g + 1) * TPG)
                for k in range(TPG):
                    last = pe.transpose(bank[g][:, k * P:(k + 1) * P], h_all[:, g * TPG + k, :], cst("ident"))
                last.then_inc(s_xt, 1)
                if g:
                    logits(g - 1)
            logits(NG - 1).then_inc(s_logit, 1)
            pe.wait_ge(s_shift, 1)
            pe.sem_inc(s_sa, 2)
            pe.sem_inc(s_hh, 2)
            pe.sem_inc(s_accc, 2)
            pe.sem_inc(s_gated, 2)
            pe.sem_inc(s_hsc, 1)

            def prepare(i, b, k):
                pe.wait_ge(s_hs, group(i, b) * TPG + (k + 1))
                pe.wait_ge(s_hsc, group(i, b) * TPG + (k + 1))
                for e in range(E):
                    last = pe.transpose(scaled[:, e * P:(e + 1) * P], hs[k % 2][:, e, :], cst("ident"))
                last.then_inc(s_hst, 1)

            for k in range(TPG):
                prepare(0, 0, k)
            pe.wait_ge(s_weights, 16 * (2 + 2 * E))
            with pe.Fori(0, ROUNDS) as i:
                for b in range(BATCH):
                    pe.wait_ge(s_xg, group(i, b) + 1)
                    pe.wait_ge(s_hsc, group(i, b) * TPG + (TPG + 1))

                    def up(dst, w, src, e, f):
                        if f is not None:
                            return pe.matmul(dst[:, :], w[:, e, f * P:(f + 1) * P], src(e), start=True, stop=True)
                        for k in range(2):
                            last = pe.matmul(dst[k * TAIL1:(k + 1) * TAIL1, :], w[:, e + k, FULL1 * P:F1], src(e + k),
                                             start=True, stop=True, tile_position=(0, k * TAIL1))
                        return last

                    def down(n):
                        e, f = units[n]
                        w = W["w2"][:, e, f, :] if f is not None else W["w2_tail"][:, e // 2, :]
                        pe.wait_ge(s_hh, unit(i, b, n + 3))
                        pe.matmul(acc[b][:, :], w, hh[n % 2][:, :], start=(n == 0), stop=(n == U - 1))\
                            .then_inc(s_down, 1)

                    for n, (e, f) in enumerate(units):
                        pe.wait_ge(s_sa, unit(i, b, n + 1))
                        up(up_a[n % 2], W["w1"], lambda e: xg[b][:, 0, :], e, f).then_inc(s_a, 1)
                        pe.wait_ge(s_hh, unit(i, b, n + 1))
                        up(up_b[n % 2], W["w3"], lambda e: xg[b][:, 1 + e, :], e, f).then_inc(s_b, 1)
                        if n == 0:
                            pe.wait_ge(s_accc, group(i, b) + 1)
                        else:
                            down(n - 1)
                        if n in prepare_at:
                            prepare(*following(i, b), prepare_at[n])
                    down(U - 1)
                    pe.wait_ge(s_accc, group(i, b) + 3)
                    pe.wait_ge(s_gated, group(i, b) + 2)
                    for k in range(TPG):
                        last = pe.transpose(back[:, k * P:(k + 1) * P], oT[b][:, k * P:(k + 1) * P], cst("ident"))
                    last.then_inc(s_back, 1)

        @block.scalar
        def _(act):
            for g in range(NG):
                act.wait_ge(s_xt, g + 1)
                act.activation(xT_all[:, g * TPG:(g + 1) * TPG, :], bank[g][:, :].rearrange("p (k n) -> p k n", k=TPG),
                               ACT.Copy).then_inc(s_keep, 1)
            act.wait_ge(s_pad, 1)
            act.wait_ge(s_shift, 1)
            act.activation(prob[:, :, 0:E], shifted[:, :, :], ACT.Exp).then_inc(s_prob, 1)

            def prepare(i, b, k):
                act.wait_ge(s_hst, group(i, b) * TPG + (k + 3))
                act.activation(xg[b][:, 1:, k * P:(k + 1) * P], scaled.rearrange("p (e n) -> p e n", e=E),
                               ACT.Copy).then_inc(s_hsc, 1)

            for k in range(TPG):
                prepare(0, 0, k)
            act.sem_inc(s_down, 2)
            with act.Fori(0, ROUNDS) as i:
                for b in range(BATCH):
                    for n in range(U):
                        act.wait_ge(s_a, unit(i, b, n + 1))
                        act.wait_ge(s_hh, unit(i, b, n + 1))
                        act.activation(sa[n % 2][:, :], up_a[n % 2][:, :], ACT.Silu).then_inc(s_sa, 1)
                        if n in prepare_at:
                            prepare(*following(i, b), prepare_at[n])
                    act.wait_ge(s_down, unit(i, b, U + 2))
                    act.activation(oT[b][:, :], acc[b][:, :], ACT.Copy).then_inc(s_accc, 1)

        @block.vector
        def _(dve):
            for g in range(NG):
                tiles = range(g * TPG, (g + 1) * TPG)
                for c in tiles:
                    dve.bn_stats(st[:, c, :], x_sb[:, c, :]).then_inc(s_st, 1)
                dve.wait_ge(s_st, (g + 1) * TPG)
                for c in tiles:
                    dve.bn_aggr(mv[:, c, :], st[:, c, :]).then_inc(s_mv, 1)
            dve.wait_ge(s_mv, TILES)
            for c in range(TILES):
                dve.scalar_tensor_tensor(out=h_all[:, c, :], in0=x_sb[:, c, :], scalar=mv[:, c, 0:1],
                                         in1=sbw[:, 1, c // CHUNKS, :], op0=ALU.subtract,
                                         op1=ALU.mult).then_inc(s_mod, 1)
            dve.wait_ge(s_rstd, 2 * NG)
            for c in range(TILES):
                dve.wait_ge(s_mod, c + 1)
                dve.scalar_tensor_tensor(out=h_all[:, c, :], in0=h_all[:, c, :], scalar=rstd[:, c:c + 1],
                                         in1=sbw[:, 0, c // CHUNKS, :], op0=ALU.mult, op1=ALU.add).then_inc(s_h, 1)
            dve.memset(prob[:, :, :], -1.0).then_inc(s_pad, 1)
            logits = bank[4][:, 0:TILES * E].rearrange("p (c e) -> p c e", e=E)
            dve.wait_ge(s_logit, 1)
            dve.tensor_reduce(best[:, :], logits, AX.X, ALU.max).then_inc(s_cw, 1)
            dve.wait_ge(s_cw, 1)
            dve.tensor_tensor(shifted[:, :, :], logits, best[:, :, None].to_broadcast([P, TILES, E]),
                              ALU.subtract).then_inc(s_shift, 1)
            dve.wait_ge(s_prob, 1)
            for c in range(TILES):
                dve.max(mx[:, c, :], prob[:, c, :]).then_inc(s_mx, 1)
            for c in range(TILES):
                dve.wait_ge(s_mx, c + 1)
                dve.max_index(idx[:, c, :], mx[:, c, :], prob[:, c, :]).then_inc(s_idx, 1)
            dve.tensor_tensor(den[:, :], mx[:, :, 0], mx[:, :, 1], ALU.add).then_inc(s_cw, 1)
            dve.wait_ge(s_cw, 2)
            dve.reciprocal(den[:, :], den[:, :]).then_inc(s_cw, 1)
            dve.wait_ge(s_idx, TILES)
            dve.tensor_copy(idf[:, :, :], idx[:, :, 0:2]).then_inc(s_cw, 1)
            dve.wait_ge(s_cw, 4)
            experts = cst("iota16")[:, None, 0:E].to_broadcast([P, TILES, E])
            for k in range(2):
                dve.tensor_tensor(cw[:, k], experts, idf[:, :, k:k + 1].to_broadcast([P, TILES, E]),
                                  ALU.is_equal).then_inc(s_cw, 1)
            for k in range(2):
                dve.wait_ge(s_cw, 5 + k)
                dve.tensor_tensor(cw[:, k], cw[:, k], mx[:, :, k:k + 1].to_broadcast([P, TILES, E]),
                                  ALU.mult).then_inc(s_cw, 1)
            dve.wait_ge(s_cw, 8)
            dve.tensor_tensor(cw[:, 0], cw[:, 0], cw[:, 1], ALU.add).then_inc(s_cw, 1)
            dve.wait_ge(s_cw, 9)
            dve.tensor_tensor(cw[:, 0], cw[:, 0], den[:, :, None].to_broadcast([P, TILES, E]),
                              ALU.mult).then_inc(s_cw, 1)
            with dve.Fori(0, ROUNDS) as i:
                for b in range(BATCH):
                    for n in range(U):
                        dve.wait_ge(s_sa, unit(i, b, n + 3))
                        dve.wait_ge(s_b, unit(i, b, n + 1))
                        dve.wait_ge(s_down, unit(i, b, n + 1))
                        dve.tensor_tensor(hh[n % 2][:, :], sa[n % 2][:, :], up_b[n % 2][:, :], ALU.mult)\
                            .then_inc(s_hh, 1)
                    dve.wait_ge(s_back, group(i, b) + 1)
                    dve.wait_ge(s_x, group(i, b) + 1)
                    dve.tensor_tensor(gated[b][:, :, :], back.rearrange("p (k n) -> p k n", k=TPG),
                                      mod_row[:, 1, 1, b, None, :].to_broadcast([P, TPG, C]), ALU.mult)\
                        .then_inc(s_gated, 1)

        @block.gpsimd
        def _(pool):
            for g in range(NG):
                part = slice(g * TPG, (g + 1) * TPG)
                pool.wait_ge(s_mv, (g + 1) * TPG)
                pool.tensor_scalar(rstd[:, part], mv[:, part, 1], LN_EPS, None, ALU.add).then_inc(s_rstd, 1)
                pool.wait_ge(s_rstd, 2 * g + 1)
                pool.tensor_tensor(rstd[:, part], rstd[:, part], eps_pow[:, 0:TPG], ALU.pow).then_inc(s_rstd, 1)
            pool.wait_ge(s_keep, NG)
            pool.wait_ge(s_h, TILES)
            pool.wait_ge(s_cw, 10)
            pool.sem_inc(s_hst, 2)

            def prepare(i, b):
                at = i * TPG + b * CHUNKS
                for k in range(TPG):
                    pool.wait_ge(s_hst, group(i, b) * TPG + (k + 1))
                    pool.tensor_tensor(hs[k % 2][:, :, :],
                                       h_all[:, bass.ds(at + k, 1), :].to_broadcast([P, E, C]),
                                       cw[:, 0, bass.ds(at + k, 1), :].rearrange("p k e -> p e k")
                                       .to_broadcast([P, E, C]), ALU.mult).then_inc(s_hs, 1)
                pool.tensor_copy(xg[b][:, 0, :].rearrange("p (k n) -> p k n", k=TPG),
                                 xT_all[:, bass.ds(at, TPG), :]).then_inc(s_xg, 1)

            prepare(0, 0)
            pool.sem_inc(s_x, 2)
            with pool.Fori(0, ROUNDS) as i:
                for b in range(BATCH):
                    prepare(*following(i, b))
                    pool.wait_ge(s_gated, group(i, b) + 3)
                    xs = x_sb[:, bass.ds(i * TPG + b * CHUNKS, TPG), :]
                    pool.tensor_tensor(xs, xs, gated[b][:, :, :], ALU.add).then_inc(s_x, 1)

        @block.sync
        def _(sp):
            sp.dma_start(gate[:, :], t["gate_cols"]).then_inc(s_gate, 16)
            with sp.Fori(0, ROUNDS) as i:
                for b in range(BATCH):
                    sp.wait_ge(s_x, group(i, b) + 3)
                    sp.dma_start(out[b].rearrange("(c p) n -> p c n", p=P)[:, bass.ds(i * TPG, TPG), :],
                                 x_sb[:, bass.ds(i * TPG + b * CHUNKS, TPG), :]).then_inc(s_out, 16)
            sp.wait_ge(s_out, 16 * NG)


def kernel(**inputs):
    import concourse.bacc as _bacc
    from concourse.bass_utils import run_bass_kernel_spmd as _run

    a = {k: np.asarray(v) for k, v in inputs.items()}
    A = {n: a["L0_attn_" + n] for n in ("miu_x", "lambda_", "A_lora", "B_lora", "td_miu", "td_A", "td_B", "u",
                                        "Wr", "Wk", "Wv", "Wg", "Wo", "gn_gamma", "gn_beta")}
    b_rows = np.zeros((MIXES, P, C), np.float32)
    for f in range(4):
        b_rows[f, f * LORA:(f + 1) * LORA] = A["B_lora"][f]
    b_rows[4, 0:LORA] = A["B_lora"][4]
    host = {
        "const": shape_constants()[1],
        "L0_attn_x": a["L0_attn_x"],
        "c_cols": np.stack([a["L0_c"].T, a["L1_c"].T], axis=1),
        "wmod": np.stack([a["L0_wmod"], a["L1_wmod"]]),
        "miu_col": A["miu_x"].reshape(C, 1),
        "lambda_cols": A["lambda_"].reshape(MIXES, C).T,
        "td_miu_col": A["td_miu"].reshape(C, 1),
        "u_col": A["u"].reshape(C, 1),
        "gn_gamma_col": A["gn_gamma"].reshape(C, 1),
        "gn_beta_col": A["gn_beta"].reshape(C, 1),
        "L0_attn_A_lora": A["A_lora"],
        "b_lora_rows": b_rows,
        "L0_attn_td_A": A["td_A"],
        "L0_attn_td_B": A["td_B"],
        "rwkv_wT": np.stack([A[n].T for n in ("Wk", "Wv", "Wr", "Wg", "Wo")]),
    }
    w1, b1, w2 = a["L0_ffn_w1"], a["L0_ffn_b1"], a["L0_ffn_w2"]
    host["experts0"] = np.concatenate([w1, w2.reshape(E0, 2, P, C).transpose(0, 2, 1, 3).reshape(E0, P, 2 * C),
                                       b1.reshape(E0, 2, P).transpose(0, 2, 1), a["L0_ffn_b2"][:, :, None]], axis=2)
    host["L0_ffn_router_w"] = a["L0_ffn_router_w"]
    for n in ("Wq", "Wk", "Wv", "Wo"):
        host["L1_attn_" + n] = a["L1_attn_" + n]
    host["gate_cols"] = a["L1_ffn_gate_w"][:E1_LIVE].T
    for n in ("w1", "w3", "w2"):
        host["moe_" + n] = a["L1_ffn_" + n][:E1_LIVE]
    nc = _bacc.Bacc("TRN2", target_bir_lowering=False, num_devices=1)
    arrays, t = {}, {}
    for name, v in host.items():
        v = np.ascontiguousarray(v)
        arrays[f"in_{name}_dram"] = v
        t[name] = nc.dram_tensor(f"in_{name}_dram", v.shape, mybir.dt.from_np(v.dtype), kind="ExternalInput").ap()
    for name in ("slots_in", "slots_out"):
        t[name] = nc.dram_tensor(name, (SLOTS, C), F32, kind="Internal").ap()
    out = nc.dram_tensor("out_0_dram", (BATCH, SEQ, C), F32, kind="ExternalOutput").ap()
    bass_adaln_stack(nc, t, out)
    r = _run(nc, [arrays], core_ids=[0])
    return r.results[0]["out_0_dram"]
```
